# Optimizing a Trainium2 kernel written in Bass

```python
import numpy as np
import jax
import jax.numpy as jnp

def _softmax(x, axis=-1):
    return jax.nn.softmax(x, axis=axis)

def _gelu(x):
    return jax.nn.gelu(x, approximate=True)

def _silu(x):
    return jax.nn.silu(x)

def _sigmoid(x):
    return jax.nn.sigmoid(x)

def _layernorm(x, axis=-1, eps=1e-05):
    m = jnp.mean(x, axis=axis, keepdims=True)
    v = jnp.var(x, axis=axis, keepdims=True)
    return (x - m) / jnp.sqrt(v + eps)

def _scatter_add(tgt, idx, src, axis=0):
    return tgt.at[idx].add(src)

def _segment_sum(src, seg, n):
    return jax.ops.segment_sum(src, seg, n)
kernel_name = 'mk_gnn_resnorm_d2_gnn_r8_902c2e'

def setup_inputs(seed: int=0):
    np.random.seed(seed)
    _w = jnp.asarray

    def _rec_inputs():
        import jax
        import jax.numpy as jnp
        _gk = jax.random.key(seed)
        x = -0.000202 + 1 * jax.random.normal(jax.random.fold_in(_gk, 1), (6250, 128), jnp.float32)
        src = jax.random.randint(jax.random.fold_in(_gk, 2), (100000,), 0, 6250, jnp.int32)
        dst = jax.random.randint(jax.random.fold_in(_gk, 3), (100000,), 0, 6250, jnp.int32)
        _o = jnp.argsort(dst, stable=True)
        src = src[_o]
        dst = dst[_o]
        return (x, src, dst)
    x, src, dst = _rec_inputs()

    def _L0_gnn_setup():
        import jax, jax.numpy as jnp
        import numpy as np
        N, E, F, H, L = (6250, 75000, 128, 128, 5)
        key = jax.random.key(seed)
        ks = jax.random.split(key, 16)
        s = 1.0 / np.sqrt(H)
        u = lambda k, shape: jax.random.uniform(k, shape, jnp.float32, -s, s)
        return {'x': jax.random.normal(ks[0], (N, F), jnp.float32), 'edge_index': jax.random.randint(ks[1], (2, E), 0, N, jnp.int64), 'enc_w1': u(ks[2], (H, F)), 'enc_b1': u(ks[3], (H,)), 'enc_w2': u(ks[4], (H, H)), 'enc_b2': u(ks[5], (H,)), 'conv_w': u(ks[6], (L, H, H)), 'gru_wih': u(ks[7], (3 * H, H)), 'gru_whh': u(ks[8], (3 * H, H)), 'gru_bih': u(ks[9], (3 * H,)), 'gru_bhh': u(ks[10], (3 * H,)), 'dec_w1': u(ks[11], (H, H)), 'dec_b1': u(ks[12], (H,)), 'dec_w2': u(ks[13], (F, H)), 'dec_b2': u(ks[14], (F,))}
    _L0_gnn_all = _L0_gnn_setup()
    _L0_gnn_in = {k: v for k, v in _L0_gnn_all.items() if k in ('enc_w1', 'enc_b1', 'enc_w2', 'enc_b2', 'conv_w', 'gru_wih', 'gru_whh', 'gru_bih', 'gru_bhh', 'dec_w1', 'dec_b1', 'dec_w2', 'dec_b2')}
    del _L0_gnn_all

    def _L1_gnn_setup():
        import jax, jax.numpy as jnp
        import numpy as np
        N, E = (6250, 100000)
        IN_DIM, HIDDEN_DIM, OUT_DIM = (128, 256, 128)
        key = jax.random.key(seed)
        k = jax.random.split(key, 7)
        x = jax.random.normal(k[0], (N, IN_DIM), dtype=jnp.float32)
        edge_src = jax.random.randint(k[1], (E,), 0, N, dtype=jnp.int32)
        edge_dst = jax.random.randint(k[2], (E,), 0, N, dtype=jnp.int32)
        W1 = jax.random.normal(k[3], (IN_DIM, HIDDEN_DIM), dtype=jnp.float32) / np.sqrt(IN_DIM)
        b1 = jax.random.normal(k[4], (HIDDEN_DIM,), dtype=jnp.float32) * 0.01
        W2 = jax.random.normal(k[5], (HIDDEN_DIM, OUT_DIM), dtype=jnp.float32) / np.sqrt(HIDDEN_DIM)
        b2 = jax.random.normal(k[6], (OUT_DIM,), dtype=jnp.float32) * 0.01
        return {'x': x, 'W1': W1, 'b1': b1, 'W2': W2, 'b2': b2, 'edge_src': edge_src, 'edge_dst': edge_dst}
    _L1_gnn_all = _L1_gnn_setup()
    _L1_gnn_in = {k: v for k, v in _L1_gnn_all.items() if k in ('W1', 'b1', 'W2', 'b2')}
    del _L1_gnn_all
    return {'x': x, 'src': src, 'dst': dst, 'L0_gnn_enc_w1': _L0_gnn_in['enc_w1'], 'L0_gnn_enc_b1': _L0_gnn_in['enc_b1'], 'L0_gnn_enc_w2': _L0_gnn_in['enc_w2'], 'L0_gnn_enc_b2': _L0_gnn_in['enc_b2'], 'L0_gnn_conv_w': _L0_gnn_in['conv_w'], 'L0_gnn_gru_wih': _L0_gnn_in['gru_wih'], 'L0_gnn_gru_whh': _L0_gnn_in['gru_whh'], 'L0_gnn_gru_bih': _L0_gnn_in['gru_bih'], 'L0_gnn_gru_bhh': _L0_gnn_in['gru_bhh'], 'L0_gnn_dec_w1': _L0_gnn_in['dec_w1'], 'L0_gnn_dec_b1': _L0_gnn_in['dec_b1'], 'L0_gnn_dec_w2': _L0_gnn_in['dec_w2'], 'L0_gnn_dec_b2': _L0_gnn_in['dec_b2'], 'L1_gnn_W1': _L1_gnn_in['W1'], 'L1_gnn_b1': _L1_gnn_in['b1'], 'L1_gnn_W2': _L1_gnn_in['W2'], 'L1_gnn_b2': _L1_gnn_in['b2']}

def reference(x, src, dst, L0_gnn_enc_w1, L0_gnn_enc_b1, L0_gnn_enc_w2, L0_gnn_enc_b2, L0_gnn_conv_w, L0_gnn_gru_wih, L0_gnn_gru_whh, L0_gnn_gru_bih, L0_gnn_gru_bhh, L0_gnn_dec_w1, L0_gnn_dec_b1, L0_gnn_dec_w2, L0_gnn_dec_b2, L1_gnn_W1, L1_gnn_b1, L1_gnn_W2, L1_gnn_b2):
    import jax
    import jax.numpy as jnp

    def _L0_gnn_ref(x, edge_index, enc_w1, enc_b1, enc_w2, enc_b2, conv_w, gru_wih, gru_whh, gru_bih, gru_bhh, dec_w1, dec_b1, dec_w2, dec_b2):
        import jax, jax.numpy as jnp
        import numpy as np
        N, E, F, H, L = (6250, 75000, 128, 128, 5)
        src, dst = (edge_index[0], edge_index[1])
        n_nodes = x.shape[0]
        h = jnp.maximum(x @ enc_w1.T + enc_b1, 0.0) @ enc_w2.T + enc_b2

        def step(h, w):
            m = h @ w
            agg = jax.ops.segment_sum(m[src], dst, num_segments=n_nodes)
            gi = agg @ gru_wih.T + gru_bih
            gh = h @ gru_whh.T + gru_bhh
            ir, iz, i_n = jnp.split(gi, 3, axis=1)
            hr, hz, h_n = jnp.split(gh, 3, axis=1)
            r = jax.nn.sigmoid(ir + hr)
            z = jax.nn.sigmoid(iz + hz)
            n = jnp.tanh(i_n + r * h_n)
            return ((1.0 - z) * n + z * h, None)
        h, _ = jax.lax.scan(step, h, conv_w)
        h = jnp.maximum(h, 0.0)
        out = jnp.maximum(h @ dec_w1.T + dec_b1, 0.0) @ dec_w2.T + dec_b2
        return jax.nn.sigmoid(out)

    def _L1_gnn_ref(x, W1, b1, W2, b2, edge_src, edge_dst):
        import jax, jax.numpy as jnp
        import numpy as np
        N, E = (6250, 100000)
        IN_DIM, HIDDEN_DIM, OUT_DIM = (128, 256, 128)
        n = x.shape[0]
        cnt = jax.ops.segment_sum(jnp.ones(edge_src.shape, dtype=x.dtype), edge_dst, num_segments=n)
        denom = jnp.maximum(cnt, 1.0)[:, None]

        def layer(h, W, b):
            s = jax.ops.segment_sum(h[edge_src], edge_dst, num_segments=n)
            neigh_mean = s / denom
            return jax.nn.relu((h + neigh_mean) @ W + b)
        h = layer(x, W1, b1)
        z = layer(h, W2, b2)
        return z
    edge_index = jnp.stack([src, dst])
    x = _layernorm(x + _L0_gnn_ref(x, edge_index, L0_gnn_enc_w1, L0_gnn_enc_b1, L0_gnn_enc_w2, L0_gnn_enc_b2, L0_gnn_conv_w, L0_gnn_gru_wih, L0_gnn_gru_whh, L0_gnn_gru_bih, L0_gnn_gru_bhh, L0_gnn_dec_w1, L0_gnn_dec_b1, L0_gnn_dec_w2, L0_gnn_dec_b2), axis=-1)
    x = _layernorm(x + _L1_gnn_ref(x, L1_gnn_W1, L1_gnn_b1, L1_gnn_W2, L1_gnn_b2, src, dst), axis=-1)
    return x

_drawn_inputs = setup_inputs


def setup_inputs(seed=0):
    import zlib

    import numpy as np

    out = dict(_drawn_inputs(seed))
    spreads = {}
    factors = {'L0_gnn_enc_w1': 21.839,
     'L0_gnn_enc_b1': 24.368,
     'L0_gnn_gru_whh': 4.935,
     'L0_gnn_gru_bih': 23.859,
     'L0_gnn_gru_bhh': 44.581,
     'L0_gnn_dec_b1': 7.353,
     'L0_gnn_dec_b2': 3.082,
     'L1_gnn_b1': 8.0,
     'L1_gnn_b2': 8.0,
     'L0_gnn_enc_b2': 6.725}
    for name, (base, spread) in spreads.items():
        noise = np.random.default_rng([zlib.crc32(name.encode()), seed]).standard_normal(out[name].shape)
        drawn = base * np.exp(spread * noise) if base else spread * noise
        out[name] = jnp.asarray(drawn.astype(out[name].dtype))
    for name, factor in factors.items():
        out[name] = (out[name] * factor).astype(out[name].dtype)
    return out
```

```python
import concourse.bass as bass
from concourse import mybir
from contextlib import ExitStack

NODES, F, EDGES, LAYERS, HID = 6250, 128, 100000, 5, 256
P = 128
STRIPS = 7
TILES = 49
TPS = TILES // STRIPS
W = TPS * P
H = W // 2
NPAD = TILES * P
CH = TPS * W
REG = STRIPS * P * TILES * W
PIECES = 6
TAIL = NODES - (TILES - 1) * P
EC = 1024
ER = -(-EDGES // EC)
EP = ER * EC
EB = EC // P
NONE = 8191
SKIP = 30
FAR = EDGES - 1
UNITS = 7 * STRIPS
X1_SCALE = 2048.0
NORM = 22.65
LOADS = 22
LAG_STEPS, GRU_STEPS, DEC_STEPS, MEAN1_STEPS, MEAN2_STEPS, PIECE_STEPS = 4, 6, 31, 2, 25, 8


class Steps:

    def __init__(self, engine, sem, hold, base=0):
        self.engine, self.sem, self.hold, self.base, self.n = engine, sem, hold, base, 0

    def did(self, instruction):
        instruction.then_inc(self.sem, 1)
        self.n += 1

    def after(self):
        self.hold(self.engine, self.sem, self.base + self.n)


def gnn_kernel(nc, x, xT, src, dst, enc_w1T, enc_b1, enc_w2T, enc_b2, conv_w, wihT, whhT, bih, bhh,
               dec_w1T, dec_b1, dec_w2T, dec_b2, W1, b1, W2, b2, out):
    dt = mybir.dt
    fp32, i32, f16, f8, u8, bf16 = dt.float32, dt.int32, dt.float16, dt.float8e5, dt.uint8, dt.bfloat16
    ALU = mybir.AluOpType
    ACT = mybir.ActivationFunctionType
    X = mybir.AxisListType.X
    RMAX = bass.bass_isa.ReduceOp.max

    A = nc.dram_tensor("edge_counts", (PIECES * REG, 1), u8, kind="Internal").ap()
    A_p = A.rearrange("(k s p x) o -> k s p (x o)", k=PIECES, s=STRIPS, p=P)
    A_z = A.rearrange("(k c p x) o -> k c p (x o)", k=PIECES, p=P, x=CH)
    ZC = REG // (P * CH)
    keys = nc.dram_tensor("edge_keys", (3 * EP,), i32, kind="Internal").ap()
    rdeg_d = nc.dram_tensor("inverse_degree", (TILES, P), fp32, kind="Internal").ap()
    x1_d = nc.dram_tensor("x1_rows", (STRIPS, P, W), fp32, kind="Internal").ap()
    y_d = nc.dram_tensor("y_rows", (STRIPS, P, W), fp32, kind="Internal").ap()
    x_t = x[0:(TILES - 1) * P, :].rearrange("(t p) f -> p t f", p=P)
    out_t = out[0:(TILES - 1) * P, :].rearrange("(t p) f -> p t f", p=P)

    ctx = ExitStack()
    with ctx:
        def sb(name, shape, d=fp32):
            return ctx.enter_context(nc.sbuf_tensor(name, shape, d))

        def sem(name):
            return ctx.enter_context(nc.semaphore(name))

        hT = sb("hT", [P, NPAD])
        parts = sb("parts", [P, 2, NPAD], f16)
        later = sb("later", [P, 2, 6 * W], f16)
        ring = sb("ring", [P, STRIPS, CH // 4])
        spare = sb("spare", [P, CH // 4])
        work = sb("work", [P, 10, W])
        w_enc1, w_enc2 = sb("w_enc1", [P, P]), sb("w_enc2", [P, P])
        w_dec1, w_dec2 = sb("w_dec1", [P, P]), sb("w_dec2", [P, P])
        w_conv, w_convs = sb("w_conv", [P, LAYERS, P]), sb("w_convs", [P, LAYERS, P])
        w_ih, w_hh = sb("w_ih", [P, 3 * P]), sb("w_hh", [P, 3 * P])
        w_1 = sb("w_1", [P, HID])
        w_2, w_2s = sb("w_2", [P, 2, P]), sb("w_2s", [P, 2, P])
        w_1sq = sb("w_1sq", [P, HID])
        ident = sb("ident", [P, P])
        ones = sb("ones", [P, 1])
        eps = sb("eps", [P, 1])
        c_enc1, c_enc2, c_dec1 = sb("c_enc1", [P, 1]), sb("c_enc2", [P, 1]), sb("c_dec1", [P, 1])
        c_ih, c_hh, c_gate = sb("c_ih", [P, 3]), sb("c_hh", [P, 3]), sb("c_gate", [P, 3])
        c_b1, c_b1a = sb("c_b1", [P, 2]), sb("c_b1a", [P, 2])
        r_dec2, r_b2 = sb("r_dec2", [P, P]), sb("r_b2", [P, P])
        stats, mv = sb("stats", [P, TPS, 6]), sb("mv", [P, TPS, 2])
        dev, rstd = sb("dev", [P, TPS]), sb("rstd", [P, TPS])
        mx, mxa = sb("mx", [P, 8]), sb("mxa", [P, 8])
        prod, expo, scale_i, undo_i = sb("prod", [P, 6]), sb("expo", [P, 6], i32), sb("scale_i", [P, 6], i32), sb("undo_i", [P, 6], i32)
        scale_b, undo_b = sb("scale_b", [P, 6], i32), sb("undo_b", [P, 6], i32)
        scale, undo = scale_b[:, :].bitcast(fp32), undo_b[:, :].bitcast(fp32)
        undo_y = sb("undo_y", [P, 1])
        norm2 = sb("norm2", [P, 2])
        eflag, eflag_a = sb("eflag", [P, 4]), sb("eflag_a", [P, 4])
        lag_f, lag_i, lag_n = sb("lag_f", [P, 2]), sb("lag_i", [P, 1], i32), sb("lag_n", [P, 1], i32)
        piece_f, piece_n = sb("piece_f", [P, 1]), sb("piece_n", [P, 1], i32)
        piece_v = sb("piece_v", [P, 1])
        idx_s, val_s = sb("idx_s", [P, 2, EB], i32), sb("val_s", [P, 2, EB], u8)
        iota = sb("iota", [P, P], i32)
        aggS, r_g, z_g, t_g, n_g, h_new = (work[:, i, :] for i in range(6))
        d1, o_s, x_s, x1_s = (work[:, i, :] for i in (6, 7, 8, 9))
        rdeg_s, u_s, h1a, h1b, y_s = (work[:, i, :] for i in (1, 2, 3, 4, 7))
        e1 = ring[:, :, :].rearrange("p a b -> p (a b)")[:, 9 * EC:9 * EC + W]
        ebuf = ring[:, :, :].rearrange("p a b -> p (a b)").bitcast(i32)

        def erow(i):
            return ebuf[0:ER, i * EC:(i + 1) * EC]

        srcN, dstN, keyN = erow(0), erow(1), erow(2)
        ahead = [erow(3), erow(4)]
        behind = [erow(5), erow(6)]
        before, after = erow(7).bitcast(fp32), erow(8).bitcast(fp32)
        pbuf = parts[:, :, :].rearrange("p a b -> p (a b)").bitcast(i32)
        keyH, dstH = pbuf[0:ER, 0:2 * EC], pbuf[0:ER, 2 * EC:4 * EC]
        same = pbuf[0:ER, 4 * EC:6 * EC].bitcast(fp32)
        wbuf = work[:, :, :].rearrange("p a b -> p (a b)")
        run = wbuf[0:ER, 0:2 * EC]
        xorb = [wbuf[0:ER, (2 + i) * EC:(3 + i) * EC].bitcast(i32) for i in range(2)]
        e_t, e_s, e_a, e_b = (wbuf[0:ER, (4 + i) * EC:(5 + i) * EC] for i in range(4))
        COLS = ER * EB
        lbuf = later[:, :, :].rearrange("p a b -> p (a b)").bitcast(i32)

        def ecol(i):
            return lbuf[:, i * COLS:(i + 1) * COLS]

        hiT, loT, rowT, cntT, idxT, bitT = (ecol(i) for i in range(6))
        valT = lbuf[:, 6 * COLS:6 * COLS + COLS // 4].bitcast(f8)
        oh_lo = [wbuf[:, i * 512:(i + 1) * 512].bitcast(bf16).rearrange("p (b c) -> p b c", c=P) for i in range(2)]
        oh_hi = [wbuf[:, (4 + i) * 256:(5 + i) * 256].bitcast(bf16).rearrange("p (b c) -> p b c", c=64) for i in range(2)]
        deg = wbuf[0:64, 1536:1536 + P]
        zeros = spare[:, :].bitcast(u8)

        psA = ctx.enter_context(nc.psum_tensor("psA", [P, 2, 512], fp32))
        psG = ctx.enter_context(nc.psum_tensor("psG", [P, 4, 512], fp32))
        psM = ctx.enter_context(nc.psum_tensor("psM", [P, 1024], fp32))
        rows_ps = psM[:, 0:W]
        x1T_ps = psG[:, 2:4, :].rearrange("p a b -> p (a b)")[:, 0:W]

        seen = {e: sem(f"passed_{e}") for e in ("pe", "act", "dve", "pool", "sp")}
        names = """edges_in weights_in x_in consts zeros_set ident_set iota_set pads_set keys_out halo_in flags
            flags_all lags_known lag_free lag_steps counted edge_cols cols_ps cols_free pieces_known max_set max_all
            hid_ps e1_set h0_ps h0_set h0_max sq_set norm_ps norm_set scales_set m0_ps m0_hi m0_lo built piece_vals
            staged zero_filled hot_set hot_used deg_ps deg_set deg_out src_ready sums sums_a sums_b gates rz
            n_in n_set h_set h_kept rows_m hi_set lo_set dec1_ps d1_set dec2_ps o_set sig_set x_rows v_set var_set
            dev_set x1_set x1_kept x1T_ps_set x1T_set rdeg_in u_set hid1_ps h1_set y_ps y_set y_kept last_in mean_set
            mean_ps w_set out_set stored x_free steps_dve steps_lag steps_gru steps_dec steps_s1 steps_s2
            x_ready tail_set steps_piece""".split()
        s = {n: sem(n) for n in names}
        a_ready = [sem(f"a_ready{c}") for c in range(STRIPS)]
        a_free = [sem(f"a_free{c}") for c in range(STRIPS - 1)]
        lag_in = [sem(f"lag_in{b}") for b in range(2)]
        scattered = [sem(f"scattered{b}") for b in range(2)]
        who = {id(nc.tensor): "pe", id(nc.scalar): "act", id(nc.vector): "dve", id(nc.gpsimd): "pool", id(nc.sync): "sp"}
        tag = {}

        def hold(engine, semaphore, value):
            engine.wait_ge(semaphore, value)
            if not isinstance(value, int):
                engine.nop().then_inc(seen[tag[id(engine)]], 1)

        block = ctx.enter_context(nc.Block())

        @block.sync
        def _(sp):
            tag[id(sp)] = "sp"
            full = EDGES // EC
            rest = EDGES - full * EC
            sp.wait_ge(s["pads_set"], 4)
            for d, t in ((src, srcN), (dst, dstN)):
                sp.dma_start(t[0:full, :], d[0:full * EC].rearrange("(p c) -> p c", c=EC)).then_inc(s["edges_in"], 16)
                sp.dma_start(t[full:ER, 0:rest], d[full * EC:EDGES].rearrange("(p c) -> p c", c=rest)).then_inc(s["edges_in"], 16)
            sp.dma_start(keys[0:EP].rearrange("(p c) -> p c", c=EC), ahead[0]).then_inc(s["keys_out"], 16)
            sp.dma_start(keys[2 * EP:3 * EP].rearrange("(p c) -> p c", c=EC), ahead[1]).then_inc(s["keys_out"], 16)
            sp.wait_ge(s["steps_dve"], 1)
            sp.dma_start(keys[EP:2 * EP].rearrange("(p c) -> p c", c=EC), keyN).then_inc(s["keys_out"], 16)
            sp.wait_ge(s["keys_out"], 48)
            halo = bass.AP(keys.tensor, EP - EC, [[EC, ER], [1, 2 * EC]])
            sp.dma_start(keyH, halo).then_inc(s["halo_in"], 16)
            sp.wait_ge(s["lags_known"], 1)
            rounds = sp.value_load(lag_n[0:1, 0:1], min_val=1, max_val=EP // 2)
            with sp.Fori(0, rounds) as i:
                for b in range(2):
                    hold(sp, s["lag_free"], i * 2 + (b + 1))
                    sp.dma_start(ahead[b], keys[bass.ds(EP - 1 - b - i * 2, EP)].rearrange("(p c) -> p c", c=EC)).then_inc(lag_in[b], 16)
                    sp.dma_start(behind[b], keys[bass.ds(EP + 1 + b + i * 2, EP)].rearrange("(p c) -> p c", c=EC)).then_inc(lag_in[b], 16)
            sp.wait_ge(s["deg_set"], 1)
            sp.dma_start(rdeg_d, deg[0:TILES, :]).then_inc(s["deg_out"], 16)
            sp.wait_ge(s["pieces_known"], 1)
            more = sp.value_load(piece_n[0:1, 0:1], min_val=0, max_val=PIECES - 1)
            with sp.If(more > 0):
                with sp.Fori(0, more) as k:
                    for c in range(ZC):
                        sp.dma_start(A_z[bass.ds(k + 1, 1), c, :, :].rearrange("k p x -> (k p) x"), zeros).then_inc(s["zero_filled"], 16)
            hold(sp, s["built"], more + 1)

            def loads(unit, strip):
                for c in range(STRIPS):
                    if not isinstance(unit, int):
                        hold(sp, a_free[c] if c < STRIPS - 1 else s["sums"], unit)
                    a = A_p[0, bass.ds(strip, 1), :, c * CH:(c + 1) * CH].rearrange("s p x -> (s p) x")
                    sp.dma_start(ring[:, c, :].bitcast(u8), a).then_inc(a_ready[c], 16)
                with sp.If(more > 0):
                    with sp.Fori(0, more) as k:
                        for c in range(STRIPS):
                            n = more * unit * STRIPS + k * STRIPS + c
                            hold(sp, s["x_free"], n + 1)
                            a = A_p[bass.ds(k + 1, 1), bass.ds(strip, 1), :, c * CH:(c + 1) * CH].rearrange("k s p x -> (k s p) x")
                            sp.dma_start(spare[:, :].bitcast(u8), a).then_inc(s["x_ready"], 16)

            loads(0, 0)
            with sp.Fori(1, STRIPS) as strip:
                loads(strip, strip)
            with sp.Fori(1, 7) as layer:
                with sp.Fori(0, STRIPS) as strip:
                    loads(layer * STRIPS + strip, strip)

        @block.gpsimd
        def _(pool):
            tag[id(pool)] = "pool"
            pool.memset(zeros, 0).then_inc(s["zeros_set"], 1)
            pool.memset(ident[:, :], 0.0).then_inc(s["ident_set"], 1)
            pool.wait_ge(s["ident_set"], 1)
            pool.affine_select(out=ident[:, :], in_=ident[:, :], compare_op=ALU.not_equal, fill=1.0, base=0,
                               pattern=[[-1, P]], channel_multiplier=1).then_inc(s["ident_set"], 1)
            pool.iota(iota[:, :], pattern=[[1, P]], base=0, channel_multiplier=0).then_inc(s["iota_set"], 1)
            pool.wait_ge(s["flags"], 1)
            pool.partition_all_reduce(eflag_a[:, 0:2], eflag[:, 0:2], P, RMAX).then_inc(s["flags_all"], 1)
            pool.wait_ge(s["flags"], 2)
            pool.partition_all_reduce(eflag_a[:, 2:3], eflag[:, 2:3], P, RMAX).then_inc(s["flags_all"], 1)
            pool.wait_ge(s["max_set"], 1)
            pool.partition_all_reduce(mxa[:, :], mx[:, :], P, RMAX).then_inc(s["max_all"], 1)

            def group(b, col, base, i):
                if i is not None:
                    hold(pool, scattered[b], base * (16 * EB * ER // 2) + i * (16 * EB))
                pool.tensor_copy(idx_s[:, b, :], idxT[:, bass.ds(col, EB)]).then_inc(s["staged"], 1)
                pool.tensor_copy(val_s[:, b, :], valT.bitcast(u8)[:, bass.ds(col, EB)]).then_inc(s["staged"], 1)
                at = base * (2 * ER) + (2 * b + 2) + (0 if i is None else i * 4)
                hold(pool, s["staged"], at)
                for j in range(EB):
                    pool.indirect_dma_start(A, bass.IndirectOffsetOnAxis(ap=idx_s[:, b, j:j + 1], axis=0),
                                            val_s[:, b, j:j + 1], None, bounds_check=PIECES * REG - 1,
                                            oob_is_err=False).then_inc(scattered[b], 16)

            def scatter(piece):
                for b in range(2):
                    group(b, b * EB, piece, None)
                with pool.Fori(1, ER // 2) as i:
                    for b in range(2):
                        group(b, i * (2 * EB) + b * EB, piece, i)
                for b in range(2):
                    hold(pool, scattered[b], (piece + 1) * (16 * EB * ER // 2))
                pool.nop().then_inc(s["built"], 1)

            pool.wait_ge(s["piece_vals"], 1)
            pool.wait_ge(s["zero_filled"], 16 * ZC)
            scatter(0)
            more = pool.value_load(piece_n[0:1, 0:1], min_val=0, max_val=PIECES - 1)
            with pool.If(more > 0):
                with pool.Fori(0, more) as k:
                    hold(pool, s["piece_vals"], k + 2)
                    hold(pool, s["zero_filled"], (k + 2) * (16 * ZC))
                    scatter(k + 1)

            pool.nop().then_inc(s["h_kept"], 1)
            with pool.Fori(0, 4) as layer:
                with pool.Fori(0, STRIPS) as strip:
                    v = layer * STRIPS + strip
                    hold(pool, s["h_set"], v * 2 + 2)
                    pool.tensor_copy(hT[:, bass.ds(strip * W, W)], h_new).then_inc(s["h_kept"], 1)

            def rows3(t):
                return t.rearrange("p (t f) -> p t f", f=F)

            def decoder(w, last):
                if not last:
                    pool.dma_start(rows3(x_s), x_t[:, bass.ds(w * TPS, TPS), :]).then_inc(s["x_rows"], 16)
                else:
                    k = TPS - 1
                    pool.memset(rows3(x_s)[:, k, :], 0.0).then_inc(s["tail_set"], 1)
                    pool.wait_ge(s["tail_set"], 1)
                    pool.dma_start(rows3(x_s)[:, 0:k, :], x_t[:, w * TPS:w * TPS + k, :]).then_inc(s["x_rows"], 16)
                    pool.wait_ge(s["x_rows"], 16 * 7)
                    pool.dma_start(rows3(x_s)[0:TAIL, k, :], x[(TILES - 1) * P:NODES, :]).then_inc(s["x_rows"], 16)
                hold(pool, s["x1_set"], w + 1)
                pool.dma_start(x1_d[bass.ds(w, 1), :, :].rearrange("s p x -> (s p) x"), x1_s).then_inc(s["x1_kept"], 16)

            decoder(0, False)
            with pool.Fori(1, STRIPS - 1) as w:
                decoder(w, False)
            decoder(STRIPS - 1, True)

            def rdeg_load(w, done):
                a = rdeg_d[bass.ds(w * TPS, TPS), :].rearrange("t p -> (t p)").partition_broadcast(P)
                pool.dma_start(rdeg_s, a).then_inc(done, 16)

            pool.wait_ge(s["deg_out"], 16)
            pool.wait_ge(s["x1_kept"], 16 * STRIPS)
            rdeg_load(0, s["rdeg_in"])
            with pool.Fori(0, STRIPS - 1) as w:
                hold(pool, s["u_set"], w + 1)
                rdeg_load(w + 1, s["rdeg_in"])
                hold(pool, s["y_set"], w + 1)
                pool.dma_start(y_d[bass.ds(w, 1), :, :].rearrange("s p x -> (s p) x"), y_s).then_inc(s["y_kept"], 16)
            pool.wait_ge(s["y_set"], STRIPS)
            pool.dma_start(y_d[STRIPS - 1, :, :], y_s).then_inc(s["y_kept"], 16)
            pool.wait_ge(s["y_kept"], 16 * STRIPS)

            def last_loads(w):
                rdeg_load(w, s["last_in"])
                pool.dma_start(y_s, y_d[bass.ds(w, 1), :, :].rearrange("s p x -> (s p) x")).then_inc(s["last_in"], 16)
                pool.dma_start(x_s, x1_d[bass.ds(w, 1), :, :].rearrange("s p x -> (s p) x")).then_inc(s["last_in"], 16)

            last_loads(0)
            with pool.Fori(0, STRIPS - 1) as w:
                hold(pool, s["v_set"], w + (STRIPS + 1))
                last_loads(w + 1)
                hold(pool, s["out_set"], w + 1)
                pool.dma_start(out_t[:, bass.ds(w * TPS, TPS), :], rows3(x1_s)).then_inc(s["stored"], 16)
            pool.wait_ge(s["out_set"], STRIPS)
            k = TPS - 1
            pool.dma_start(out_t[:, (STRIPS - 1) * TPS:, :], rows3(x1_s)[:, 0:k, :]).then_inc(s["stored"], 16)
            pool.dma_start(out[(TILES - 1) * P:NODES, :], rows3(x1_s)[0:TAIL, k, :]).then_inc(s["stored"], 16)
            pool.wait_ge(s["stored"], 16 * (STRIPS + 1))

        @block.scalar
        def _(act):
            tag[id(act)] = "act"
            act.wait_ge(s["pads_set"], 5)
            act.dma_start(hT[:, 0:NODES], xT).then_inc(s["x_in"], 16)

            loads = [(w_enc1[:, :], enc_w1T), (w_enc2[:, :], enc_w2T),
                     (w_conv[:, :, :], conv_w.rearrange("l k f -> k l f")), (w_ih[:, :], wihT), (w_hh[:, :], whhT),
                     (w_dec1[:, :], dec_w1T),
                     (w_dec2[:, :], dec_w2T), (r_dec2[:, :], dec_b2.partition_broadcast(P)), (w_1[:, :], W1),
                     (w_2[:, :, :], W2.rearrange("(h k) f -> k h f", k=P)), (r_b2[:, :], b2.partition_broadcast(P))]
            for t, a in ((c_enc1, enc_b1), (c_enc2, enc_b2), (c_ih, bih), (c_hh, bhh), (c_dec1, dec_b1), (c_b1, b1)):
                for g in range(a.shape[0] // P):
                    loads.append((t[:, g:g + 1], a[g * P:(g + 1) * P].rearrange("(p o) -> p o", o=1)))
            assert len(loads) == LOADS
            for t, a in loads:
                act.dma_start(t, a).then_inc(s["weights_in"], 16)
            act.wait_ge(s["zeros_set"], 1)
            for c in range(ZC):
                act.dma_start(A_z[0, c, :, :], zeros).then_inc(s["zero_filled"], 16)

            act.wait_ge(s["weights_in"], 16 * LOADS)
            for j in range(2 * STRIPS):
                b = j % 2
                act.wait_ge(s["hid_ps"], j + 1)
                act.activation(e1[:, b * H:(b + 1) * H], psG[:, 2 * b, 0:H], ACT.Relu, bias=c_enc1[:, :]).then_inc(s["e1_set"], 1)
                act.wait_ge(s["h0_ps"], j + 1)
                act.activation(hT[:, j * H:(j + 1) * H], psG[:, 2 * b + 1, 0:H], ACT.Identity, bias=c_enc2[:, :]).then_inc(s["h0_set"], 1)
            act.wait_ge(s["norm_ps"], 1)
            act.activation(norm2[:, :], psM[:, 0:2], ACT.Sqrt).then_inc(s["norm_set"], 1)
            for t in range(STRIPS):
                act.wait_ge(s["m0_ps"], t + 1)
                act.activation(parts[:, 0, t * W:(t + 1) * W], rows_ps, ACT.Copy).then_inc(s["m0_hi"], 1)

            def sums_out(v, by):
                hold(act, s["sums"], v + 1)
                act.activation(aggS[:, 0:H], psA[:, 0, 0:H], ACT.Copy if isinstance(by, float) else ACT.Identity,
                               scale=by).then_inc(s["sums_a"], 1)

            def gates(v):
                for b in range(2):
                    hb = slice(b * H, (b + 1) * H)
                    hold(act, s["gates"], v * 2 + (b + 1))
                    act.activation(r_g[:, hb], psG[:, 0, 0:H], ACT.Sigmoid, bias=c_gate[:, 0:1]).then_inc(s["rz"], 1)
                    act.activation(z_g[:, hb], psG[:, 1, 0:H], ACT.Sigmoid, bias=c_gate[:, 1:2]).then_inc(s["rz"], 1)
                    hold(act, s["n_in"], v * 2 + (b + 1))
                    act.activation(n_g[:, hb], t_g[:, hb], ACT.Tanh, bias=c_ih[:, 2:3]).then_inc(s["n_set"], 1)

            def high(v, ready, target, source, by):
                hold(act, ready, v)
                act.activation(target, source, ACT.Copy, scale=by).then_inc(s["hi_set"], 1)

            def gru(v, layer, strip):
                sums_out(v, undo[:, bass.ds(layer, 1)])
                gates(v)
                t = parts[:, 0, 6 * W:7 * W] if isinstance(strip, int) else later[:, 0, bass.ds(strip * W, W)]
                high(v + 1, s["rows_m"], t, rows_ps, 1.0)

            with act.Fori(0, 4) as layer:
                with act.Fori(0, STRIPS - 1) as strip:
                    gru(layer * STRIPS + strip, layer, strip)
                gru(layer * STRIPS + 6, layer, 6)

            def deviation(n):
                hold(act, s["var_set"], n + 1)
                act.activation(dev[:, :], mv[:, :, 1], ACT.Sqrt, bias=eps[:, :]).then_inc(s["dev_set"], 1)

            def decoder(w, last):
                v = w + 4 * STRIPS
                sums_out(v, undo[:, 4:5])
                gates(v)
                hold(act, s["dec1_ps"], w + 1)
                act.activation(d1.rearrange("p (a b) -> p a b", a=2), psG[:, 0:2, 0:H], ACT.Relu, bias=c_dec1[:, :]).then_inc(s["d1_set"], 1)
                hold(act, s["o_set"], w + 1)
                act.activation(t_g, o_s, ACT.Sigmoid).then_inc(s["sig_set"], 1)
                deviation(w)
                t = parts[:, 0, 6 * W:7 * W] if last else later[:, 0, bass.ds(w * W, W)]
                high(w + 1, s["x1_set"], t, x1_s, X1_SCALE)
                hold(act, s["x1T_ps_set"], w + 1)
                act.activation(hT[:, bass.ds(w * W, W)], x1T_ps, ACT.Copy).then_inc(s["x1T_set"], 1)

            with act.Fori(0, STRIPS - 1) as w:
                decoder(w, False)
            decoder(STRIPS - 1, True)

            def mean1(w, last):
                v = w + 5 * STRIPS
                sums_out(v, 2.0 / X1_SCALE)
                hold(act, s["hid1_ps"], w + 1)
                for hb, t in enumerate((h1a, h1b)):
                    act.activation(t.rearrange("p (a b) -> p a b", a=2), psG[:, 2 * hb:2 * hb + 2, 0:H], ACT.Relu,
                                   bias=c_b1[:, hb:hb + 1]).then_inc(s["h1_set"], 1)
                t = parts[:, 0, 6 * W:7 * W] if last else later[:, 0, bass.ds(w * W, W)]
                high(w + 1, s["y_ps"], t, rows_ps, 1.0)

            with act.Fori(0, STRIPS - 1) as w:
                mean1(w, False)
            mean1(STRIPS - 1, True)

            with act.Fori(0, STRIPS) as w:
                sums_out(w + 6 * STRIPS, undo[:, 5:6])
                deviation(w + STRIPS)

        @block.vector
        def _(dve):
            tag[id(dve)] = "dve"
            my = Steps(dve, s["steps_dve"], hold)
            for t, value in ((srcN, NONE), (dstN, NONE), (ahead[0], -1), (ahead[1], (NONE << 13) | NONE)):
                dve.memset(t, value).then_inc(s["pads_set"], 1)
            dve.memset(hT[:, NODES:NPAD], 0.0).then_inc(s["pads_set"], 1)
            dve.memset(ones[:, :], 1.0).then_inc(s["consts"], 1)
            dve.memset(eps[:, :], 1e-5).then_inc(s["consts"], 1)
            dve.memset(eflag[:, :], 0.0).then_inc(s["consts"], 1)
            dve.memset(before, 0.0).then_inc(s["consts"], 1)
            dve.memset(after, 0.0).then_inc(s["consts"], 1)

            dve.wait_ge(s["edges_in"], 64)
            my.did(dve.scalar_tensor_tensor(keyN, dstN, 13, srcN, ALU.logical_shift_left, ALU.bitwise_or))
            dve.wait_ge(s["halo_in"], 16)
            my.did(dve.tensor_scalar(dstH, keyH, 13, None, ALU.arith_shift_right))
            my.after()
            n = 2 * EC
            my.did(dve.tensor_tensor(same[:, 1:n], dstH[:, 1:n], dstH[:, 0:n - 1], ALU.is_lt))
            my.after()
            dve.wait_ge(s["consts"], 5)
            my.did(dve.tensor_reduce(eflag[0:ER, 1:2], same[:, 1:n], X, ALU.max))
            my.after()
            my.did(dve.tensor_tensor(same[:, 1:n], dstH[:, 1:n], dstH[:, 0:n - 1], ALU.is_equal))
            my.after()
            my.did(dve.scalar_tensor_tensor(same[:, 1:n], dstH[:, 1:n], float(NONE), same[:, 1:n], ALU.is_lt, ALU.mult))
            my.after()
            my.did(dve.tensor_tensor_scan(run[:, 1:n], same[:, 1:n], same[:, 1:n], 0.0, ALU.mult, ALU.add))
            my.after()
            my.did(dve.tensor_reduce(eflag[0:ER, 0:1], run[:, EC:n], X, ALU.max))
            my.after()
            dve.nop().then_inc(s["flags"], 1)
            dve.wait_ge(s["flags_all"], 1)
            my.did(dve.tensor_scalar(lag_f[:, 0:1], eflag_a[:, 0:1], float(EC - 1), float(FAR), ALU.is_ge, ALU.mult))
            my.did(dve.tensor_scalar(lag_f[:, 1:2], eflag_a[:, 1:2], float(FAR), 2.0, ALU.mult, ALU.max))
            my.after()
            my.did(dve.tensor_tensor(lag_f[:, 0:1], lag_f[:, 0:1], lag_f[:, 1:2], ALU.max))
            my.after()
            my.did(dve.tensor_tensor(lag_f[:, 0:1], lag_f[:, 0:1], eflag_a[:, 0:1], ALU.max))
            my.after()
            my.did(dve.tensor_scalar(lag_i[:, :], lag_f[:, 0:1], 1.0, None, ALU.add))
            my.after()
            my.did(dve.tensor_scalar(lag_n[:, :], lag_i[:, :], 1, None, ALU.logical_shift_right))
            my.after()
            dve.nop().then_inc(s["lags_known"], 1)
            rounds = dve.value_load(lag_n[0:1, 0:1], min_val=1, max_val=EP // 2)
            dve.nop().then_inc(s["lag_free"], 2)
            with dve.Fori(0, rounds) as i:
                lag = Steps(dve, s["lag_steps"], hold, i * (2 * LAG_STEPS))
                for b in range(2):
                    hold(dve, lag_in[b], i * 32 + 32)
                    lag.did(dve.tensor_tensor(xorb[0], keyN, ahead[b], ALU.bitwise_xor))
                    lag.did(dve.tensor_tensor(xorb[1], keyN, behind[b], ALU.bitwise_xor))
                    lag.after()
                    dve.nop().then_inc(s["lag_free"], 1)
                    lag.did(dve.scalar_tensor_tensor(before, xorb[0], 0.0, before, ALU.is_equal, ALU.add))
                    lag.did(dve.scalar_tensor_tensor(after, xorb[1], 0.0, after, ALU.is_equal, ALU.add))
                    lag.after()
                assert lag.n == 2 * LAG_STEPS
            hold(dve, s["lag_steps"], rounds * (2 * LAG_STEPS))
            my.did(dve.tensor_scalar(e_t, before, 0.0, None, ALU.is_equal))
            my.did(dve.tensor_tensor(e_s, before, after, ALU.add))
            my.after()
            my.did(dve.scalar_tensor_tensor(e_s, e_s, 1.0, e_t, ALU.add, ALU.mult))
            my.after()
            my.did(dve.scalar_tensor_tensor(e_s, dstN, float(NONE), e_s, ALU.is_lt, ALU.mult))
            my.after()
            my.did(dve.tensor_reduce(eflag[0:ER, 2:3], e_s, X, ALU.max))
            my.after()
            dve.nop().then_inc(s["flags"], 1)
            a_i, b_i, c_i = xorb[0], xorb[1], ahead[0]
            my.did(dve.tensor_scalar(a_i, srcN, P - 1, None, ALU.bitwise_and))
            my.did(dve.tensor_scalar(b_i, srcN, 7, None, ALU.logical_shift_right))
            my.did(dve.tensor_scalar(c_i, dstN, 7, None, ALU.logical_shift_right))
            my.after()
            my.did(dve.tensor_copy(e_b, c_i))
            my.after()
            my.did(dve.scalar_tensor_tensor(e_a, b_i, float(TPS), e_b, ALU.mult, ALU.add))
            my.after()
            my.did(dve.scalar_tensor_tensor(e_a, a_i, float(TILES * TPS), e_a, ALU.mult, ALU.add))
            my.after()
            per_strip = float(P * TILES * TPS - TPS)
            for k in range(1, STRIPS):
                my.did(dve.tensor_scalar(e_t, dstN, float(k * W), per_strip, ALU.is_ge, ALU.mult))
                my.after()
                my.did(dve.tensor_tensor(e_a, e_a, e_t, ALU.add))
                my.after()
            my.did(dve.tensor_scalar(c_i, dstN, P - 1, None, ALU.bitwise_and))
            my.after()
            my.did(dve.tensor_copy(e_t, c_i))
            my.after()
            dve.nop().then_inc(s["counted"], 1)
            for a, t in enumerate((hiT, loT, rowT, cntT)):
                dve.wait_ge(s["cols_ps"], a + 1)
                bank = psG[:, 2 * (a % 2):2 * (a % 2) + 2, :].rearrange("q a (b p) -> q p (a b)", p=P)[:, 0:ER, :]
                my.did(dve.tensor_copy(t.rearrange("q (p b) -> q p b", b=EB), bank))
                my.after()
                dve.nop().then_inc(s["cols_free"], 1)
            my.did(dve.scalar_tensor_tensor(idxT, hiT, 7, loT, ALU.logical_shift_left, ALU.bitwise_or))
            my.did(dve.tensor_scalar(bitT, cntT, 0.0, None, ALU.is_equal))
            my.after()
            my.did(dve.scalar_tensor_tensor(idxT, bitT, SKIP, idxT, ALU.logical_shift_left, ALU.bitwise_or))
            my.after()
            my.did(dve.tensor_scalar(bitT, cntT, 7, None, ALU.bitwise_and))
            my.after()
            my.did(dve.tensor_scalar(valT, bitT, 0.5, None, ALU.mult, saturate=False))
            my.after()
            dve.nop().then_inc(s["piece_vals"], 1)
            dve.wait_ge(s["flags_all"], 2)
            my.did(dve.tensor_scalar(piece_f[:, :], eflag_a[:, 2:3], 8.0, None, ALU.is_ge))
            my.after()
            for k in range(2, PIECES):
                my.did(dve.scalar_tensor_tensor(piece_f[:, :], eflag_a[:, 2:3], float(8 ** k), piece_f[:, :], ALU.is_ge, ALU.add))
                my.after()
            my.did(dve.tensor_copy(piece_n[:, :], piece_f[:, :]))
            my.did(dve.memset(piece_v[:, :], 0.5))
            my.after()
            dve.nop().then_inc(s["pieces_known"], 1)

            dve.wait_ge(s["weights_in"], 16 * LOADS)
            my.did(dve.tensor_tensor(w_1sq[:, :], w_1[:, :], w_1[:, :], ALU.mult))
            my.after()
            dve.nop().then_inc(s["sq_set"], 1)
            my.did(dve.tensor_tensor(c_gate[:, :], c_ih[:, :], c_hh[:, :], ALU.add))
            for k in range(LAYERS):
                my.did(dve.tensor_reduce(mx[:, k:k + 1], w_conv[:, k, :], X, ALU.max, apply_absolute_value=True))
            my.did(dve.tensor_reduce(mx[:, 7:8], w_2[:, :, :].rearrange("p a b -> p (a b)"), X, ALU.max, apply_absolute_value=True))
            my.did(dve.scalar_tensor_tensor(c_b1a[:, :], c_b1[:, :], -1.0, c_b1[:, :], ALU.mult, ALU.max))
            dve.wait_ge(s["norm_set"], 1)
            my.after()
            my.did(dve.scalar_tensor_tensor(norm2[:, :], norm2[:, :], NORM, c_b1a[:, :], ALU.mult, ALU.add))
            my.after()
            my.did(dve.tensor_reduce(mx[:, 6:7], norm2[:, :], X, ALU.max))
            dve.wait_ge(s["h0_set"], 2 * STRIPS)
            my.did(dve.tensor_reduce(mx[:, 5:6], hT[:, :], X, ALU.max, apply_absolute_value=True))
            my.after()
            dve.nop().then_inc(s["max_set"], 1)
            dve.wait_ge(s["max_all"], 1)
            my.did(dve.tensor_scalar(mxa[:, 5:6], mxa[:, 5:6], 1.0, None, ALU.max))
            my.after()
            my.did(dve.tensor_scalar(prod[:, 0:LAYERS], mxa[:, 0:LAYERS], mxa[:, 5:6], None, ALU.mult))
            my.did(dve.scalar_tensor_tensor(prod[:, 5:6], mxa[:, 6:7], 2.0, mxa[:, 7:8], ALU.mult, ALU.mult))
            my.after()
            my.did(dve.tensor_scalar(expo[:, :], prod[:, :].bitcast(i32), 23, None, ALU.logical_shift_right))
            my.after()
            my.did(dve.tensor_scalar(expo[:, :], expo[:, :], 8.0, 253.0, ALU.max, ALU.min))
            my.after()
            my.did(dve.tensor_scalar(scale_i[:, :], expo[:, :], -1.0, 261.0, ALU.mult, ALU.add))
            my.did(dve.tensor_scalar(undo_i[:, :], expo[:, :], -6.0, None, ALU.add))
            my.after()
            my.did(dve.tensor_scalar(scale_b[:, :], scale_i[:, :], 23, None, ALU.logical_shift_left))
            my.did(dve.tensor_scalar(undo_b[:, :], undo_i[:, :], 23, None, ALU.logical_shift_left))
            my.after()
            for k in range(LAYERS):
                my.did(dve.tensor_scalar(w_convs[:, k, :], w_conv[:, k, :], scale[:, k:k + 1], None, ALU.mult))
            my.did(dve.tensor_scalar(w_2s[:, :, :], w_2[:, :, :], scale[:, 5:6], None, ALU.mult))
            my.did(dve.tensor_scalar(undo_y[:, :], undo[:, 5:6], 0.5, None, ALU.mult))
            my.after()
            dve.nop().then_inc(s["scales_set"], 1)
            for t in range(STRIPS):
                dve.wait_ge(s["m0_hi"], t + 1)
                dve.tensor_tensor(parts[:, 1, t * W:(t + 1) * W], rows_ps, parts[:, 0, t * W:(t + 1) * W], ALU.subtract).then_inc(s["m0_lo"], 1)
            dve.wait_ge(s["m0_lo"], STRIPS)
            dve.nop().then_inc(s["src_ready"], 3)

            dve.wait_ge(s["iota_set"], 1)

            def hot(b, col):
                lo, hi = loT[:, bass.ds(col, EB)], rowT[:, bass.ds(col, EB)]
                dve.tensor_tensor(oh_lo[b], lo.unsqueeze(2).broadcast_to((P, EB, P)), iota[:, :].unsqueeze(1).broadcast_to((P, EB, P)),
                                  ALU.is_equal).then_inc(s["hot_set"], 1)
                dve.tensor_tensor(oh_hi[b], hi.unsqueeze(2).broadcast_to((P, EB, 64)), iota[:, 0:64].unsqueeze(1).broadcast_to((P, EB, 64)),
                                  ALU.is_equal).then_inc(s["hot_set"], 1)

            for b in range(2):
                hot(b, b * EB)
            with dve.Fori(1, ER // 2) as i:
                for b in range(2):
                    hold(dve, s["hot_used"], i * 2 + (b - 1))
                    hot(b, i * (2 * EB) + b * EB)
            dve.wait_ge(s["deg_ps"], 1)
            my.did(dve.tensor_scalar(deg, psA[0:64, 0, 0:P], 1.0, None, ALU.max))
            my.after()
            my.did(dve.reciprocal(deg, deg))
            my.after()
            dve.nop().then_inc(s["deg_set"], 1)

            more = dve.value_load(piece_n[0:1, 0:1], min_val=0, max_val=PIECES - 1)
            with dve.If(more > 0):
                dve.tensor_copy(rowT, cntT).then_inc(s["steps_piece"], 1)
                with dve.Fori(0, more) as k:
                    hold(dve, s["built"], k + 1)
                    st = Steps(dve, s["steps_piece"], hold, k * PIECE_STEPS + 1)
                    st.after()
                    st.did(dve.tensor_scalar(hiT, hiT, float(REG // P), None, ALU.add))
                    st.did(dve.tensor_scalar(piece_v[:, :], piece_v[:, :], 8.0, None, ALU.mult))
                    st.did(dve.tensor_scalar(bitT, cntT, 0.0, None, ALU.is_equal))
                    st.did(dve.tensor_scalar(rowT, rowT, 3, None, ALU.logical_shift_right))
                    st.after()
                    st.did(dve.scalar_tensor_tensor(idxT, hiT, 7, loT, ALU.logical_shift_left, ALU.bitwise_or))
                    st.after()
                    st.did(dve.scalar_tensor_tensor(idxT, bitT, SKIP, idxT, ALU.logical_shift_left, ALU.bitwise_or))
                    st.after()
                    st.did(dve.tensor_scalar(bitT, rowT, 7, None, ALU.bitwise_and))
                    st.after()
                    st.did(dve.tensor_scalar(valT, bitT, piece_v[:, 0:1], None, ALU.mult, saturate=False))
                    st.after()
                    assert st.n == PIECE_STEPS
                    dve.nop().then_inc(s["piece_vals"], 1)

            def sums_out(v, by):
                hold(dve, s["sums"], v + 1)
                dve.tensor_scalar(aggS[:, H:W], psA[:, 1, 0:H], by, None, ALU.mult).then_inc(s["sums_b"], 1)

            def promote(v):
                hold(dve, s["hi_set"], v)
                hold(dve, s["lo_set"], v)
                for k in range(2):
                    dve.tensor_copy(parts[:, k, 0:6 * W], later[:, k, :]).then_inc(s["src_ready"], 1)

            def low(v, target, source, by, hi):
                hold(dve, s["hi_set"], v + 1)
                if by is None:
                    dve.tensor_tensor(target, source, hi, ALU.subtract).then_inc(s["lo_set"], 1)
                else:
                    dve.scalar_tensor_tensor(target, source, by, hi, ALU.mult, ALU.subtract).then_inc(s["lo_set"], 1)
                hold(dve, s["lo_set"], v + 1)
                dve.nop().then_inc(s["src_ready"], 1)

            def gates(v, strip, st, relu):
                for b in range(2):
                    hb = slice(b * H, (b + 1) * H)
                    hold(dve, s["rz"], v * 4 + (2 * b + 1))
                    st.did(dve.scalar_tensor_tensor(t_g[:, hb], psG[:, 3, 0:H], c_hh[:, 2:3], r_g[:, hb], ALU.add, ALU.mult))
                    st.after()
                    dve.tensor_tensor(t_g[:, hb], psG[:, 2, 0:H], t_g[:, hb], ALU.add).then_inc(s["n_in"], 1)
                    hold(dve, s["n_set"], v * 2 + (b + 1))
                    st.did(dve.tensor_tensor(r_g[:, hb], hT[:, bass.ds(strip * W + b * H, H)], n_g[:, hb], ALU.subtract))
                    st.after()
                    st.did(dve.tensor_tensor(r_g[:, hb], z_g[:, hb], r_g[:, hb], ALU.mult))
                    st.after()
                    if relu:
                        st.did(dve.tensor_tensor(r_g[:, hb], n_g[:, hb], r_g[:, hb], ALU.add))
                        st.after()
                        dve.tensor_scalar(h_new[:, hb], r_g[:, hb], 0.0, None, ALU.max).then_inc(s["h_set"], 1)
                    else:
                        if b == 0:
                            hold(dve, s["h_kept"], v + 1)
                        dve.tensor_tensor(h_new[:, hb], n_g[:, hb], r_g[:, hb], ALU.add).then_inc(s["h_set"], 1)

            def gru(v, layer, strip):
                st = Steps(dve, s["steps_gru"], hold, v * GRU_STEPS)
                last = isinstance(strip, int)
                sums_out(v, undo[:, bass.ds(layer, 1)])
                if last:
                    promote(v)
                else:
                    dve.nop().then_inc(s["src_ready"], 2)
                gates(v, strip, st, False)
                pick = (lambda k: parts[:, k, 6 * W:7 * W]) if last else (lambda k: later[:, k, bass.ds(strip * W, W)])
                low(v, pick(1), rows_ps, None, pick(0))
                assert st.n == GRU_STEPS

            with dve.Fori(0, 4) as layer:
                with dve.Fori(0, STRIPS - 1) as strip:
                    gru(layer * STRIPS + strip, layer, strip)
                gru(layer * STRIPS + 6, layer, 6)
            dve.wait_ge(s["h_kept"], 4 * STRIPS + 1)

            def rows3(t):
                return t.rearrange("p (t f) -> p t f", f=F)

            def rows_of(t):
                return t.unsqueeze(1).broadcast_to((P, TPS, F))

            def normalise(st, value, target, n, free, when):
                for t in range(TPS):
                    st.did(dve.bn_stats(stats[:, t, :], rows3(value)[:, t, :]))
                st.after()
                for t in range(TPS):
                    st.did(dve.bn_aggr(mv[:, t, :], stats[:, t, :]))
                st.after()
                dve.nop().then_inc(s["var_set"], 1)
                hold(dve, s["dev_set"], n + 1)
                st.did(dve.reciprocal(rstd[:, :], dev[:, :]))
                st.after()
                if when is not None:
                    hold(dve, free, when)
                for t in range(TPS):
                    st.did(dve.tensor_scalar(rows3(target)[:, t, :], rows3(value)[:, t, :], mv[:, t, 0:1], rstd[:, t:t + 1],
                                             ALU.subtract, ALU.mult))
                st.after()

            def decoder(w, first, last):
                v = w + 4 * STRIPS
                st = Steps(dve, s["steps_dec"], hold, w * DEC_STEPS)
                sums_out(v, undo[:, 4:5])
                if last:
                    promote(v)
                else:
                    dve.nop().then_inc(s["src_ready"], 2)
                gates(v, w, st, True)
                hold(dve, s["dec2_ps"], w + 1)
                dve.tensor_tensor(rows3(o_s), rows3(rows_ps), rows_of(r_dec2[:, :]), ALU.add).then_inc(s["o_set"], 1)
                hold(dve, s["sig_set"], w + 1)
                hold(dve, s["x_rows"], 16 * 8 if last else w * 16 + 16)
                st.did(dve.tensor_tensor(o_s, t_g, x_s, ALU.add))
                st.after()
                dve.nop().then_inc(s["v_set"], 1)
                normalise(st, o_s, x1_s, w, s["x1_kept"], None if first else w * 16)
                dve.nop().then_inc(s["x1_set"], 1)
                pick = (lambda k: parts[:, k, 6 * W:7 * W]) if last else (lambda k: later[:, k, bass.ds(w * W, W)])
                low(v, pick(1), x1_s, X1_SCALE, pick(0))
                assert st.n == DEC_STEPS, st.n

            decoder(0, True, False)
            with dve.Fori(1, STRIPS - 1) as w:
                decoder(w, False, False)
            decoder(STRIPS - 1, False, True)

            def mean1(w, first, last):
                v = w + 5 * STRIPS
                st = Steps(dve, s["steps_s1"], hold, w * MEAN1_STEPS)
                sums_out(v, 2.0 / X1_SCALE)
                if last:
                    promote(v)
                else:
                    dve.nop().then_inc(s["src_ready"], 2)
                hold(dve, s["sums_a"], v + 1)
                hold(dve, s["sums_b"], v + 1)
                hold(dve, s["rdeg_in"], w * 16 + 16)
                st.did(dve.tensor_tensor(u_s, aggS, rdeg_s, ALU.mult))
                st.after()
                dve.tensor_tensor(u_s, u_s, hT[:, bass.ds(w * W, W)], ALU.add).then_inc(s["u_set"], 1)
                pick = (lambda k: parts[:, k, 6 * W:7 * W]) if last else (lambda k: later[:, k, bass.ds(w * W, W)])
                low(v, pick(1), rows_ps, None, pick(0))
                if not first:
                    hold(dve, s["y_kept"], w * 16)
                st.did(dve.tensor_scalar(y_s, rows_ps, undo_y[:, 0:1], None, ALU.mult))
                st.after()
                dve.nop().then_inc(s["y_set"], 1)

            mean1(0, True, False)
            with dve.Fori(1, STRIPS - 1) as w:
                mean1(w, False, False)
            mean1(STRIPS - 1, False, True)

            def mean2(w, first):
                v = w + 6 * STRIPS
                st = Steps(dve, s["steps_s2"], hold, w * MEAN2_STEPS)
                sums_out(v, undo[:, 5:6])
                dve.nop().then_inc(s["src_ready"], 3)
                hold(dve, s["sums_a"], v + 1)
                hold(dve, s["sums_b"], v + 1)
                hold(dve, s["last_in"], w * 48 + 48)
                dve.tensor_tensor(u_s, aggS, rdeg_s, ALU.mult).then_inc(s["mean_set"], 1)
                hold(dve, s["mean_ps"], w + 1)
                st.did(dve.tensor_tensor(o_w, rows_ps, y_s, ALU.add))
                st.after()
                dve.nop().then_inc(s["w_set"], 1)
                st.did(dve.tensor_tensor(rows3(o_w), rows3(o_w), rows_of(r_b2[:, :]), ALU.add))
                st.after()
                st.did(dve.scalar_tensor_tensor(o_w, o_w, 0.0, x_s, ALU.max, ALU.add))
                st.after()
                dve.nop().then_inc(s["v_set"], 1)
                normalise(st, o_w, x1_s, w + STRIPS, s["stored"], None if first else w * 16)
                dve.nop().then_inc(s["out_set"], 1)
                assert st.n == MEAN2_STEPS

            o_w = d1
            mean2(0, True)
            with dve.Fori(1, STRIPS) as w:
                mean2(w, False)

        @block.tensor
        def _(pe):
            tag[id(pe)] = "pe"
            pe.wait_ge(s["x_in"], 16)
            pe.wait_ge(s["weights_in"], 16 * LOADS)
            for j in range(2 * STRIPS):
                b = j % 2
                if j >= 2:
                    pe.wait_ge(s["e1_set"], j - 1)
                pe.matmul(psG[:, 2 * b, 0:H], w_enc1[:, :], hT[:, j * H:(j + 1) * H], start=True, stop=True).then_inc(s["hid_ps"], 1)
                if j >= 2:
                    pe.wait_ge(s["h0_set"], j - 1)
                pe.wait_ge(s["e1_set"], j + 1)
                pe.matmul(psG[:, 2 * b + 1, 0:H], w_enc2[:, :], e1[:, b * H:(b + 1) * H], start=True, stop=True).then_inc(s["h0_ps"], 1)
            pe.wait_ge(s["ident_set"], 2)
            pe.wait_ge(s["h0_set"], 2 * STRIPS)
            pe.wait_ge(s["counted"], 1)
            for a, t in enumerate((e_a, e_t, e_b, e_s)):
                if a >= 2:
                    pe.wait_ge(s["cols_free"], a - 1)
                for b in range(EB):
                    last = pe.matmul(psG[:, 2 * (a % 2) + b // 4, (b % 4) * P:(b % 4) * P + ER], t[:, b * P:(b + 1) * P],
                                     ident[0:ER, 0:ER], start=True, stop=True)
                last.then_inc(s["cols_ps"], 1)
            pe.wait_ge(s["sq_set"], 1)
            pe.wait_ge(s["consts"], 5)
            for k in range(2):
                last = pe.matmul(psM[:, k:k + 1], w_1sq[:, k * P:(k + 1) * P], ones[:, :], start=True, stop=True)
            last.then_inc(s["norm_ps"], 1)
            pe.wait_ge(s["norm_set"], 1)
            pe.wait_ge(s["scales_set"], 1)
            for t in range(STRIPS):
                if t:
                    pe.wait_ge(s["m0_lo"], t)
                for k in range(TPS):
                    last = pe.matmul(psM[:, k * P:(k + 1) * P], hT[:, (t * TPS + k) * P:(t * TPS + k + 1) * P], w_convs[:, 0, :],
                                     start=True, stop=True)
                last.then_inc(s["m0_ps"], 1)

            def degrees(b, first, last):
                for j in range(EB):
                    mm = pe.matmul(psA[0:64, 0, 0:P], oh_hi[b][:, j, :], oh_lo[b][:, j, :], start=first and j == 0, stop=last and j == EB - 1)
                return mm

            pe.wait_ge(s["hot_set"], 2)
            degrees(0, True, False).then_inc(s["hot_used"], 1)
            with pe.Fori(0, ER // 2 - 1) as i:
                hold(pe, s["hot_set"], i * 4 + 4)
                degrees(1, False, False).then_inc(s["hot_used"], 1)
                hold(pe, s["hot_set"], i * 4 + 6)
                degrees(0, False, False).then_inc(s["hot_used"], 1)
            pe.wait_ge(s["hot_set"], 2 * ER)
            degrees(1, False, True).then_inc(s["deg_ps"], 1)

            pe.wait_ge(s["pieces_known"], 1)
            more = pe.value_load(piece_n[0:1, 0:1], min_val=0, max_val=PIECES - 1)
            pe.nop().then_inc(s["x_free"], 1)
            pe.wait_ge(s["deg_set"], 1)

            def tile(slot, t, k, start, stop):
                for part in range(2):
                    lhsT = parts[:, part, t * P:(t + 1) * P]
                    for b in range(2):
                        last = pe.matmul(psA[:, b, 0:H], lhsT, slot[:, k * W + b * H:k * W + (b + 1) * H],
                                         start=start and part == 0, stop=stop and part == 1, skip_group_check=True)
                return last

            def chunk(u, c):
                slot = ring[:, c, :].bitcast(f8)
                if c == 0:
                    if not (isinstance(u, int) and u == 0):
                        hold(pe, s["sums_a"], u)
                        hold(pe, s["sums_b"], u)
                    hold(pe, s["src_ready"], u * 3 + 2)
                if c == STRIPS - 1:
                    hold(pe, s["src_ready"], u * 3 + 3)
                hold(pe, a_ready[c], u * 16 + 16)
                for k in range(TPS):
                    if c == STRIPS - 1 and k == TPS - 1:
                        with pe.If(more > 0):
                            with pe.Fori(0, more) as piece:
                                for cc in range(STRIPS):
                                    n = more * u * STRIPS + piece * STRIPS + cc
                                    hold(pe, s["x_ready"], n * 16 + 16)
                                    for kk in range(TPS):
                                        last = tile(spare[:, :].bitcast(f8), cc * TPS + kk, kk, False, False)
                                    last.then_inc(s["x_free"], 1)
                    last = tile(slot, c * TPS + k, k, c == 0 and k == 0, c == STRIPS - 1 and k == TPS - 1)
                if c < STRIPS - 1:
                    last.then_inc(a_free[c], 1)
                else:
                    last.then_inc(s["sums"], 1)

            def chunks(u, a, b):
                for c in range(a, b):
                    chunk(u, c)

            def gates(v, strip, b):
                h = hT[:, bass.ds(strip * W + b * H, H)]
                if not (isinstance(v, int) and v == 0 and b == 0):
                    hold(pe, s["rz"], v * 4 + 2 * b)
                    hold(pe, s["n_in"], v * 2 + b)
                for g, bank in ((0, 0), (1, 1), (2, 3)):
                    pe.matmul(psG[:, bank, 0:H], w_hh[:, g * P:(g + 1) * P], h, start=True, stop=g == 2)
                hold(pe, s["sums_a"] if b == 0 else s["sums_b"], v + 1)
                for g in range(3):
                    last = pe.matmul(psG[:, g, 0:H], w_ih[:, g * P:(g + 1) * P], aggS[:, b * H:(b + 1) * H], start=g == 2, stop=True)
                last.then_inc(s["gates"], 1)

            def gru(v, layer, strip, first):
                gates(v, strip, 0)
                chunks(v + 1, 0, 1)
                gates(v, strip, 1)
                chunks(v + 1, 1, 4)
                hold(pe, s["h_set"], v * 2 + 2)
                if not first:
                    hold(pe, s["lo_set"], v)
                for k in range(TPS):
                    last = pe.matmul(psM[:, k * P:(k + 1) * P], h_new[:, k * P:(k + 1) * P], w_convs[:, bass.ds(layer + 1, 1), :].rearrange("p a b -> p (a b)"),
                                     start=True, stop=True)
                last.then_inc(s["rows_m"], 1)
                chunks(v + 1, 4, 7)

            chunks(0, 0, 7)
            gru(0, 0, 0, True)
            with pe.Fori(1, STRIPS) as strip:
                gru(strip, 0, strip, False)
            with pe.Fori(1, 4) as layer:
                with pe.Fori(0, STRIPS) as strip:
                    hold(pe, s["h_kept"], (layer - 1) * STRIPS + strip + 2)
                    gru(layer * STRIPS + strip, layer, strip, False)

            def decoder(w, first):
                v = w + 4 * STRIPS
                hold(pe, s["h_kept"], w + (3 * STRIPS + 2))
                if not first:
                    hold(pe, s["x1T_set"], w)
                gates(v, w, 0)
                chunks(v + 1, 0, 1)
                gates(v, w, 1)
                chunks(v + 1, 1, 3)
                hold(pe, s["h_set"], v * 2 + 2)
                hold(pe, s["rz"], v * 4 + 4)
                for b in range(2):
                    last = pe.matmul(psG[:, b, 0:H], w_dec1[:, :], h_new[:, b * H:(b + 1) * H], start=True, stop=True)
                last.then_inc(s["dec1_ps"], 1)
                chunks(v + 1, 3, 4)
                hold(pe, s["d1_set"], w + 1)
                if first:
                    pe.wait_ge(s["lo_set"], 4 * STRIPS)
                else:
                    hold(pe, s["o_set"], w)
                for k in range(TPS):
                    last = pe.matmul(psM[:, k * P:(k + 1) * P], d1[:, k * P:(k + 1) * P], w_dec2[:, :], start=True, stop=True)
                last.then_inc(s["dec2_ps"], 1)
                chunks(v + 1, 4, 6)
                hold(pe, s["x1_set"], w + 1)
                hold(pe, s["n_in"], v * 2 + 2)
                for k in range(TPS):
                    last = pe.matmul(x1T_ps[:, k * P:(k + 1) * P], x1_s[:, k * P:(k + 1) * P], ident[:, :], start=True, stop=True)
                last.then_inc(s["x1T_ps_set"], 1)
                chunks(v + 1, 6, 7)

            decoder(0, True)
            with pe.Fori(1, STRIPS) as w:
                decoder(w, False)
            pe.wait_ge(s["x1T_set"], STRIPS)
            pe.wait_ge(s["d1_set"], STRIPS)
            pe.wait_ge(s["o_set"], STRIPS)

            def mean1(w, first):
                v = w + 5 * STRIPS
                chunks(v + 1, 0, 1)
                hold(pe, s["u_set"], w + 1)
                if not first:
                    hold(pe, s["h1_set"], w * 2)
                for hb in range(2):
                    for b in range(2):
                        last = pe.matmul(psG[:, 2 * hb + b, 0:H], w_1[:, hb * P:(hb + 1) * P], u_s[:, b * H:(b + 1) * H], start=True, stop=True)
                last.then_inc(s["hid1_ps"], 1)
                chunks(v + 1, 1, 3)
                hold(pe, s["h1_set"], w * 2 + 2)
                if not first:
                    hold(pe, s["y_set"], w)
                for k in range(TPS):
                    for hb, t in enumerate((h1a, h1b)):
                        last = pe.matmul(psM[:, k * P:(k + 1) * P], t[:, k * P:(k + 1) * P], w_2s[:, hb, :], start=hb == 0, stop=hb == 1)
                last.then_inc(s["y_ps"], 1)
                chunks(v + 1, 3, 7)

            mean1(0, True)
            with pe.Fori(1, STRIPS) as w:
                mean1(w, False)
            pe.wait_ge(s["y_set"], STRIPS)

            def mean2(w, first):
                hold(pe, s["mean_set"], w + 1)
                if not first:
                    hold(pe, s["w_set"], w)
                for k in range(TPS):
                    last = pe.matmul(psM[:, k * P:(k + 1) * P], u_s[:, k * P:(k + 1) * P], ident[:, :], start=True, stop=True)
                last.then_inc(s["mean_ps"], 1)

            v0 = 6 * STRIPS
            chunks(v0 + 1, 0, 2)
            mean2(0, True)
            chunks(v0 + 1, 2, 7)
            with pe.Fori(1, STRIPS - 1) as w:
                chunks(w + (v0 + 1), 0, 2)
                mean2(w, False)
                chunks(w + (v0 + 1), 2, 7)
            mean2(STRIPS - 1, False)


_INS = ["x", "xT", "src", "dst", "enc_w1T", "enc_b1", "enc_w2T", "enc_b2", "conv_w", "wihT", "whhT", "bih", "bhh",
        "dec_w1T", "dec_b1", "dec_w2T", "dec_b2", "W1", "b1", "W2", "b2"]


def kernel(x, src, dst, L0_gnn_enc_w1, L0_gnn_enc_b1, L0_gnn_enc_w2, L0_gnn_enc_b2, L0_gnn_conv_w, L0_gnn_gru_wih,
           L0_gnn_gru_whh, L0_gnn_gru_bih, L0_gnn_gru_bhh, L0_gnn_dec_w1, L0_gnn_dec_b1, L0_gnn_dec_w2, L0_gnn_dec_b2,
           L1_gnn_W1, L1_gnn_b1, L1_gnn_W2, L1_gnn_b2):
    import numpy as np
    import concourse.bacc as bacc
    from concourse.bass_utils import run_bass_kernel_spmd as run

    nc = bacc.Bacc("TRN2", target_bir_lowering=False, num_devices=1)

    def t(a):
        return np.ascontiguousarray(np.asarray(a).T)

    given = [x, t(x), src, dst, t(L0_gnn_enc_w1), L0_gnn_enc_b1, t(L0_gnn_enc_w2), L0_gnn_enc_b2, L0_gnn_conv_w,
             t(L0_gnn_gru_wih), t(L0_gnn_gru_whh), L0_gnn_gru_bih, L0_gnn_gru_bhh, t(L0_gnn_dec_w1), L0_gnn_dec_b1,
             t(L0_gnn_dec_w2), L0_gnn_dec_b2, L1_gnn_W1, L1_gnn_b1, L1_gnn_W2, L1_gnn_b2]
    arrays, args = {}, []
    for name, a in zip(_INS, given):
        a = np.ascontiguousarray(a)
        arrays[f"in_{name}"] = a
        args.append(nc.dram_tensor(f"in_{name}", a.shape, mybir.dt.from_np(a.dtype), kind="ExternalInput").ap())
    out = nc.dram_tensor("rows_out", (NODES, F), mybir.dt.float32, kind="ExternalOutput").ap()
    gnn_kernel(nc, *args, out)
    r = run(nc, [arrays], core_ids=[0])
    return r.results[0]["rows_out"]
```

```python
import concourse.bass as bass
from concourse import mybir
from contextlib import ExitStack

NODES, F, EDGES, LAYERS, HID = 6250, 128, 100000, 5, 256
P = 128
STRIPS = 7
TILES = 49
TPS = TILES // STRIPS
W = TPS * P
H = W // 2
NPAD = TILES * P
CH = TPS * W
REG = STRIPS * P * TILES * W
PIECES = 6
TAIL = NODES - (TILES - 1) * P
EC = 1024
ER = -(-EDGES // EC)
EP = ER * EC
EB = EC // P
NONE = 8191
KEY = 0x20000000
FAR = ER - 1
SKIP = 30
UNITS = 7 * STRIPS
X1_SCALE = 2048.0
NORM = 22.65
LOADS = 22
GRU_STEPS, DEC_STEPS, MEAN1_STEPS, MEAN2_STEPS, PIECE_STEPS = 6, 31, 2, 25, 8


class Steps:

    def __init__(self, engine, sem, hold, base=0):
        self.engine, self.sem, self.hold, self.base, self.n = engine, sem, hold, base, 0

    def did(self, instruction):
        instruction.then_inc(self.sem, 1)
        self.n += 1

    def after(self):
        self.hold(self.engine, self.sem, self.base + self.n)


def gnn_kernel(nc, x, xT, src, dst, enc_w1T, enc_b1, enc_w2T, enc_b2, conv_w, wihT, whhT, bih, bhh,
               dec_w1T, dec_b1, dec_w2T, dec_b2, W1, b1, W2, b2, out):
    dt = mybir.dt
    fp32, i32, f16, f8, u8, bf16 = dt.float32, dt.int32, dt.float16, dt.float8e5, dt.uint8, dt.bfloat16
    ALU = mybir.AluOpType
    ACT = mybir.ActivationFunctionType
    X = mybir.AxisListType.X
    RMAX = bass.bass_isa.ReduceOp.max

    A = nc.dram_tensor("edge_counts", (PIECES * REG, 1), u8, kind="Internal").ap()
    A_p = A.rearrange("(k s p x) o -> k s p (x o)", k=PIECES, s=STRIPS, p=P)
    A_z = A.rearrange("(k c p x) o -> k c p (x o)", k=PIECES, p=P, x=CH)
    ZC = REG // (P * CH)
    keys = nc.dram_tensor("edge_keys", (3 * EP,), i32, kind="Internal").ap()
    rdeg_d = nc.dram_tensor("inverse_degree", (TILES, P), fp32, kind="Internal").ap()
    x1_d = nc.dram_tensor("x1_rows", (STRIPS, P, W), fp32, kind="Internal").ap()
    y_d = nc.dram_tensor("y_rows", (STRIPS, P, W), fp32, kind="Internal").ap()
    x_t = x[0:(TILES - 1) * P, :].rearrange("(t p) f -> p t f", p=P)
    out_t = out[0:(TILES - 1) * P, :].rearrange("(t p) f -> p t f", p=P)

    ctx = ExitStack()
    with ctx:
        def sb(name, shape, d=fp32):
            return ctx.enter_context(nc.sbuf_tensor(name, shape, d))

        def sem(name):
            return ctx.enter_context(nc.semaphore(name))

        hT = sb("hT", [P, NPAD])
        parts = sb("parts", [P, 2, NPAD], f16)
        later = sb("later", [P, 2, 6 * W], f16)
        ring = sb("ring", [P, STRIPS, CH // 4])
        spare = sb("spare", [P, CH // 4])
        work = sb("work", [P, 10, W])
        w_enc1, w_enc2 = sb("w_enc1", [P, P]), sb("w_enc2", [P, P])
        w_dec1, w_dec2 = sb("w_dec1", [P, P]), sb("w_dec2", [P, P])
        w_conv, w_convs = sb("w_conv", [P, LAYERS, P]), sb("w_convs", [P, LAYERS, P])
        w_ih, w_hh = sb("w_ih", [P, 3 * P]), sb("w_hh", [P, 3 * P])
        w_1 = sb("w_1", [P, HID])
        w_2, w_2s = sb("w_2", [P, 2, P]), sb("w_2s", [P, 2, P])
        w_1sq = sb("w_1sq", [P, HID])
        ident = sb("ident", [P, P])
        ones = sb("ones", [P, 1])
        eps = sb("eps", [P, 1])
        c_enc1, c_enc2, c_dec1 = sb("c_enc1", [P, 1]), sb("c_enc2", [P, 1]), sb("c_dec1", [P, 1])
        c_ih, c_hh, c_gate = sb("c_ih", [P, 3]), sb("c_hh", [P, 3]), sb("c_gate", [P, 3])
        c_b1, c_b1a = sb("c_b1", [P, 2]), sb("c_b1a", [P, 2])
        r_dec2, r_b2 = sb("r_dec2", [P, P]), sb("r_b2", [P, P])
        stats, mv = sb("stats", [P, TPS, 6]), sb("mv", [P, TPS, 2])
        dev, rstd = sb("dev", [P, TPS]), sb("rstd", [P, TPS])
        mx, mxa = sb("mx", [P, 8]), sb("mxa", [P, 8])
        prod, expo, scale_i, undo_i = sb("prod", [P, 6]), sb("expo", [P, 6], i32), sb("scale_i", [P, 6], i32), sb("undo_i", [P, 6], i32)
        scale_b, undo_b = sb("scale_b", [P, 6], i32), sb("undo_b", [P, 6], i32)
        scale, undo = scale_b[:, :].bitcast(fp32), undo_b[:, :].bitcast(fp32)
        undo_y = sb("undo_y", [P, 1])
        norm2 = sb("norm2", [P, 2])
        eflag, eflag_a = sb("eflag", [P, 12]), sb("eflag_a", [P, 12])
        lag_f, lag_i = sb("lag_f", [P, 2]), sb("lag_i", [P, 2], i32)
        lag_n = sb("lag_n", [P, 2], i32)
        rows_min, row_no, ends = sb("rows_min", [P, 1]), sb("row_no", [P, 1], i32), sb("ends", [P, STRIPS], i32)
        row_f, ends_f = sb("row_f", [P, 1]), sb("ends_f", [P, STRIPS])
        strip_i, strip_n = sb("strip_i", [P, STRIPS], i32), sb("strip_n", [P, STRIPS], i32)
        ident_b = sb("ident_b", [P, P], bf16)
        piece_f, piece_n = sb("piece_f", [P, 1]), sb("piece_n", [P, 1], i32)
        piece_v = sb("piece_v", [P, 1])
        idx_s, val_s = sb("idx_s", [P, 2, EB], i32), sb("val_s", [P, 2, EB], u8)
        iota = sb("iota", [P, P], i32)
        aggS, r_g, z_g, t_g, n_g, h_new = (work[:, i, :] for i in range(6))
        d1, o_s, x_s, x1_s = (work[:, i, :] for i in (6, 7, 8, 9))
        rdeg_s, u_s, h1a, h1b, y_s = (work[:, i, :] for i in (1, 2, 3, 4, 7))
        e1 = ring[:, :, :].rearrange("p a b -> p (a b)")[:, 9 * EC:9 * EC + W]
        ebuf = ring[:, :, :].rearrange("p a b -> p (a b)").bitcast(i32)

        def erow(i):
            return ebuf[0:ER, i * EC:(i + 1) * EC]

        srcN, dstN, keyN = erow(0), erow(1), erow(2)
        keysB, keysA = ebuf[0:ER, 3 * EC:5 * EC], ebuf[0:ER, 5 * EC:7 * EC]
        eqb = ebuf[0:ER, 7 * EC:9 * EC].bitcast(bf16)
        eqB, eqA = [eqb[:, b * EC:(b + 1) * EC] for b in range(2)], [eqb[:, (2 + b) * EC:(3 + b) * EC] for b in range(2)]
        padB, padA = erow(7), erow(8)
        pbuf = parts[:, :, :].rearrange("p a b -> p (a b)").bitcast(i32)
        dstH = pbuf[0:ER, 0:2 * EC]
        same = pbuf[0:ER, 2 * EC:4 * EC].bitcast(fp32)
        wbuf = work[:, :, :].rearrange("p a b -> p (a b)")
        run = wbuf[0:ER, 0:2 * EC]
        a_i, b_i, c_i, d_i = (pbuf[0:ER, i * EC:(i + 1) * EC] for i in (4, 5, 0, 1))
        e_t, e_s, e_a, e_b = (wbuf[0:ER, (4 + i) * EC:(5 + i) * EC] for i in range(4))
        COLS = ER * EB
        lbuf = later[:, :, :].rearrange("p a b -> p (a b)").bitcast(i32)

        def ecol(i):
            return lbuf[:, i * COLS:(i + 1) * COLS]

        hiT, loT, rowT, cntT, idxT, bitT = (ecol(i) for i in range(6))
        valT = lbuf[:, 6 * COLS:6 * COLS + COLS // 4].bitcast(f8)
        oh_lo = [wbuf[:, i * 512:(i + 1) * 512].bitcast(bf16).rearrange("p (b c) -> p b c", c=P) for i in range(2)]
        oh_hi = [wbuf[:, (4 + i) * 256:(5 + i) * 256].bitcast(bf16).rearrange("p (b c) -> p b c", c=64) for i in range(2)]
        deg = wbuf[0:64, 1536:1536 + P]
        zeros = spare[:, :].bitcast(u8)

        psA = ctx.enter_context(nc.psum_tensor("psA", [P, 2, 512], fp32))
        psG = ctx.enter_context(nc.psum_tensor("psG", [P, 4, 512], fp32))
        psM = ctx.enter_context(nc.psum_tensor("psM", [P, 1024], fp32))
        rows_ps = psM[:, 0:W]
        x1T_ps = psG[:, 2:4, :].rearrange("p a b -> p (a b)")[:, 0:W]

        seen = {e: sem(f"passed_{e}") for e in ("pe", "act", "dve", "pool", "sp")}
        names = """edges_in weights_in x_in consts zeros_set ident_set iota_set pads_set keys_out halo_in flags
            flags_all lags_known eq_used eq_set counts_ps after_set places_set fields_set fields_f counted edge_cols
            cols_ps cols_dve cols_act pieces_known strips_known row_set more_keys keys_used ident_b_set max_set max_all
            hid_ps e1_set h0_ps h0_set h0_max sq_set norm_ps norm_set scales_set m0_ps m0_hi m0_lo built piece_vals
            staged zero_filled hot_set hot_used deg_ps deg_set deg_out src_ready sums sums_a sums_b gates rz
            n_in n_set h_set h_kept rows_m hi_set lo_set dec1_ps d1_set dec2_ps o_set sig_set x_rows v_set var_set
            dev_set x1_set x1_kept x1T_ps_set x1T_set rdeg_in u_set hid1_ps h1_set y_ps y_set y_kept last_in mean_set
            mean_ps w_set out_set stored x_free steps_dve steps_lag steps_gru steps_dec steps_s1 steps_s2
            x_ready tail_set steps_piece""".split()
        s = {n: sem(n) for n in names}
        a_ready = [sem(f"a_ready{c}") for c in range(STRIPS)]
        a_free = [sem(f"a_free{c}") for c in range(STRIPS - 1)]
        scattered = [sem(f"scattered{b}") for b in range(2)]
        tag = {}

        def hold(engine, semaphore, value):
            engine.wait_ge(semaphore, value)
            if not isinstance(value, int):
                engine.nop().then_inc(seen[tag[id(engine)]], 1)

        block = ctx.enter_context(nc.Block())

        @block.sync
        def _(sp):
            tag[id(sp)] = "sp"
            full = EDGES // EC
            rest = EDGES - full * EC
            sp.wait_ge(s["pads_set"], 4)
            for d, t in ((src, srcN), (dst, dstN)):
                sp.dma_start(t[0:full, :], d[0:full * EC].rearrange("(p c) -> p c", c=EC)).then_inc(s["edges_in"], 16)
                sp.dma_start(t[full:ER, 0:rest], d[full * EC:EDGES].rearrange("(p c) -> p c", c=rest)).then_inc(s["edges_in"], 16)
            sp.dma_start(keys[0:EP].rearrange("(p c) -> p c", c=EC), padB).then_inc(s["keys_out"], 16)
            sp.dma_start(keys[2 * EP:3 * EP].rearrange("(p c) -> p c", c=EC), padA).then_inc(s["keys_out"], 16)
            sp.wait_ge(s["steps_dve"], 2)
            sp.dma_start(keys[EP:2 * EP].rearrange("(p c) -> p c", c=EC), keyN).then_inc(s["keys_out"], 16)
            sp.wait_ge(s["keys_out"], 48)

            def two_rows(start):
                return bass.AP(keys.tensor, start, [[EC, ER], [1, 2 * EC]])

            sp.dma_start(keysB, two_rows(EP - EC)).then_inc(s["halo_in"], 16)
            sp.dma_start(keysA, two_rows(EP)).then_inc(s["more_keys"], 16)
            sp.wait_ge(s["lags_known"], 1)
            far = sp.value_load(lag_n[0:1, 1:2], min_val=0, max_val=FAR)
            with sp.If(far > 0):
                with sp.Fori(0, far) as q:
                    hold(sp, s["keys_used"], q + 1)
                    sp.dma_start(keysB, two_rows((EP - 2 * EC) - q * EC)).then_inc(s["halo_in"], 16)
                    sp.dma_start(keysA, two_rows((EP + EC) + q * EC)).then_inc(s["more_keys"], 16)
            sp.wait_ge(s["pieces_known"], 1)
            more = sp.value_load(piece_n[0:1, 0:1], min_val=0, max_val=PIECES - 1)
            with sp.If(more > 0):
                with sp.Fori(0, more) as k:
                    for c in range(ZC):
                        sp.dma_start(A_z[bass.ds(k + 1, 1), c, :, :].rearrange("k p x -> (k p) x"), zeros).then_inc(s["zero_filled"], 16)
                hold(sp, s["built"], more + 1)

            def loads(unit, strip):
                for c in range(STRIPS):
                    if not isinstance(unit, int):
                        hold(sp, a_free[c] if c < STRIPS - 1 else s["sums"], unit)
                    a = A_p[0, bass.ds(strip, 1), :, c * CH:(c + 1) * CH].rearrange("s p x -> (s p) x")
                    sp.dma_start(ring[:, c, :].bitcast(u8), a).then_inc(a_ready[c], 16)
                with sp.If(more > 0):
                    with sp.Fori(0, more) as k:
                        for c in range(STRIPS):
                            n = more * unit * STRIPS + k * STRIPS + c
                            hold(sp, s["x_free"], n + 1)
                            a = A_p[bass.ds(k + 1, 1), bass.ds(strip, 1), :, c * CH:(c + 1) * CH].rearrange("k s p x -> (k s p) x")
                            sp.dma_start(spare[:, :].bitcast(u8), a).then_inc(s["x_ready"], 16)

            sp.wait_ge(s["strips_known"], 1)

            def strip_built(strip):
                at = sp.value_load(strip_n[0:1, bass.ds(strip, 1)], min_val=P, max_val=P * ER // 2)
                for b in range(2):
                    hold(sp, scattered[b], at)

            strip_built(0)
            loads(0, 0)
            with sp.Fori(1, STRIPS) as strip:
                strip_built(strip)
                loads(strip, strip)
            hold(sp, s["built"], more + 1)
            with sp.Fori(1, 7) as layer:
                with sp.Fori(0, STRIPS) as strip:
                    loads(layer * STRIPS + strip, strip)

        @block.gpsimd
        def _(pool):
            tag[id(pool)] = "pool"
            pool.memset(zeros, 0).then_inc(s["zeros_set"], 1)
            pool.memset(ident[:, :], 0.0).then_inc(s["ident_set"], 1)
            pool.wait_ge(s["ident_set"], 1)
            pool.affine_select(out=ident[:, :], in_=ident[:, :], compare_op=ALU.not_equal, fill=1.0, base=0,
                               pattern=[[-1, P]], channel_multiplier=1).then_inc(s["ident_set"], 1)
            pool.iota(iota[:, :], pattern=[[1, P]], base=0, channel_multiplier=0).then_inc(s["iota_set"], 1)
            pool.iota(row_no[:, :], pattern=[[0, 1]], base=1, channel_multiplier=1).then_inc(s["row_set"], 1)
            pool.iota(ends[:, :], pattern=[[W, STRIPS]], base=W, channel_multiplier=0).then_inc(s["row_set"], 1)
            pool.wait_ge(s["flags"], 1)
            pool.partition_all_reduce(eflag_a[:, 0:2], eflag[:, 0:2], P, RMAX).then_inc(s["flags_all"], 1)
            pool.wait_ge(s["flags"], 2)
            pool.partition_all_reduce(eflag_a[:, 2:10], eflag[:, 2:10], P, RMAX).then_inc(s["flags_all"], 1)

            def group(b, col, base, i):
                if i is not None:
                    hold(pool, scattered[b], base * (16 * EB * ER // 2) + i * (16 * EB))
                pool.tensor_copy(idx_s[:, b, :], idxT[:, bass.ds(col, EB)]).then_inc(s["staged"], 1)
                pool.tensor_copy(val_s[:, b, :], valT.bitcast(u8)[:, bass.ds(col, EB)]).then_inc(s["staged"], 1)
                at = base * (2 * ER) + (2 * b + 2) + (0 if i is None else i * 4)
                hold(pool, s["staged"], at)
                for j in range(EB):
                    pool.indirect_dma_start(A, bass.IndirectOffsetOnAxis(ap=idx_s[:, b, j:j + 1], axis=0),
                                            val_s[:, b, j:j + 1], None, bounds_check=PIECES * REG - 1,
                                            oob_is_err=False).then_inc(scattered[b], 16)

            def scatter(piece, first=False):
                for b in range(2):
                    group(b, b * EB, piece, None)

                def pairs(a, z):
                    with pool.Fori(a, z) as i:
                        for b in range(2):
                            group(b, i * (2 * EB) + b * EB, piece, i)

                if first:
                    pairs(1, 5)
                    pool.wait_ge(s["max_set"], 1)
                    pool.partition_all_reduce(mxa[:, :], mx[:, :], P, RMAX).then_inc(s["max_all"], 1)
                    pairs(5, ER // 2)
                else:
                    pairs(1, ER // 2)
                for b in range(2):
                    hold(pool, scattered[b], (piece + 1) * (16 * EB * ER // 2))
                pool.nop().then_inc(s["built"], 1)

            pool.wait_ge(s["piece_vals"], 1)
            pool.wait_ge(s["zero_filled"], 16 * ZC)
            scatter(0, True)
            more = pool.value_load(piece_n[0:1, 0:1], min_val=0, max_val=PIECES - 1)
            with pool.If(more > 0):
                with pool.Fori(0, more) as k:
                    hold(pool, s["piece_vals"], k + 2)
                    hold(pool, s["zero_filled"], (k + 2) * (16 * ZC))
                    scatter(k + 1)

            pool.nop().then_inc(s["h_kept"], 1)
            with pool.Fori(0, 4) as layer:
                with pool.Fori(0, STRIPS) as strip:
                    v = layer * STRIPS + strip
                    hold(pool, s["h_set"], v * 2 + 2)
                    pool.tensor_copy(hT[:, bass.ds(strip * W, W)], h_new).then_inc(s["h_kept"], 1)

            def rows3(t):
                return t.rearrange("p (t f) -> p t f", f=F)

            def decoder(w, last):
                if not last:
                    pool.dma_start(rows3(x_s), x_t[:, bass.ds(w * TPS, TPS), :]).then_inc(s["x_rows"], 16)
                else:
                    k = TPS - 1
                    pool.memset(rows3(x_s)[:, k, :], 0.0).then_inc(s["tail_set"], 1)
                    pool.wait_ge(s["tail_set"], 1)
                    pool.dma_start(rows3(x_s)[:, 0:k, :], x_t[:, w * TPS:w * TPS + k, :]).then_inc(s["x_rows"], 16)
                    pool.wait_ge(s["x_rows"], 16 * 7)
                    pool.dma_start(rows3(x_s)[0:TAIL, k, :], x[(TILES - 1) * P:NODES, :]).then_inc(s["x_rows"], 16)
                hold(pool, s["x1_set"], w + 1)
                pool.dma_start(x1_d[bass.ds(w, 1), :, :].rearrange("s p x -> (s p) x"), x1_s).then_inc(s["x1_kept"], 16)

            decoder(0, False)
            with pool.Fori(1, STRIPS - 1) as w:
                decoder(w, False)
            decoder(STRIPS - 1, True)

            def rdeg_load(w, done):
                a = rdeg_d[bass.ds(w * TPS, TPS), :].rearrange("t p -> (t p)").partition_broadcast(P)
                pool.dma_start(rdeg_s, a).then_inc(done, 16)

            pool.wait_ge(s["deg_out"], 16)
            pool.wait_ge(s["x1_kept"], 16 * STRIPS)
            rdeg_load(0, s["rdeg_in"])
            with pool.Fori(0, STRIPS - 1) as w:
                hold(pool, s["u_set"], w + 1)
                rdeg_load(w + 1, s["rdeg_in"])
                hold(pool, s["y_set"], w + 1)
                pool.dma_start(y_d[bass.ds(w, 1), :, :].rearrange("s p x -> (s p) x"), y_s).then_inc(s["y_kept"], 16)
            pool.wait_ge(s["y_set"], STRIPS)
            pool.dma_start(y_d[STRIPS - 1, :, :], y_s).then_inc(s["y_kept"], 16)
            pool.wait_ge(s["y_kept"], 16 * STRIPS)

            def last_loads(w):
                rdeg_load(w, s["last_in"])
                pool.dma_start(y_s, y_d[bass.ds(w, 1), :, :].rearrange("s p x -> (s p) x")).then_inc(s["last_in"], 16)
                pool.dma_start(x_s, x1_d[bass.ds(w, 1), :, :].rearrange("s p x -> (s p) x")).then_inc(s["last_in"], 16)

            last_loads(0)
            with pool.Fori(0, STRIPS - 1) as w:
                hold(pool, s["v_set"], w + (STRIPS + 1))
                last_loads(w + 1)
                hold(pool, s["out_set"], w + 1)
                pool.dma_start(out_t[:, bass.ds(w * TPS, TPS), :], rows3(x1_s)).then_inc(s["stored"], 16)
            pool.wait_ge(s["out_set"], STRIPS)
            k = TPS - 1
            pool.dma_start(out_t[:, (STRIPS - 1) * TPS:, :], rows3(x1_s)[:, 0:k, :]).then_inc(s["stored"], 16)
            pool.dma_start(out[(TILES - 1) * P:NODES, :], rows3(x1_s)[0:TAIL, k, :]).then_inc(s["stored"], 16)
            pool.wait_ge(s["stored"], 16 * (STRIPS + 1))

        @block.scalar
        def _(act):
            tag[id(act)] = "act"
            act.wait_ge(s["pads_set"], 5)
            act.dma_start(hT[:, 0:NODES], xT).then_inc(s["x_in"], 16)

            loads = [(w_enc1[:, :], enc_w1T), (w_enc2[:, :], enc_w2T),
                     (w_conv[:, :, :], conv_w.rearrange("l k f -> k l f")), (w_ih[:, :], wihT), (w_hh[:, :], whhT),
                     (w_dec1[:, :], dec_w1T),
                     (w_dec2[:, :], dec_w2T), (r_dec2[:, :], dec_b2.partition_broadcast(P)), (w_1[:, :], W1),
                     (w_2[:, :, :], W2.rearrange("(h k) f -> k h f", k=P)), (r_b2[:, :], b2.partition_broadcast(P))]
            for t, a in ((c_enc1, enc_b1), (c_enc2, enc_b2), (c_ih, bih), (c_hh, bhh), (c_dec1, dec_b1), (c_b1, b1)):
                for g in range(a.shape[0] // P):
                    loads.append((t[:, g:g + 1], a[g * P:(g + 1) * P].rearrange("(p o) -> p o", o=1)))
            assert len(loads) == LOADS
            for t, a in loads:
                act.dma_start(t, a).then_inc(s["weights_in"], 16)
            act.wait_ge(s["zeros_set"], 1)
            for c in range(ZC):
                act.dma_start(A_z[0, c, :, :], zeros).then_inc(s["zero_filled"], 16)

            act.wait_ge(s["ident_set"], 2)
            act.activation(ident_b[:, :], ident[:, :], ACT.Copy).then_inc(s["ident_b_set"], 1)
            act.wait_ge(s["fields_set"], 1)
            act.activation(e_b, c_i, ACT.Copy).then_inc(s["fields_f"], 1)
            act.activation(e_t, d_i, ACT.Copy).then_inc(s["fields_f"], 1)
            act.wait_ge(s["counts_ps"], 1)
            act.activation(e_s, psM[0:ER, :], ACT.Copy, bias=1.0).then_inc(s["after_set"], 1)

            def columns(t, banks):
                a = psG[:, banks:banks + 2, :].rearrange("q a (b p) -> q p (a b)", p=P)[:, 0:ER, :]
                return t.rearrange("q (p b) -> q p b", b=EB), a

            for a, t in ((2, loT), (4, rowT)):
                act.wait_ge(s["cols_ps"], a)
                o, i = columns(t, 2)
                act.activation(o, i, ACT.Copy).then_inc(s["cols_act"], 1)

            act.wait_ge(s["weights_in"], 16 * LOADS)
            for j in range(2 * STRIPS):
                b = j % 2
                act.wait_ge(s["hid_ps"], j + 1)
                act.activation(e1[:, b * H:(b + 1) * H], psG[:, 2 * b, 0:H], ACT.Relu, bias=c_enc1[:, :]).then_inc(s["e1_set"], 1)
                act.wait_ge(s["h0_ps"], j + 1)
                act.activation(hT[:, j * H:(j + 1) * H], psG[:, 2 * b + 1, 0:H], ACT.Identity, bias=c_enc2[:, :]).then_inc(s["h0_set"], 1)
            act.wait_ge(s["norm_ps"], 1)
            act.activation(norm2[:, :], psM[:, 0:2], ACT.Sqrt).then_inc(s["norm_set"], 1)
            act.wait_ge(s["deg_set"], 1)
            act.dma_start(rdeg_d, deg[0:TILES, :]).then_inc(s["deg_out"], 16)
            for t in range(STRIPS):
                act.wait_ge(s["m0_ps"], t + 1)
                act.activation(parts[:, 0, t * W:(t + 1) * W], rows_ps, ACT.Copy).then_inc(s["m0_hi"], 1)

            def sums_out(v, by):
                hold(act, s["sums"], v + 1)
                act.activation(aggS[:, 0:H], psA[:, 0, 0:H], ACT.Copy if isinstance(by, float) else ACT.Identity,
                               scale=by).then_inc(s["sums_a"], 1)

            def gates(v):
                for b in range(2):
                    hb = slice(b * H, (b + 1) * H)
                    hold(act, s["gates"], v * 2 + (b + 1))
                    act.activation(r_g[:, hb], psG[:, 0, 0:H], ACT.Sigmoid, bias=c_gate[:, 0:1]).then_inc(s["rz"], 1)
                    act.activation(z_g[:, hb], psG[:, 1, 0:H], ACT.Sigmoid, bias=c_gate[:, 1:2]).then_inc(s["rz"], 1)
                    hold(act, s["n_in"], v * 2 + (b + 1))
                    act.activation(n_g[:, hb], t_g[:, hb], ACT.Tanh, bias=c_ih[:, 2:3]).then_inc(s["n_set"], 1)

            def high(v, ready, target, source, by):
                hold(act, ready, v)
                act.activation(target, source, ACT.Copy, scale=by).then_inc(s["hi_set"], 1)

            def gru(v, layer, strip):
                sums_out(v, undo[:, bass.ds(layer, 1)])
                gates(v)
                t = parts[:, 0, 6 * W:7 * W] if isinstance(strip, int) else later[:, 0, bass.ds(strip * W, W)]
                high(v + 1, s["rows_m"], t, rows_ps, 1.0)

            act.wait_ge(s["deg_out"], 16)
            with act.Fori(0, 4) as layer:
                with act.Fori(0, STRIPS - 1) as strip:
                    gru(layer * STRIPS + strip, layer, strip)
                gru(layer * STRIPS + 6, layer, 6)

            def deviation(n):
                hold(act, s["var_set"], n + 1)
                act.activation(dev[:, :], mv[:, :, 1], ACT.Sqrt, bias=eps[:, :]).then_inc(s["dev_set"], 1)

            def decoder(w, last):
                v = w + 4 * STRIPS
                sums_out(v, undo[:, 4:5])
                gates(v)
                hold(act, s["dec1_ps"], w + 1)
                act.activation(d1.rearrange("p (a b) -> p a b", a=2), psG[:, 0:2, 0:H], ACT.Relu, bias=c_dec1[:, :]).then_inc(s["d1_set"], 1)
                hold(act, s["o_set"], w + 1)
                act.activation(t_g, o_s, ACT.Sigmoid).then_inc(s["sig_set"], 1)
                deviation(w)
                t = parts[:, 0, 6 * W:7 * W] if last else later[:, 0, bass.ds(w * W, W)]
                high(w + 1, s["x1_set"], t, x1_s, X1_SCALE)
                hold(act, s["x1T_ps_set"], w + 1)
                act.activation(hT[:, bass.ds(w * W, W)], x1T_ps, ACT.Copy).then_inc(s["x1T_set"], 1)

            with act.Fori(0, STRIPS - 1) as w:
                decoder(w, False)
            decoder(STRIPS - 1, True)

            def mean1(w, last):
                v = w + 5 * STRIPS
                sums_out(v, 2.0 / X1_SCALE)
                hold(act, s["hid1_ps"], w + 1)
                for hb, t in enumerate((h1a, h1b)):
                    act.activation(t.rearrange("p (a b) -> p a b", a=2), psG[:, 2 * hb:2 * hb + 2, 0:H], ACT.Relu,
                                   bias=c_b1[:, hb:hb + 1]).then_inc(s["h1_set"], 1)
                t = parts[:, 0, 6 * W:7 * W] if last else later[:, 0, bass.ds(w * W, W)]
                high(w + 1, s["y_ps"], t, rows_ps, 1.0)

            with act.Fori(0, STRIPS - 1) as w:
                mean1(w, False)
            mean1(STRIPS - 1, True)

            with act.Fori(0, STRIPS) as w:
                sums_out(w + 6 * STRIPS, undo[:, 5:6])
                deviation(w + STRIPS)

        @block.vector
        def _(dve):
            tag[id(dve)] = "dve"
            my = Steps(dve, s["steps_dve"], hold)
            for t, value in ((srcN, NONE), (dstN, NONE), (padB, 0), (padA, KEY | (NONE << 13) | NONE)):
                dve.memset(t, value).then_inc(s["pads_set"], 1)
            dve.memset(hT[:, NODES:NPAD], 0.0).then_inc(s["pads_set"], 1)
            dve.memset(ones[:, :], 1.0).then_inc(s["consts"], 1)
            dve.memset(eps[:, :], 1e-5).then_inc(s["consts"], 1)
            dve.memset(eflag[:, :], 0.0).then_inc(s["consts"], 1)

            dve.wait_ge(s["edges_in"], 64)
            my.did(dve.scalar_tensor_tensor(keyN, dstN, 13, srcN, ALU.logical_shift_left, ALU.bitwise_or))
            my.after()
            my.did(dve.tensor_scalar(keyN, keyN, KEY, None, ALU.bitwise_or))
            my.did(dve.tensor_scalar(c_i, dstN, 7, None, ALU.logical_shift_right))
            my.did(dve.tensor_scalar(d_i, dstN, P - 1, None, ALU.bitwise_and))
            my.did(dve.tensor_scalar(a_i, srcN, P - 1, None, ALU.bitwise_and))
            my.did(dve.tensor_scalar(b_i, srcN, 7, None, ALU.logical_shift_right))
            my.after()
            dve.nop().then_inc(s["fields_set"], 1)
            dve.wait_ge(s["fields_f"], 1)
            my.did(dve.scalar_tensor_tensor(e_a, b_i, float(TPS), e_b, ALU.mult, ALU.add))
            my.after()
            my.did(dve.tensor_scalar(b_i, e_b, 37.0, None, ALU.mult))
            my.did(dve.scalar_tensor_tensor(e_a, a_i, float(TILES * TPS), e_a, ALU.mult, ALU.add))
            my.after()
            my.did(dve.tensor_scalar(b_i, b_i, 8, None, ALU.logical_shift_right))
            my.after()
            my.did(dve.scalar_tensor_tensor(e_a, b_i, float(P * TILES * TPS - TPS), e_a, ALU.mult, ALU.add))
            my.did(dve.tensor_reduce(rows_min[0:ER, :], dstN, X, ALU.min))
            dve.wait_ge(s["row_set"], 2)
            my.did(dve.tensor_copy(row_f[:, :], row_no[:, :]))
            my.did(dve.tensor_copy(ends_f[:, :], ends[:, :]))
            my.after()
            dve.wait_ge(s["consts"], 3)
            my.did(dve.tensor_scalar(eflag[0:ER, 3:3 + STRIPS], ends_f[0:ER, :], rows_min[0:ER, 0:1], row_f[0:ER, 0:1], ALU.is_gt, ALU.mult))
            dve.wait_ge(s["fields_f"], 2)
            dve.wait_ge(s["halo_in"], 16)
            my.after()
            my.did(dve.tensor_scalar(dstH, keysB, 13, None, ALU.logical_shift_right))
            my.after()
            n = 2 * EC
            my.did(dve.tensor_tensor(same[:, 1:n], dstH[:, 1:n], dstH[:, 0:n - 1], ALU.is_lt))
            my.after()
            my.did(dve.tensor_reduce(eflag[0:ER, 1:2], same[:, 1:n], X, ALU.max))
            my.after()
            my.did(dve.tensor_tensor(same[:, 1:n], dstH[:, 1:n], dstH[:, 0:n - 1], ALU.is_equal))
            my.after()
            my.did(dve.scalar_tensor_tensor(same[:, 1:n], dstH[:, 1:n], float((KEY >> 13) + NONE), same[:, 1:n], ALU.is_lt, ALU.mult))
            my.after()
            my.did(dve.tensor_tensor_scan(run[:, 1:n], same[:, 1:n], same[:, 1:n], 0.0, ALU.mult, ALU.add))
            my.after()
            my.did(dve.tensor_reduce(eflag[0:ER, 0:1], run[:, EC:n], X, ALU.max))
            my.after()
            dve.nop().then_inc(s["flags"], 1)
            dve.wait_ge(s["flags_all"], 1)
            my.did(dve.tensor_scalar(lag_f[:, 0:1], eflag_a[:, 0:1], float(EC - 1), None, ALU.is_ge))
            my.after()
            my.did(dve.tensor_tensor(lag_f[:, 0:1], lag_f[:, 0:1], eflag_a[:, 1:2], ALU.max))
            my.after()
            my.did(dve.tensor_scalar(lag_f[:, 1:2], lag_f[:, 0:1], float(EC), eflag_a[:, 0:1], ALU.mult, ALU.max))
            my.after()
            my.did(dve.tensor_scalar(lag_i[:, 0:1], lag_f[:, 1:2], 1.0, 2.0, ALU.add, ALU.max))
            my.did(dve.tensor_scalar(lag_n[:, 1:2], lag_f[:, 0:1], float(FAR), None, ALU.mult))
            my.after()
            my.did(dve.tensor_scalar(lag_n[:, 0:1], lag_i[:, 0:1], 1, None, ALU.logical_shift_right))
            my.after()
            dve.nop().then_inc(s["lags_known"], 1)
            rounds = dve.value_load(lag_n[0:1, 0:1], min_val=1, max_val=EC // 2)
            far = dve.value_load(lag_n[0:1, 1:2], min_val=0, max_val=FAR)
            dve.nop().then_inc(s["eq_used"], 2)
            keyF, beforeF, afterF = keyN.bitcast(fp32), keysB.bitcast(fp32), keysA.bitcast(fp32)

            def distances(q):
                with dve.Fori(0, rounds) as i:
                    for b in range(2):
                        hold(dve, s["eq_used"], (rounds * q + i) * 2 + (b + 1))
                        dve.tensor_tensor(eqB[b], keyF, beforeF[:, bass.ds(EC - 1 - b - i * 2, EC)], ALU.is_equal).then_inc(s["eq_set"], 1)
                        dve.tensor_tensor(eqA[b], keyF, afterF[:, bass.ds(1 + b + i * 2, EC)], ALU.is_equal).then_inc(s["eq_set"], 1)

            dve.wait_ge(s["more_keys"], 16)
            distances(0)
            with dve.If(far > 0):
                with dve.Fori(0, far) as q:
                    hold(dve, s["eq_set"], (rounds * q + rounds) * 4)
                    dve.nop().then_inc(s["keys_used"], 1)
                    hold(dve, s["halo_in"], q * 16 + 32)
                    hold(dve, s["more_keys"], q * 16 + 32)
                    distances(q + 1)
            dve.wait_ge(s["after_set"], 1)
            before = psA[0:ER, :, :].rearrange("p a b -> p (a b)")
            my.did(dve.tensor_tensor(e_s, before, e_s, ALU.add))
            my.after()
            my.did(dve.scalar_tensor_tensor(e_s, before, 0.0, e_s, ALU.is_equal, ALU.mult))
            my.after()
            my.did(dve.scalar_tensor_tensor(e_s, dstN, float(NONE), e_s, ALU.is_lt, ALU.mult))
            my.after()
            dve.nop().then_inc(s["counted"], 1)
            my.did(dve.tensor_reduce(eflag[0:ER, 2:3], e_s, X, ALU.max))
            my.after()
            dve.nop().then_inc(s["flags"], 1)
            for a, t in ((1, hiT), (3, cntT)):
                dve.wait_ge(s["cols_ps"], a)
                bank = psG[:, 0:2, :].rearrange("q a (b p) -> q p (a b)", p=P)[:, 0:ER, :]
                my.did(dve.tensor_copy(t.rearrange("q (p b) -> q p b", b=EB), bank))
                my.after()
                dve.nop().then_inc(s["cols_dve"], 1)
            dve.wait_ge(s["cols_act"], 1)
            my.did(dve.scalar_tensor_tensor(idxT, hiT, 7, loT, ALU.logical_shift_left, ALU.bitwise_or))
            my.did(dve.tensor_scalar(bitT, cntT, 0.0, None, ALU.is_equal))
            my.after()
            my.did(dve.scalar_tensor_tensor(idxT, bitT, SKIP, idxT, ALU.logical_shift_left, ALU.bitwise_or))
            my.after()
            my.did(dve.tensor_scalar(bitT, cntT, 7, None, ALU.bitwise_and))
            my.after()
            my.did(dve.tensor_scalar(valT, bitT, 0.5, None, ALU.mult, saturate=False))
            my.after()
            dve.nop().then_inc(s["piece_vals"], 1)
            dve.wait_ge(s["flags_all"], 2)
            my.did(dve.tensor_scalar(strip_i[:, :], eflag_a[:, 3:3 + STRIPS], 1.0, 2.0, ALU.add, ALU.max))
            my.after()
            my.did(dve.tensor_scalar(strip_i[:, :], strip_i[:, :], 1, None, ALU.logical_shift_right))
            my.after()
            my.did(dve.tensor_scalar(strip_n[:, :], strip_i[:, :], 16 * EB, None, ALU.mult))
            my.after()
            dve.nop().then_inc(s["strips_known"], 1)
            my.did(dve.tensor_scalar(piece_f[:, :], eflag_a[:, 2:3], 8.0, None, ALU.is_ge))
            my.after()
            for k in range(2, PIECES):
                my.did(dve.scalar_tensor_tensor(piece_f[:, :], eflag_a[:, 2:3], float(8 ** k), piece_f[:, :], ALU.is_ge, ALU.add))
                my.after()
            my.did(dve.tensor_copy(piece_n[:, :], piece_f[:, :]))
            my.did(dve.memset(piece_v[:, :], 0.5))
            my.after()
            dve.nop().then_inc(s["pieces_known"], 1)

            dve.wait_ge(s["weights_in"], 16 * LOADS)
            my.did(dve.tensor_tensor(w_1sq[:, :], w_1[:, :], w_1[:, :], ALU.mult))
            my.after()
            dve.nop().then_inc(s["sq_set"], 1)
            my.did(dve.tensor_tensor(c_gate[:, :], c_ih[:, :], c_hh[:, :], ALU.add))
            for k in range(LAYERS):
                my.did(dve.tensor_reduce(mx[:, k:k + 1], w_conv[:, k, :], X, ALU.max, apply_absolute_value=True))
            my.did(dve.tensor_reduce(mx[:, 7:8], w_2[:, :, :].rearrange("p a b -> p (a b)"), X, ALU.max, apply_absolute_value=True))
            my.did(dve.scalar_tensor_tensor(c_b1a[:, :], c_b1[:, :], -1.0, c_b1[:, :], ALU.mult, ALU.max))
            my.after()

            dve.wait_ge(s["iota_set"], 1)
            dve.wait_ge(s["cols_act"], 2)

            def hot(b, col):
                lo, hi = loT[:, bass.ds(col, EB)], rowT[:, bass.ds(col, EB)]
                dve.tensor_tensor(oh_lo[b], lo.unsqueeze(2).broadcast_to((P, EB, P)), iota[:, :].unsqueeze(1).broadcast_to((P, EB, P)),
                                  ALU.is_equal).then_inc(s["hot_set"], 1)
                dve.tensor_tensor(oh_hi[b], hi.unsqueeze(2).broadcast_to((P, EB, 64)), iota[:, 0:64].unsqueeze(1).broadcast_to((P, EB, 64)),
                                  ALU.is_equal).then_inc(s["hot_set"], 1)

            for b in range(2):
                hot(b, b * EB)
            with dve.Fori(1, ER // 2) as i:
                for b in range(2):
                    hold(dve, s["hot_used"], i * 2 + (b - 1))
                    hot(b, i * (2 * EB) + b * EB)
            dve.wait_ge(s["deg_ps"], 1)
            my.did(dve.tensor_scalar(deg, psA[0:64, 0, 0:P], 1.0, None, ALU.max))
            my.after()
            my.did(dve.reciprocal(deg, deg))
            my.after()
            dve.nop().then_inc(s["deg_set"], 1)

            dve.wait_ge(s["norm_set"], 1)
            my.after()
            my.did(dve.scalar_tensor_tensor(norm2[:, :], norm2[:, :], NORM, c_b1a[:, :], ALU.mult, ALU.add))
            my.after()
            my.did(dve.tensor_reduce(mx[:, 6:7], norm2[:, :], X, ALU.max))
            dve.wait_ge(s["h0_set"], 2 * STRIPS)
            my.did(dve.tensor_reduce(mx[:, 5:6], hT[:, :], X, ALU.max, apply_absolute_value=True))
            my.after()
            dve.nop().then_inc(s["max_set"], 1)
            dve.wait_ge(s["max_all"], 1)
            my.did(dve.tensor_scalar(mxa[:, 5:6], mxa[:, 5:6], 1.0, None, ALU.max))
            my.after()
            my.did(dve.tensor_scalar(prod[:, 0:LAYERS], mxa[:, 0:LAYERS], mxa[:, 5:6], None, ALU.mult))
            my.did(dve.scalar_tensor_tensor(prod[:, 5:6], mxa[:, 6:7], 2.0, mxa[:, 7:8], ALU.mult, ALU.mult))
            my.after()
            my.did(dve.tensor_scalar(expo[:, :], prod[:, :].bitcast(i32), 23, None, ALU.logical_shift_right))
            my.after()
            my.did(dve.tensor_scalar(expo[:, :], expo[:, :], 8.0, 253.0, ALU.max, ALU.min))
            my.after()
            my.did(dve.tensor_scalar(scale_i[:, :], expo[:, :], -1.0, 261.0, ALU.mult, ALU.add))
            my.did(dve.tensor_scalar(undo_i[:, :], expo[:, :], -6.0, None, ALU.add))
            my.after()
            my.did(dve.tensor_scalar(scale_b[:, :], scale_i[:, :], 23, None, ALU.logical_shift_left))
            my.did(dve.tensor_scalar(undo_b[:, :], undo_i[:, :], 23, None, ALU.logical_shift_left))
            my.after()
            for k in range(LAYERS):
                my.did(dve.tensor_scalar(w_convs[:, k, :], w_conv[:, k, :], scale[:, k:k + 1], None, ALU.mult))
            my.did(dve.tensor_scalar(w_2s[:, :, :], w_2[:, :, :], scale[:, 5:6], None, ALU.mult))
            my.did(dve.tensor_scalar(undo_y[:, :], undo[:, 5:6], 0.5, None, ALU.mult))
            my.after()
            dve.nop().then_inc(s["scales_set"], 1)
            for t in range(STRIPS):
                dve.wait_ge(s["m0_hi"], t + 1)
                dve.tensor_tensor(parts[:, 1, t * W:(t + 1) * W], rows_ps, parts[:, 0, t * W:(t + 1) * W], ALU.subtract).then_inc(s["m0_lo"], 1)
            dve.wait_ge(s["m0_lo"], STRIPS)
            dve.nop().then_inc(s["src_ready"], 3)

            more = dve.value_load(piece_n[0:1, 0:1], min_val=0, max_val=PIECES - 1)
            with dve.If(more > 0):
                dve.tensor_copy(rowT, cntT).then_inc(s["steps_piece"], 1)
                with dve.Fori(0, more) as k:
                    hold(dve, s["built"], k + 1)
                    st = Steps(dve, s["steps_piece"], hold, k * PIECE_STEPS + 1)
                    st.after()
                    st.did(dve.tensor_scalar(hiT, hiT, float(REG // P), None, ALU.add))
                    st.did(dve.tensor_scalar(piece_v[:, :], piece_v[:, :], 8.0, None, ALU.mult))
                    st.did(dve.tensor_scalar(bitT, cntT, 0.0, None, ALU.is_equal))
                    st.did(dve.tensor_scalar(rowT, rowT, 3, None, ALU.logical_shift_right))
                    st.after()
                    st.did(dve.scalar_tensor_tensor(idxT, hiT, 7, loT, ALU.logical_shift_left, ALU.bitwise_or))
                    st.after()
                    st.did(dve.scalar_tensor_tensor(idxT, bitT, SKIP, idxT, ALU.logical_shift_left, ALU.bitwise_or))
                    st.after()
                    st.did(dve.tensor_scalar(bitT, rowT, 7, None, ALU.bitwise_and))
                    st.after()
                    st.did(dve.tensor_scalar(valT, bitT, piece_v[:, 0:1], None, ALU.mult, saturate=False))
                    st.after()
                    assert st.n == PIECE_STEPS
                    dve.nop().then_inc(s["piece_vals"], 1)

            def sums_out(v, by):
                hold(dve, s["sums"], v + 1)
                dve.tensor_scalar(aggS[:, H:W], psA[:, 1, 0:H], by, None, ALU.mult).then_inc(s["sums_b"], 1)

            def promote(v):
                hold(dve, s["hi_set"], v)
                hold(dve, s["lo_set"], v)
                for k in range(2):
                    dve.tensor_copy(parts[:, k, 0:6 * W], later[:, k, :]).then_inc(s["src_ready"], 1)

            def low(v, target, source, by, hi):
                hold(dve, s["hi_set"], v + 1)
                if by is None:
                    dve.tensor_tensor(target, source, hi, ALU.subtract).then_inc(s["lo_set"], 1)
                else:
                    dve.scalar_tensor_tensor(target, source, by, hi, ALU.mult, ALU.subtract).then_inc(s["lo_set"], 1)
                hold(dve, s["lo_set"], v + 1)
                dve.nop().then_inc(s["src_ready"], 1)

            def gates(v, strip, st, relu):
                for b in range(2):
                    hb = slice(b * H, (b + 1) * H)
                    hold(dve, s["rz"], v * 4 + (2 * b + 1))
                    st.did(dve.scalar_tensor_tensor(t_g[:, hb], psG[:, 3, 0:H], c_hh[:, 2:3], r_g[:, hb], ALU.add, ALU.mult))
                    st.after()
                    dve.tensor_tensor(t_g[:, hb], psG[:, 2, 0:H], t_g[:, hb], ALU.add).then_inc(s["n_in"], 1)
                    hold(dve, s["n_set"], v * 2 + (b + 1))
                    st.did(dve.tensor_tensor(r_g[:, hb], hT[:, bass.ds(strip * W + b * H, H)], n_g[:, hb], ALU.subtract))
                    st.after()
                    st.did(dve.tensor_tensor(r_g[:, hb], z_g[:, hb], r_g[:, hb], ALU.mult))
                    st.after()
                    if relu:
                        st.did(dve.tensor_tensor(r_g[:, hb], n_g[:, hb], r_g[:, hb], ALU.add))
                        st.after()
                        dve.tensor_scalar(h_new[:, hb], r_g[:, hb], 0.0, None, ALU.max).then_inc(s["h_set"], 1)
                    else:
                        if b == 0:
                            hold(dve, s["h_kept"], v + 1)
                        dve.tensor_tensor(h_new[:, hb], n_g[:, hb], r_g[:, hb], ALU.add).then_inc(s["h_set"], 1)

            def gru(v, layer, strip):
                st = Steps(dve, s["steps_gru"], hold, v * GRU_STEPS)
                last = isinstance(strip, int)
                sums_out(v, undo[:, bass.ds(layer, 1)])
                if last:
                    promote(v)
                else:
                    dve.nop().then_inc(s["src_ready"], 2)
                gates(v, strip, st, False)
                pick = (lambda k: parts[:, k, 6 * W:7 * W]) if last else (lambda k: later[:, k, bass.ds(strip * W, W)])
                low(v, pick(1), rows_ps, None, pick(0))
                assert st.n == GRU_STEPS

            with dve.Fori(0, 4) as layer:
                with dve.Fori(0, STRIPS - 1) as strip:
                    gru(layer * STRIPS + strip, layer, strip)
                gru(layer * STRIPS + 6, layer, 6)
            dve.wait_ge(s["h_kept"], 4 * STRIPS + 1)

            def rows3(t):
                return t.rearrange("p (t f) -> p t f", f=F)

            def rows_of(t):
                return t.unsqueeze(1).broadcast_to((P, TPS, F))

            def normalise(st, value, target, n, free, when):
                for t in range(TPS):
                    st.did(dve.bn_stats(stats[:, t, :], rows3(value)[:, t, :]))
                st.after()
                for t in range(TPS):
                    st.did(dve.bn_aggr(mv[:, t, :], stats[:, t, :]))
                st.after()
                dve.nop().then_inc(s["var_set"], 1)
                hold(dve, s["dev_set"], n + 1)
                st.did(dve.reciprocal(rstd[:, :], dev[:, :]))
                st.after()
                if when is not None:
                    hold(dve, free, when)
                for t in range(TPS):
                    st.did(dve.tensor_scalar(rows3(target)[:, t, :], rows3(value)[:, t, :], mv[:, t, 0:1], rstd[:, t:t + 1],
                                             ALU.subtract, ALU.mult))
                st.after()

            def decoder(w, first, last):
                v = w + 4 * STRIPS
                st = Steps(dve, s["steps_dec"], hold, w * DEC_STEPS)
                sums_out(v, undo[:, 4:5])
                if last:
                    promote(v)
                else:
                    dve.nop().then_inc(s["src_ready"], 2)
                gates(v, w, st, True)
                hold(dve, s["dec2_ps"], w + 1)
                dve.tensor_tensor(rows3(o_s), rows3(rows_ps), rows_of(r_dec2[:, :]), ALU.add).then_inc(s["o_set"], 1)
                hold(dve, s["sig_set"], w + 1)
                hold(dve, s["x_rows"], 16 * 8 if last else w * 16 + 16)
                st.did(dve.tensor_tensor(o_s, t_g, x_s, ALU.add))
                st.after()
                dve.nop().then_inc(s["v_set"], 1)
                normalise(st, o_s, x1_s, w, s["x1_kept"], None if first else w * 16)
                dve.nop().then_inc(s["x1_set"], 1)
                pick = (lambda k: parts[:, k, 6 * W:7 * W]) if last else (lambda k: later[:, k, bass.ds(w * W, W)])
                low(v, pick(1), x1_s, X1_SCALE, pick(0))
                assert st.n == DEC_STEPS, st.n

            decoder(0, True, False)
            with dve.Fori(1, STRIPS - 1) as w:
                decoder(w, False, False)
            decoder(STRIPS - 1, False, True)

            def mean1(w, first, last):
                v = w + 5 * STRIPS
                st = Steps(dve, s["steps_s1"], hold, w * MEAN1_STEPS)
                sums_out(v, 2.0 / X1_SCALE)
                if last:
                    promote(v)
                else:
                    dve.nop().then_inc(s["src_ready"], 2)
                hold(dve, s["sums_a"], v + 1)
                hold(dve, s["sums_b"], v + 1)
                hold(dve, s["rdeg_in"], w * 16 + 16)
                st.did(dve.tensor_tensor(u_s, aggS, rdeg_s, ALU.mult))
                st.after()
                dve.tensor_tensor(u_s, u_s, hT[:, bass.ds(w * W, W)], ALU.add).then_inc(s["u_set"], 1)
                pick = (lambda k: parts[:, k, 6 * W:7 * W]) if last else (lambda k: later[:, k, bass.ds(w * W, W)])
                low(v, pick(1), rows_ps, None, pick(0))
                if not first:
                    hold(dve, s["y_kept"], w * 16)
                st.did(dve.tensor_scalar(y_s, rows_ps, undo_y[:, 0:1], None, ALU.mult))
                st.after()
                dve.nop().then_inc(s["y_set"], 1)

            mean1(0, True, False)
            with dve.Fori(1, STRIPS - 1) as w:
                mean1(w, False, False)
            mean1(STRIPS - 1, False, True)

            def mean2(w, first):
                v = w + 6 * STRIPS
                st = Steps(dve, s["steps_s2"], hold, w * MEAN2_STEPS)
                sums_out(v, undo[:, 5:6])
                dve.nop().then_inc(s["src_ready"], 3)
                hold(dve, s["sums_a"], v + 1)
                hold(dve, s["sums_b"], v + 1)
                hold(dve, s["last_in"], w * 48 + 48)
                dve.tensor_tensor(u_s, aggS, rdeg_s, ALU.mult).then_inc(s["mean_set"], 1)
                hold(dve, s["mean_ps"], w + 1)
                st.did(dve.tensor_tensor(o_w, rows_ps, y_s, ALU.add))
                st.after()
                dve.nop().then_inc(s["w_set"], 1)
                st.did(dve.tensor_tensor(rows3(o_w), rows3(o_w), rows_of(r_b2[:, :]), ALU.add))
                st.after()
                st.did(dve.scalar_tensor_tensor(o_w, o_w, 0.0, x_s, ALU.max, ALU.add))
                st.after()
                dve.nop().then_inc(s["v_set"], 1)
                normalise(st, o_w, x1_s, w + STRIPS, s["stored"], None if first else w * 16)
                dve.nop().then_inc(s["out_set"], 1)
                assert st.n == MEAN2_STEPS

            o_w = d1
            mean2(0, True)
            with dve.Fori(1, STRIPS) as w:
                mean2(w, False)

        @block.tensor
        def _(pe):
            tag[id(pe)] = "pe"
            pe.wait_ge(s["ident_b_set"], 1)
            pe.wait_ge(s["zeros_set"], 1)

            def add(rowsB, rowsA, start, stop):
                for t, ps in ((rowsB, psA[0:ER, :, :].rearrange("p a b -> p (a b)")), (rowsA, psM[0:ER, :])):
                    for h in range(2):
                        last = pe.matmul(ps[:, h * 512:(h + 1) * 512], ident_b[0:ER, 0:ER], t[:, h * 512:(h + 1) * 512],
                                         start=start, stop=stop, skip_group_check=True)
                return last

            nothing = zeros.bitcast(bf16)[0:ER, 0:EC]
            add(nothing, nothing, True, False)
            pe.wait_ge(s["lags_known"], 1)
            rounds = pe.value_load(lag_n[0:1, 0:1], min_val=1, max_val=EC // 2)
            far = pe.value_load(lag_n[0:1, 1:2], min_val=0, max_val=FAR)

            def distances(q):
                with pe.Fori(0, rounds) as i:
                    for b in range(2):
                        hold(pe, s["eq_set"], (rounds * q + i) * 4 + (2 * b + 2))
                        add(eqB[b], eqA[b], False, False).then_inc(s["eq_used"], 1)

            distances(0)
            with pe.If(far > 0):
                with pe.Fori(0, far) as q:
                    distances(q + 1)
            add(nothing, nothing, False, True).then_inc(s["counts_ps"], 1)
            pe.wait_ge(s["ident_set"], 2)
            pe.wait_ge(s["counted"], 1)
            pe.wait_ge(s["fields_f"], 2)
            for a, t in enumerate((e_a, e_t, e_s, e_b)):
                if a >= 2:
                    pe.wait_ge(s["cols_dve"] if a == 2 else s["cols_act"], 1)
                for b in range(EB):
                    last = pe.matmul(psG[:, 2 * (a % 2) + b // 4, (b % 4) * P:(b % 4) * P + ER], t[:, b * P:(b + 1) * P],
                                     ident[0:ER, 0:ER], start=True, stop=True)
                last.then_inc(s["cols_ps"], 1)
            pe.wait_ge(s["cols_dve"], 2)
            pe.wait_ge(s["cols_act"], 2)
            pe.wait_ge(s["x_in"], 16)
            pe.wait_ge(s["weights_in"], 16 * LOADS)
            for j in range(2 * STRIPS):
                b = j % 2
                if j >= 2:
                    pe.wait_ge(s["e1_set"], j - 1)
                pe.matmul(psG[:, 2 * b, 0:H], w_enc1[:, :], hT[:, j * H:(j + 1) * H], start=True, stop=True).then_inc(s["hid_ps"], 1)
                if j >= 2:
                    pe.wait_ge(s["h0_set"], j - 1)
                pe.wait_ge(s["e1_set"], j + 1)
                pe.matmul(psG[:, 2 * b + 1, 0:H], w_enc2[:, :], e1[:, b * H:(b + 1) * H], start=True, stop=True).then_inc(s["h0_ps"], 1)
            pe.wait_ge(s["sq_set"], 1)
            pe.wait_ge(s["consts"], 3)
            for k in range(2):
                last = pe.matmul(psM[:, k:k + 1], w_1sq[:, k * P:(k + 1) * P], ones[:, :], start=True, stop=True)
            last.then_inc(s["norm_ps"], 1)
            def degrees(b, first, last):
                for j in range(EB):
                    mm = pe.matmul(psA[0:64, 0, 0:P], oh_hi[b][:, j, :], oh_lo[b][:, j, :], start=first and j == 0, stop=last and j == EB - 1)
                return mm

            pe.wait_ge(s["hot_set"], 2)
            degrees(0, True, False).then_inc(s["hot_used"], 1)
            with pe.Fori(0, ER // 2 - 1) as i:
                hold(pe, s["hot_set"], i * 4 + 4)
                degrees(1, False, False).then_inc(s["hot_used"], 1)
                hold(pe, s["hot_set"], i * 4 + 6)
                degrees(0, False, False).then_inc(s["hot_used"], 1)
            pe.wait_ge(s["hot_set"], 2 * ER)
            degrees(1, False, True).then_inc(s["deg_ps"], 1)

            pe.wait_ge(s["norm_set"], 1)
            pe.wait_ge(s["scales_set"], 1)
            for t in range(STRIPS):
                if t:
                    pe.wait_ge(s["m0_lo"], t)
                for k in range(TPS):
                    last = pe.matmul(psM[:, k * P:(k + 1) * P], hT[:, (t * TPS + k) * P:(t * TPS + k + 1) * P], w_convs[:, 0, :],
                                     start=True, stop=True)
                last.then_inc(s["m0_ps"], 1)

            pe.wait_ge(s["pieces_known"], 1)
            more = pe.value_load(piece_n[0:1, 0:1], min_val=0, max_val=PIECES - 1)
            pe.nop().then_inc(s["x_free"], 1)
            pe.wait_ge(s["deg_set"], 1)

            def tile(slot, t, k, start, stop):
                for part in range(2):
                    lhsT = parts[:, part, t * P:(t + 1) * P]
                    for b in range(2):
                        last = pe.matmul(psA[:, b, 0:H], lhsT, slot[:, k * W + b * H:k * W + (b + 1) * H],
                                         start=start and part == 0, stop=stop and part == 1, skip_group_check=True)
                return last

            def chunk(u, c):
                slot = ring[:, c, :].bitcast(f8)
                if c == 0:
                    if not (isinstance(u, int) and u == 0):
                        hold(pe, s["sums_a"], u)
                        hold(pe, s["sums_b"], u)
                    hold(pe, s["src_ready"], u * 3 + 2)
                if c == STRIPS - 1:
                    hold(pe, s["src_ready"], u * 3 + 3)
                hold(pe, a_ready[c], u * 16 + 16)
                for k in range(TPS):
                    if c == STRIPS - 1 and k == TPS - 1:
                        with pe.If(more > 0):
                            with pe.Fori(0, more) as piece:
                                for cc in range(STRIPS):
                                    n = more * u * STRIPS + piece * STRIPS + cc
                                    hold(pe, s["x_ready"], n * 16 + 16)
                                    for kk in range(TPS):
                                        last = tile(spare[:, :].bitcast(f8), cc * TPS + kk, kk, False, False)
                                    last.then_inc(s["x_free"], 1)
                    last = tile(slot, c * TPS + k, k, c == 0 and k == 0, c == STRIPS - 1 and k == TPS - 1)
                if c < STRIPS - 1:
                    last.then_inc(a_free[c], 1)
                else:
                    last.then_inc(s["sums"], 1)

            def chunks(u, a, b):
                for c in range(a, b):
                    chunk(u, c)

            def gates(v, strip, b):
                h = hT[:, bass.ds(strip * W + b * H, H)]
                if not (isinstance(v, int) and v == 0 and b == 0):
                    hold(pe, s["rz"], v * 4 + 2 * b)
                    hold(pe, s["n_in"], v * 2 + b)
                for g, bank in ((0, 0), (1, 1), (2, 3)):
                    pe.matmul(psG[:, bank, 0:H], w_hh[:, g * P:(g + 1) * P], h, start=True, stop=g == 2)
                hold(pe, s["sums_a"] if b == 0 else s["sums_b"], v + 1)
                for g in range(3):
                    last = pe.matmul(psG[:, g, 0:H], w_ih[:, g * P:(g + 1) * P], aggS[:, b * H:(b + 1) * H], start=g == 2, stop=True)
                last.then_inc(s["gates"], 1)

            def gru(v, layer, strip, first):
                gates(v, strip, 0)
                chunks(v + 1, 0, 1)
                gates(v, strip, 1)
                chunks(v + 1, 1, 4)
                hold(pe, s["h_set"], v * 2 + 2)
                if not first:
                    hold(pe, s["lo_set"], v)
                for k in range(TPS):
                    last = pe.matmul(psM[:, k * P:(k + 1) * P], h_new[:, k * P:(k + 1) * P], w_convs[:, bass.ds(layer + 1, 1), :].rearrange("p a b -> p (a b)"),
                                     start=True, stop=True)
                last.then_inc(s["rows_m"], 1)
                chunks(v + 1, 4, 7)

            chunks(0, 0, 7)
            gru(0, 0, 0, True)
            with pe.Fori(1, STRIPS) as strip:
                gru(strip, 0, strip, False)
            with pe.Fori(1, 4) as layer:
                with pe.Fori(0, STRIPS) as strip:
                    hold(pe, s["h_kept"], (layer - 1) * STRIPS + strip + 2)
                    gru(layer * STRIPS + strip, layer, strip, False)

            def decoder(w, first):
                v = w + 4 * STRIPS
                hold(pe, s["h_kept"], w + (3 * STRIPS + 2))
                if not first:
                    hold(pe, s["x1T_set"], w)
                gates(v, w, 0)
                chunks(v + 1, 0, 1)
                gates(v, w, 1)
                chunks(v + 1, 1, 3)
                hold(pe, s["h_set"], v * 2 + 2)
                hold(pe, s["rz"], v * 4 + 4)
                for b in range(2):
                    last = pe.matmul(psG[:, b, 0:H], w_dec1[:, :], h_new[:, b * H:(b + 1) * H], start=True, stop=True)
                last.then_inc(s["dec1_ps"], 1)
                chunks(v + 1, 3, 4)
                hold(pe, s["d1_set"], w + 1)
                if first:
                    pe.wait_ge(s["lo_set"], 4 * STRIPS)
                else:
                    hold(pe, s["o_set"], w)
                for k in range(TPS):
                    last = pe.matmul(psM[:, k * P:(k + 1) * P], d1[:, k * P:(k + 1) * P], w_dec2[:, :], start=True, stop=True)
                last.then_inc(s["dec2_ps"], 1)
                chunks(v + 1, 4, 6)
                hold(pe, s["x1_set"], w + 1)
                hold(pe, s["n_in"], v * 2 + 2)
                for k in range(TPS):
                    last = pe.matmul(x1T_ps[:, k * P:(k + 1) * P], x1_s[:, k * P:(k + 1) * P], ident[:, :], start=True, stop=True)
                last.then_inc(s["x1T_ps_set"], 1)
                chunks(v + 1, 6, 7)

            decoder(0, True)
            with pe.Fori(1, STRIPS) as w:
                decoder(w, False)
            pe.wait_ge(s["x1T_set"], STRIPS)
            pe.wait_ge(s["d1_set"], STRIPS)
            pe.wait_ge(s["o_set"], STRIPS)

            def mean1(w, first):
                v = w + 5 * STRIPS
                chunks(v + 1, 0, 1)
                hold(pe, s["u_set"], w + 1)
                if not first:
                    hold(pe, s["h1_set"], w * 2)
                for hb in range(2):
                    for b in range(2):
                        last = pe.matmul(psG[:, 2 * hb + b, 0:H], w_1[:, hb * P:(hb + 1) * P], u_s[:, b * H:(b + 1) * H], start=True, stop=True)
                last.then_inc(s["hid1_ps"], 1)
                chunks(v + 1, 1, 3)
                hold(pe, s["h1_set"], w * 2 + 2)
                if not first:
                    hold(pe, s["y_set"], w)
                for k in range(TPS):
                    for hb, t in enumerate((h1a, h1b)):
                        last = pe.matmul(psM[:, k * P:(k + 1) * P], t[:, k * P:(k + 1) * P], w_2s[:, hb, :], start=hb == 0, stop=hb == 1)
                last.then_inc(s["y_ps"], 1)
                chunks(v + 1, 3, 7)

            mean1(0, True)
            with pe.Fori(1, STRIPS) as w:
                mean1(w, False)
            pe.wait_ge(s["y_set"], STRIPS)

            def mean2(w, first):
                hold(pe, s["mean_set"], w + 1)
                if not first:
                    hold(pe, s["w_set"], w)
                for k in range(TPS):
                    last = pe.matmul(psM[:, k * P:(k + 1) * P], u_s[:, k * P:(k + 1) * P], ident[:, :], start=True, stop=True)
                last.then_inc(s["mean_ps"], 1)

            v0 = 6 * STRIPS
            chunks(v0 + 1, 0, 2)
            mean2(0, True)
            chunks(v0 + 1, 2, 7)
            with pe.Fori(1, STRIPS - 1) as w:
                chunks(w + (v0 + 1), 0, 2)
                mean2(w, False)
                chunks(w + (v0 + 1), 2, 7)
            mean2(STRIPS - 1, False)


_INS = ["x", "xT", "src", "dst", "enc_w1T", "enc_b1", "enc_w2T", "enc_b2", "conv_w", "wihT", "whhT", "bih", "bhh",
        "dec_w1T", "dec_b1", "dec_w2T", "dec_b2", "W1", "b1", "W2", "b2"]


def kernel(x, src, dst, L0_gnn_enc_w1, L0_gnn_enc_b1, L0_gnn_enc_w2, L0_gnn_enc_b2, L0_gnn_conv_w, L0_gnn_gru_wih,
           L0_gnn_gru_whh, L0_gnn_gru_bih, L0_gnn_gru_bhh, L0_gnn_dec_w1, L0_gnn_dec_b1, L0_gnn_dec_w2, L0_gnn_dec_b2,
           L1_gnn_W1, L1_gnn_b1, L1_gnn_W2, L1_gnn_b2):
    import numpy as np
    import concourse.bacc as bacc
    from concourse.bass_utils import run_bass_kernel_spmd as run

    nc = bacc.Bacc("TRN2", target_bir_lowering=False, num_devices=1)

    def t(a):
        return np.ascontiguousarray(np.asarray(a).T)

    given = [x, t(x), src, dst, t(L0_gnn_enc_w1), L0_gnn_enc_b1, t(L0_gnn_enc_w2), L0_gnn_enc_b2, L0_gnn_conv_w,
             t(L0_gnn_gru_wih), t(L0_gnn_gru_whh), L0_gnn_gru_bih, L0_gnn_gru_bhh, t(L0_gnn_dec_w1), L0_gnn_dec_b1,
             t(L0_gnn_dec_w2), L0_gnn_dec_b2, L1_gnn_W1, L1_gnn_b1, L1_gnn_W2, L1_gnn_b2]
    arrays, args = {}, []
    for name, a in zip(_INS, given):
        a = np.ascontiguousarray(a)
        arrays[f"in_{name}"] = a
        args.append(nc.dram_tensor(f"in_{name}", a.shape, mybir.dt.from_np(a.dtype), kind="ExternalInput").ap())
    out = nc.dram_tensor("rows_out", (NODES, F), mybir.dt.float32, kind="ExternalOutput").ap()
    gnn_kernel(nc, *args, out)
    r = run(nc, [arrays], core_ids=[0])
    return r.results[0]["rows_out"]
```

```python
import concourse.bass as bass
from concourse import mybir
from contextlib import ExitStack

NODES, F, EDGES, LAYERS, HID = 6250, 128, 100000, 5, 256
P = 128
STRIPS = 7
TILES = 49
TPS = TILES // STRIPS
W = TPS * P
H = W // 2
NPAD = TILES * P
CH = TPS * W
REG = STRIPS * P * TILES * W
PIECES = 6
TAIL = NODES - (TILES - 1) * P
EC = 1024
ER = -(-EDGES // EC)
EP = ER * EC
EB = EC // P
GR = 7
NONE = 8191
KEY = 0x20000000
FAR = ER - 1
SKIP = 30
X1_SCALE = 2048.0
NORM = 22.65
LOADS = 22
GRU_STEPS, DEC_STEPS, MEAN1_STEPS, MEAN2_STEPS, PIECE_STEPS = 8, 33, 2, 25, 8


class Steps:

    def __init__(self, engine, sem, hold, base=0):
        self.engine, self.sem, self.hold, self.base, self.n = engine, sem, hold, base, 0

    def did(self, instruction):
        instruction.then_inc(self.sem, 1)
        self.n += 1

    def after(self):
        self.hold(self.engine, self.sem, self.base + self.n)


def gnn_kernel(nc, x, xT, src, dst, enc_w1T, enc_b1, enc_w2T, enc_b2, conv_w, wihT, whhT, bih, bhh,
               dec_w1T, dec_b1, dec_w2T, dec_b2, W1, b1, W2, b2, out):
    dt = mybir.dt
    fp32, f32r, i32, f16, f8, u8, bf16 = dt.float32, dt.float32r, dt.int32, dt.float16, dt.float8e5, dt.uint8, dt.bfloat16
    ALU = mybir.AluOpType
    ACT = mybir.ActivationFunctionType
    X = mybir.AxisListType.X
    COLS = ER * EB
    RMAX = bass.bass_isa.ReduceOp.max

    A = nc.dram_tensor("edge_counts", (PIECES * REG, 1), u8, kind="Internal").ap()
    A_p = A.rearrange("(k s p x) o -> k s p (x o)", k=PIECES, s=STRIPS, p=P)
    A_z = A.rearrange("(k c p x) o -> k c p (x o)", k=PIECES, p=P, x=CH)
    ZC = REG // (P * CH)
    keys = nc.dram_tensor("edge_keys", (3 * EP,), i32, kind="Internal").ap()
    rdeg_d = nc.dram_tensor("inverse_degree", (TILES, P), fp32, kind="Internal").ap()
    x1_d = nc.dram_tensor("x1_rows", (STRIPS, P, W), fp32, kind="Internal").ap()
    y_d = nc.dram_tensor("y_rows", (STRIPS, P, W), fp32, kind="Internal").ap()
    x_t = x[0:(TILES - 1) * P, :].rearrange("(t p) f -> p t f", p=P)
    out_t = out[0:(TILES - 1) * P, :].rearrange("(t p) f -> p t f", p=P)

    ctx = ExitStack()
    with ctx:
        def sb(name, shape, d=fp32):
            return ctx.enter_context(nc.sbuf_tensor(name, shape, d))

        def sem(name):
            return ctx.enter_context(nc.semaphore(name))

        hT = sb("hT", [P, NPAD])
        parts = sb("parts", [P, 2, NPAD], f16)
        later = sb("later", [P, 2, 6 * W], f16)
        ring = sb("ring", [P, STRIPS, CH // 4])
        spare = sb("spare", [P, CH // 4])
        work = sb("work", [P, 8, W])
        gate_in = sb("gate_in", [P, 4, W], f32r)
        w_enc1, w_enc2 = sb("w_enc1", [P, P]), sb("w_enc2", [P, P])
        w_dec1, w_dec2 = sb("w_dec1", [P, P]), sb("w_dec2", [P, P])
        w_conv, w_convs = sb("w_conv", [P, LAYERS, P]), sb("w_convs", [P, LAYERS, P])
        w_ih2, w_hh2 = sb("w_ih2", [P, 2, 3 * P], f32r), sb("w_hh2", [P, 2, 3 * P], f32r)
        w_1 = sb("w_1", [P, HID])
        w_2, w_2s = sb("w_2", [P, 2, P]), sb("w_2s", [P, 2, P])
        w_1sq = sb("w_1sq", [P, HID])
        ident = sb("ident", [P, P])
        ones = sb("ones", [P, 1])
        eps = sb("eps", [P, 1])
        c_enc1, c_enc2, c_dec1 = sb("c_enc1", [P, 1]), sb("c_enc2", [P, 1]), sb("c_dec1", [P, 1])
        c_ih, c_hh, c_gate = sb("c_ih", [P, 3]), sb("c_hh", [P, 3]), sb("c_gate", [P, 3])
        c_b1, c_b1a = sb("c_b1", [P, 2]), sb("c_b1a", [P, 2])
        r_dec2, r_b2 = sb("r_dec2", [P, P]), sb("r_b2", [P, P])
        stats, mv = sb("stats", [P, TPS, 6]), sb("mv", [P, TPS, 2])
        dev, rstd = sb("dev", [P, TPS]), sb("rstd", [P, TPS])
        mx, mxa = sb("mx", [P, 8]), sb("mxa", [P, 8])
        prod, expo, scale_i, undo_i = sb("prod", [P, 6]), sb("expo", [P, 6], i32), sb("scale_i", [P, 6], i32), sb("undo_i", [P, 6], i32)
        scale_b, undo_b = sb("scale_b", [P, 6], i32), sb("undo_b", [P, 6], i32)
        scale, undo = scale_b[:, :].bitcast(fp32), undo_b[:, :].bitcast(fp32)
        undo_y = sb("undo_y", [P, 1])
        norm2 = sb("norm2", [P, 2])
        eflag, eflag_a = sb("eflag", [P, 12]), sb("eflag_a", [P, 12])
        lag_f, lag_i = sb("lag_f", [P, 2]), sb("lag_i", [P, 2], i32)
        lag_n = sb("lag_n", [P, 2], i32)
        rows_min, row_no, ends = sb("rows_min", [P, 1]), sb("row_no", [P, 1], i32), sb("ends", [P, STRIPS], i32)
        row_f, ends_f = sb("row_f", [P, 1]), sb("ends_f", [P, STRIPS])
        strip_i, strip_n = sb("strip_i", [P, STRIPS], i32), sb("strip_n", [P, STRIPS], i32)
        ident_b = sb("ident_b", [P, P], bf16)
        piece_f, piece_n = sb("piece_f", [P, 1]), sb("piece_n", [P, 1], i32)
        piece_v = sb("piece_v", [P, 1])
        idx_s, val_s = sb("idx_s", [P, 2, GR * EB], i32), sb("val_s", [P, 2, GR * EB], u8)
        iota = sb("iota", [P, P], i32)
        idxT, valT = sb("idxT", [P, COLS], i32)[:, :], sb("valT", [P, COLS], f8)[:, :]
        aggS, r_g, z_g, t_g, n_g, h_new = (work[:, i, :] for i in range(6))
        d1, o_s, x_s, x1_s = (work[:, i, :] for i in (0, 4, 6, 7))
        agg_hi, agg_lo, h_hi, h_lo = (gate_in[:, i, :] for i in range(4))
        rdeg_s, u_s, h1a, h1b, y_s = (work[:, i, :] for i in (1, 2, 3, 4, 5))
        e1 = ring[:, :, :].rearrange("p a b -> p (a b)")[:, 9 * EC:9 * EC + W]
        ebuf = ring[:, :, :].rearrange("p a b -> p (a b)").bitcast(i32)

        def erow(i):
            return ebuf[0:ER, i * EC:(i + 1) * EC]

        srcN, dstN, keyN = erow(0), erow(1), erow(2)
        keysB, keysA = ebuf[0:ER, 3 * EC:5 * EC], ebuf[0:ER, 5 * EC:7 * EC]
        eqb = ebuf[0:ER, 7 * EC:9 * EC].bitcast(bf16)
        eqB, eqA = [eqb[:, b * EC:(b + 1) * EC] for b in range(2)], [eqb[:, (2 + b) * EC:(3 + b) * EC] for b in range(2)]
        padB, padA = erow(7), erow(8)
        pbuf = parts[:, :, :].rearrange("p a b -> p (a b)").bitcast(i32)
        dstH = pbuf[0:ER, 0:2 * EC]
        same = pbuf[0:ER, 2 * EC:4 * EC].bitcast(fp32)
        wbuf = work[:, :, :].rearrange("p a b -> p (a b)")
        run = wbuf[0:ER, 0:2 * EC]
        a_i, b_i, c_i, d_i = (pbuf[0:ER, i * EC:(i + 1) * EC] for i in (4, 5, 0, 1))
        e_t, e_s, e_a, e_b = (wbuf[0:ER, (3 + i) * EC:(4 + i) * EC] for i in range(4))
        lbuf = later[:, :, :].rearrange("p a b -> p (a b)").bitcast(i32)

        def ecol(i):
            return lbuf[:, i * COLS:(i + 1) * COLS]

        hiT, loT, rowT, cntT, bitT = (ecol(i) for i in range(5))
        w_ih, w_hh = (lbuf[:, 5 * COLS + i * 3 * P:5 * COLS + (i + 1) * 3 * P].bitcast(fp32) for i in range(2))
        oh_lo = [wbuf[:, i * 512:(i + 1) * 512].bitcast(bf16).rearrange("p (b c) -> p b c", c=P) for i in range(2)]
        oh_hi = [wbuf[:, (4 + i) * 256:(5 + i) * 256].bitcast(bf16).rearrange("p (b c) -> p b c", c=64) for i in range(2)]
        deg = wbuf[0:64, 1536:1536 + P]
        zeros = spare[:, :].bitcast(u8)

        psA = ctx.enter_context(nc.psum_tensor("psA", [P, 2, 512], fp32))
        psG = ctx.enter_context(nc.psum_tensor("psG", [P, 4, 512], fp32))
        psM = ctx.enter_context(nc.psum_tensor("psM", [P, 1024], fp32))
        rows_ps = psM[:, 0:W]
        x1T_ps = psG[:, 2:4, :].rearrange("p a b -> p (a b)")[:, 0:W]

        seen = {e: sem(f"passed_{e}") for e in ("pe", "act", "dve", "pool", "sp")}
        names = """edges_in weights_in x_in consts zeros_set ident_set iota_set pads_set keys_out halo_in flags
            flags_all lags_known eq_used eq_set counts_ps after_set fields_set fields_f counted cols_ps cols_dve
            cols_act pieces_known strips_known row_set more_keys keys_used ident_b_set max_set max_all hid_ps
            e1_set h0_ps h0_set sq_set norm_ps norm_set scales_set m0_ps m0_hi m0_lo built piece_vals staged
            zero_filled zero_more hot_set hot_used deg_ps deg_set deg_out src_ready sums0 sums sums_a sums_b
            h_hi_set h_lo_set parts_hi parts_lo gates rz n_in n_set h_set h_kept rows_m hi_set lo_set dec1_ps
            d1_set dec2_ps o_set sig_set x_rows v_set var_set dev_set x1_set x1_kept x1T_ps_set x1T_set rdeg_in
            u_set hid1_ps h1_set y_ps y_set y_kept last_in mean_set mean_ps w_set out_set stored x_free
            steps_dve steps_gru steps_dec steps_s1 steps_s2 x_ready tail_set tail_zero steps_piece""".split()
        s = {n: sem(n) for n in names}
        a_ready = [sem(f"a_ready{c}") for c in range(STRIPS)]
        a_free = [sem(f"a_free{c}") for c in range(STRIPS - 1)]
        scattered = [sem(f"scattered{b}") for b in range(2)]
        tag = {}

        def hold(engine, semaphore, value):
            engine.wait_ge(semaphore, value)
            if not isinstance(value, int):
                engine.nop().then_inc(seen[tag[id(engine)]], 1)

        block = ctx.enter_context(nc.Block())

        @block.sync
        def _(sp):
            tag[id(sp)] = "sp"
            full = EDGES // EC
            rest = EDGES - full * EC
            sp.wait_ge(s["pads_set"], 2)
            for d, t in ((src, srcN), (dst, dstN)):
                sp.dma_start(t[0:full, :], d[0:full * EC].rearrange("(p c) -> p c", c=EC)).then_inc(s["edges_in"], 16)
                sp.dma_start(t[full:ER, 0:rest], d[full * EC:EDGES].rearrange("(p c) -> p c", c=rest)).then_inc(s["edges_in"], 16)
            sp.wait_ge(s["zeros_set"], 1)
            for c in range(3):
                sp.dma_start(A_z[0, c, :, :], zeros).then_inc(s["zero_filled"], 16)
            sp.wait_ge(s["pads_set"], 4)
            sp.dma_start(keys[0:EP].rearrange("(p c) -> p c", c=EC), padB).then_inc(s["keys_out"], 16)
            sp.dma_start(keys[2 * EP:3 * EP].rearrange("(p c) -> p c", c=EC), padA).then_inc(s["keys_out"], 16)
            sp.wait_ge(s["steps_dve"], 2)
            sp.dma_start(keys[EP:2 * EP].rearrange("(p c) -> p c", c=EC), keyN).then_inc(s["keys_out"], 16)
            sp.wait_ge(s["keys_out"], 48)

            def two_rows(start):
                return bass.AP(keys.tensor, start, [[EC, ER], [1, 2 * EC]])

            sp.dma_start(keysB, two_rows(EP - EC)).then_inc(s["halo_in"], 16)
            sp.dma_start(keysA, two_rows(EP)).then_inc(s["more_keys"], 16)
            for c in range(3, ZC):
                sp.dma_start(A_z[0, c, :, :], zeros).then_inc(s["zero_filled"], 16)
            sp.wait_ge(s["tail_zero"], 1)
            sp.dma_start(hT[:, 0:NODES], xT).then_inc(s["x_in"], 16)
            sp.wait_ge(s["lags_known"], 1)
            far = sp.value_load(lag_n[0:1, 1:2], min_val=0, max_val=FAR)
            with sp.If(far > 0):
                with sp.Fori(0, far) as q:
                    hold(sp, s["keys_used"], q + 1)
                    sp.dma_start(keysB, two_rows((EP - 2 * EC) - q * EC)).then_inc(s["halo_in"], 16)
                    sp.dma_start(keysA, two_rows((EP + EC) + q * EC)).then_inc(s["more_keys"], 16)
            sp.wait_ge(s["pieces_known"], 1)
            more = sp.value_load(piece_n[0:1, 0:1], min_val=0, max_val=PIECES - 1)
            with sp.If(more > 0):
                with sp.Fori(0, more) as k:
                    for c in range(ZC):
                        sp.dma_start(A_z[bass.ds(k + 1, 1), c, :, :].rearrange("k p x -> (k p) x"), zeros).then_inc(s["zero_more"], 16)
                hold(sp, s["built"], more + 1)

            def loads(unit, strip):
                for c in range(STRIPS):
                    if not isinstance(unit, int):
                        hold(sp, a_free[c] if c < STRIPS - 1 else s["sums"], unit)
                    a = A_p[0, bass.ds(strip, 1), :, c * CH:(c + 1) * CH].rearrange("s p x -> (s p) x")
                    sp.dma_start(ring[:, c, :].bitcast(u8), a).then_inc(a_ready[c], 16)
                with sp.If(more > 0):
                    with sp.Fori(0, more) as k:
                        for c in range(STRIPS):
                            n = more * unit * STRIPS + k * STRIPS + c
                            hold(sp, s["x_free"], n + 1)
                            a = A_p[bass.ds(k + 1, 1), bass.ds(strip, 1), :, c * CH:(c + 1) * CH].rearrange("k s p x -> (k s p) x")
                            sp.dma_start(spare[:, :].bitcast(u8), a).then_inc(s["x_ready"], 16)

            sp.wait_ge(s["strips_known"], 1)

            def strip_built(strip):
                at = sp.value_load(strip_n[0:1, bass.ds(strip, 1)], min_val=P, max_val=P * ER // 2)
                for b in range(2):
                    hold(sp, scattered[b], at)

            sp.wait_ge(s["h0_set"], 2 * STRIPS)
            strip_built(0)
            loads(0, 0)
            with sp.Fori(1, STRIPS) as strip:
                strip_built(strip)
                loads(strip, strip)
            hold(sp, s["built"], more + 1)
            with sp.Fori(1, 7) as layer:
                with sp.Fori(0, STRIPS) as strip:
                    loads(layer * STRIPS + strip, strip)

        @block.gpsimd
        def _(pool):
            tag[id(pool)] = "pool"
            pool.memset(zeros, 0).then_inc(s["zeros_set"], 1)
            pool.memset(ident[:, :], 0.0).then_inc(s["ident_set"], 1)
            pool.wait_ge(s["ident_set"], 1)
            pool.affine_select(out=ident[:, :], in_=ident[:, :], compare_op=ALU.not_equal, fill=1.0, base=0,
                               pattern=[[-1, P]], channel_multiplier=1).then_inc(s["ident_set"], 1)
            pool.iota(iota[:, :], pattern=[[1, P]], base=0, channel_multiplier=0).then_inc(s["iota_set"], 1)
            pool.iota(row_no[:, :], pattern=[[0, 1]], base=1, channel_multiplier=1).then_inc(s["row_set"], 1)
            pool.iota(ends[:, :], pattern=[[W, STRIPS]], base=W, channel_multiplier=0).then_inc(s["row_set"], 1)
            pool.wait_ge(s["flags"], 1)
            pool.partition_all_reduce(eflag_a[:, 0:2], eflag[:, 0:2], P, RMAX).then_inc(s["flags_all"], 1)
            pool.wait_ge(s["flags"], 2)
            pool.partition_all_reduce(eflag_a[:, 2:10], eflag[:, 2:10], P, RMAX).then_inc(s["flags_all"], 1)

            def group(b, col, base, i):
                pool.tensor_copy(idx_s[:, b, :], idxT[:, bass.ds(col, GR * EB)]).then_inc(s["staged"], 1)
                pool.tensor_copy(val_s[:, b, :], valT.bitcast(u8)[:, bass.ds(col, GR * EB)]).then_inc(s["staged"], 1)
                at = base * (2 * ER // GR) + (2 * b + 2) + (0 if i is None else i * 4)
                hold(pool, s["staged"], at)
                for r in range(b * GR, (b + 1) * GR):
                    if i is not None or r >= 2:
                        hold(pool, scattered[r % 2], base * (16 * EB * ER // 2) + (r // 2) * (16 * EB) + (0 if i is None else i * (16 * EB * GR)))
                    for j in range(EB):
                        k = (r - b * GR) * EB + j
                        pool.indirect_dma_start(A, bass.IndirectOffsetOnAxis(ap=idx_s[:, b, k:k + 1], axis=0),
                                                val_s[:, b, k:k + 1], None, bounds_check=PIECES * REG - 1,
                                                oob_is_err=False).then_inc(scattered[r % 2], 16)

            def scatter(piece, first=False):
                if not (isinstance(piece, int) and piece == 0):
                    for b in range(2):
                        hold(pool, scattered[b], piece * (16 * EB * ER // 2))
                for b in range(2):
                    group(b, b * GR * EB, piece, None)

                def pairs(a, z):
                    with pool.Fori(a, z) as i:
                        for b in range(2):
                            group(b, i * (2 * GR * EB) + b * GR * EB, piece, i)

                if first:
                    pairs(1, 2)
                    pool.wait_ge(s["max_set"], 1)
                    pool.partition_all_reduce(mxa[:, :], mx[:, :], P, RMAX).then_inc(s["max_all"], 1)
                    pairs(2, ER // (2 * GR))
                else:
                    pairs(1, ER // (2 * GR))
                for b in range(2):
                    hold(pool, scattered[b], (piece + 1) * (16 * EB * ER // 2))
                pool.nop().then_inc(s["built"], 1)

            pool.wait_ge(s["piece_vals"], 1)
            pool.wait_ge(s["zero_filled"], 16 * ZC)
            scatter(0, True)
            more = pool.value_load(piece_n[0:1, 0:1], min_val=0, max_val=PIECES - 1)
            with pool.If(more > 0):
                with pool.Fori(0, more) as k:
                    hold(pool, s["piece_vals"], k + 2)
                    hold(pool, s["zero_more"], (k + 1) * (16 * ZC))
                    scatter(k + 1)

            def rows3(t):
                return t.rearrange("p (t f) -> p t f", f=F)

            def decoder(w, last):
                if not last:
                    pool.dma_start(rows3(x_s), x_t[:, bass.ds(w * TPS, TPS), :]).then_inc(s["x_rows"], 16)
                else:
                    k = TPS - 1
                    pool.memset(rows3(x_s)[:, k, :], 0.0).then_inc(s["tail_set"], 1)
                    pool.wait_ge(s["tail_set"], 1)
                    pool.dma_start(rows3(x_s)[:, 0:k, :], x_t[:, w * TPS:w * TPS + k, :]).then_inc(s["x_rows"], 16)
                    pool.wait_ge(s["x_rows"], 16 * 7)
                    pool.dma_start(rows3(x_s)[0:TAIL, k, :], x[(TILES - 1) * P:NODES, :]).then_inc(s["x_rows"], 16)
                hold(pool, s["x1_set"], w + 1)
                pool.dma_start(x1_d[bass.ds(w, 1), :, :].rearrange("s p x -> (s p) x"), x1_s).then_inc(s["x1_kept"], 16)

            decoder(0, False)
            with pool.Fori(1, STRIPS - 1) as w:
                decoder(w, False)
            decoder(STRIPS - 1, True)

            def rdeg_load(w, done):
                a = rdeg_d[bass.ds(w * TPS, TPS), :].rearrange("t p -> (t p)").partition_broadcast(P)
                pool.dma_start(rdeg_s, a).then_inc(done, 16)

            pool.wait_ge(s["deg_out"], 16)
            pool.wait_ge(s["x1_kept"], 16 * STRIPS)
            rdeg_load(0, s["rdeg_in"])
            with pool.Fori(0, STRIPS - 1) as w:
                hold(pool, s["u_set"], w + 1)
                rdeg_load(w + 1, s["rdeg_in"])
                hold(pool, s["y_set"], w + 1)
                pool.dma_start(y_d[bass.ds(w, 1), :, :].rearrange("s p x -> (s p) x"), y_s).then_inc(s["y_kept"], 16)
            pool.wait_ge(s["y_set"], STRIPS)
            pool.dma_start(y_d[STRIPS - 1, :, :], y_s).then_inc(s["y_kept"], 16)
            pool.wait_ge(s["y_kept"], 16 * STRIPS)

            def last_loads(w):
                rdeg_load(w, s["last_in"])
                pool.dma_start(y_s, y_d[bass.ds(w, 1), :, :].rearrange("s p x -> (s p) x")).then_inc(s["last_in"], 16)
                pool.dma_start(x_s, x1_d[bass.ds(w, 1), :, :].rearrange("s p x -> (s p) x")).then_inc(s["last_in"], 16)

            last_loads(0)
            with pool.Fori(0, STRIPS - 1) as w:
                hold(pool, s["v_set"], w + (STRIPS + 1))
                last_loads(w + 1)
                hold(pool, s["out_set"], w + 1)
                pool.dma_start(out_t[:, bass.ds(w * TPS, TPS), :], rows3(x1_s)).then_inc(s["stored"], 16)
            pool.wait_ge(s["out_set"], STRIPS)
            k = TPS - 1
            pool.dma_start(out_t[:, (STRIPS - 1) * TPS:, :], rows3(x1_s)[:, 0:k, :]).then_inc(s["stored"], 16)
            pool.dma_start(out[(TILES - 1) * P:NODES, :], rows3(x1_s)[0:TAIL, k, :]).then_inc(s["stored"], 16)
            pool.wait_ge(s["stored"], 16 * (STRIPS + 1))

        @block.scalar
        def _(act):
            tag[id(act)] = "act"
            act.wait_ge(s["ident_set"], 2)
            act.activation(ident_b[:, :], ident[:, :], ACT.Copy).then_inc(s["ident_b_set"], 1)
            act.wait_ge(s["fields_set"], 1)
            act.activation(e_b, c_i, ACT.Copy).then_inc(s["fields_f"], 1)
            act.activation(e_t, d_i, ACT.Copy).then_inc(s["fields_f"], 1)
            loads = [(w_enc1[:, :], enc_w1T), (w_enc2[:, :], enc_w2T),
                     (w_conv[:, :, :], conv_w.rearrange("l k f -> k l f")), (w_ih, wihT), (w_hh, whhT),
                     (w_dec1[:, :], dec_w1T),
                     (w_dec2[:, :], dec_w2T), (r_dec2[:, :], dec_b2.partition_broadcast(P)), (w_1[:, :], W1),
                     (w_2[:, :, :], W2.rearrange("(h k) f -> k h f", k=P)), (r_b2[:, :], b2.partition_broadcast(P))]
            for t, a in ((c_enc1, enc_b1), (c_enc2, enc_b2), (c_ih, bih), (c_hh, bhh), (c_dec1, dec_b1), (c_b1, b1)):
                for g in range(a.shape[0] // P):
                    loads.append((t[:, g:g + 1], a[g * P:(g + 1) * P].rearrange("(p o) -> p o", o=1)))
            assert len(loads) == LOADS
            act.wait_ge(s["halo_in"], 16)
            act.wait_ge(s["more_keys"], 16)
            for t, a in loads:
                act.dma_start(t, a).then_inc(s["weights_in"], 16)

            act.wait_ge(s["counts_ps"], 1)
            act.activation(e_s, psM[0:ER, :], ACT.Copy, bias=1.0).then_inc(s["after_set"], 1)

            def columns(t, banks):
                a = psG[:, banks:banks + 2, :].rearrange("q a (b p) -> q p (a b)", p=P)[:, 0:ER, :]
                return t.rearrange("q (p b) -> q p b", b=EB), a

            for a, t in ((2, loT), (4, rowT)):
                act.wait_ge(s["cols_ps"], a)
                o, i = columns(t, 2)
                act.activation(o, i, ACT.Copy).then_inc(s["cols_act"], 1)

            act.wait_ge(s["weights_in"], 16 * LOADS)
            for j in range(2 * STRIPS):
                b = j % 2
                act.wait_ge(s["hid_ps"], j + 1)
                act.activation(e1[:, b * H:(b + 1) * H], psG[:, 2 * b, 0:H], ACT.Relu, bias=c_enc1[:, :]).then_inc(s["e1_set"], 1)
                act.wait_ge(s["h0_ps"], j + 1)
                act.activation(hT[:, j * H:(j + 1) * H], psG[:, 2 * b + 1, 0:H], ACT.Identity, bias=c_enc2[:, :]).then_inc(s["h0_set"], 1)
            for t, a in ((w_ih2, w_ih), (w_hh2, w_hh)):
                act.activation(t[:, 0, :], a, ACT.Copy).then_inc(s["parts_hi"], 1)
            act.wait_ge(s["norm_ps"], 1)
            act.activation(norm2[:, :], psM[:, 0:2], ACT.Sqrt).then_inc(s["norm_set"], 1)
            act.wait_ge(s["deg_set"], 1)
            act.dma_start(rdeg_d, deg[0:TILES, :]).then_inc(s["deg_out"], 16)
            for t in range(STRIPS):
                act.wait_ge(s["m0_ps"], t + 1)
                act.activation(parts[:, 0, t * W:(t + 1) * W], rows_ps, ACT.Copy).then_inc(s["m0_hi"], 1)

            def sums_out(v, by):
                hold(act, s["sums0"], v + 1)
                act.activation(aggS[:, 0:H], psA[:, 0, 0:H], ACT.Copy if isinstance(by, float) else ACT.Identity,
                               scale=by).then_inc(s["sums_a"], 1)

            def h_high(v, strip):
                hold(act, s["h_kept"], v)
                act.activation(h_hi, hT[:, bass.ds(strip * W, W)], ACT.Copy).then_inc(s["h_hi_set"], 1)

            def gates(v):
                for b in range(2):
                    hb = slice(b * H, (b + 1) * H)
                    hold(act, s["gates"], v * 2 + (b + 1))
                    act.activation(r_g[:, hb], psG[:, 0, 0:H], ACT.Sigmoid, bias=c_gate[:, 0:1]).then_inc(s["rz"], 1)
                    act.activation(z_g[:, hb], psG[:, 1, 0:H], ACT.Sigmoid, bias=c_gate[:, 1:2]).then_inc(s["rz"], 1)
                    hold(act, s["n_in"], v * 2 + (b + 1))
                    act.activation(n_g[:, hb], t_g[:, hb], ACT.Tanh, bias=c_ih[:, 2:3]).then_inc(s["n_set"], 1)

            def high(v, ready, target, source, by):
                hold(act, ready, v)
                act.activation(target, source, ACT.Copy, scale=by).then_inc(s["hi_set"], 1)

            def gru(v, layer, strip):
                gates(v)
                h_high(v + 1, 0 if isinstance(strip, int) else strip + 1)
                hold(act, s["h_set"], v * 2 + 2)
                act.activation(hT[:, bass.ds(strip * W, W)], h_new, ACT.Copy).then_inc(s["h_kept"], 1)
                t = parts[:, 0, 6 * W:7 * W] if isinstance(strip, int) else later[:, 0, bass.ds(strip * W, W)]
                high(v + 1, s["rows_m"], t, rows_ps, 1.0)

            act.nop().then_inc(s["h_kept"], 1)
            act.wait_ge(s["deg_out"], 16)
            act.activation(h_hi, hT[:, 0:W], ACT.Copy).then_inc(s["h_hi_set"], 1)
            with act.Fori(0, 4) as layer:
                with act.Fori(0, STRIPS - 1) as strip:
                    gru(layer * STRIPS + strip, layer, strip)
                gru(layer * STRIPS + 6, layer, 6)

            def deviation(n):
                hold(act, s["var_set"], n + 1)
                act.activation(dev[:, :], mv[:, :, 1], ACT.Sqrt, bias=eps[:, :]).then_inc(s["dev_set"], 1)

            def decoder(w, last):
                v = w + 4 * STRIPS
                gates(v)
                if not last:
                    act.activation(h_hi, hT[:, bass.ds((w + 1) * W, W)], ACT.Copy).then_inc(s["h_hi_set"], 1)
                hold(act, s["dec1_ps"], w + 1)
                act.activation(d1.rearrange("p (a b) -> p a b", a=2), psG[:, 0:2, 0:H], ACT.Relu, bias=c_dec1[:, :]).then_inc(s["d1_set"], 1)
                hold(act, s["o_set"], w + 1)
                act.activation(t_g, o_s, ACT.Sigmoid).then_inc(s["sig_set"], 1)
                deviation(w)
                t = parts[:, 0, 6 * W:7 * W] if last else later[:, 0, bass.ds(w * W, W)]
                high(w + 1, s["x1_set"], t, x1_s, X1_SCALE)
                hold(act, s["x1T_ps_set"], w + 1)
                act.activation(hT[:, bass.ds(w * W, W)], x1T_ps, ACT.Copy).then_inc(s["x1T_set"], 1)

            with act.Fori(0, STRIPS - 1) as w:
                decoder(w, False)
            decoder(STRIPS - 1, True)

            def mean1(w, last):
                v = w + 5 * STRIPS
                sums_out(v, 2.0 / X1_SCALE)
                hold(act, s["hid1_ps"], w + 1)
                for hb, t in enumerate((h1a, h1b)):
                    act.activation(t.rearrange("p (a b) -> p a b", a=2), psG[:, 2 * hb:2 * hb + 2, 0:H], ACT.Relu,
                                   bias=c_b1[:, hb:hb + 1]).then_inc(s["h1_set"], 1)
                t = parts[:, 0, 6 * W:7 * W] if last else later[:, 0, bass.ds(w * W, W)]
                high(w + 1, s["y_ps"], t, rows_ps, 1.0)

            with act.Fori(0, STRIPS - 1) as w:
                mean1(w, False)
            mean1(STRIPS - 1, True)

            with act.Fori(0, STRIPS) as w:
                sums_out(w + 6 * STRIPS, undo[:, 5:6])
                deviation(w + STRIPS)

        @block.vector
        def _(dve):
            tag[id(dve)] = "dve"
            my = Steps(dve, s["steps_dve"], hold)
            for t in (srcN, dstN):
                dve.memset(t[96:ER, EDGES % EC:], NONE).then_inc(s["pads_set"], 1)
            for t, value in ((padB, 0), (padA, KEY | (NONE << 13) | NONE)):
                dve.memset(t, value).then_inc(s["pads_set"], 1)
            dve.memset(hT[:, NODES:NPAD], 0.0).then_inc(s["tail_zero"], 1)
            dve.memset(ones[:, :], 1.0).then_inc(s["consts"], 1)
            dve.memset(eps[:, :], 1e-5).then_inc(s["consts"], 1)
            dve.memset(eflag[:, :], 0.0).then_inc(s["consts"], 1)

            dve.wait_ge(s["pads_set"], 2)
            dve.wait_ge(s["edges_in"], 64)
            my.did(dve.scalar_tensor_tensor(keyN, dstN, 13, srcN, ALU.logical_shift_left, ALU.bitwise_or))
            my.after()
            my.did(dve.tensor_scalar(keyN, keyN, KEY, None, ALU.bitwise_or))
            my.did(dve.tensor_scalar(c_i, dstN, 7, None, ALU.logical_shift_right))
            my.did(dve.tensor_scalar(d_i, dstN, P - 1, None, ALU.bitwise_and))
            my.did(dve.tensor_scalar(a_i, srcN, P - 1, None, ALU.bitwise_and))
            my.did(dve.tensor_scalar(b_i, srcN, 7, None, ALU.logical_shift_right))
            my.after()
            dve.nop().then_inc(s["fields_set"], 1)
            dve.wait_ge(s["fields_f"], 1)
            my.did(dve.scalar_tensor_tensor(e_a, b_i, float(TPS), e_b, ALU.mult, ALU.add))
            my.after()
            my.did(dve.tensor_scalar(b_i, e_b, 37.0, None, ALU.mult))
            my.did(dve.scalar_tensor_tensor(e_a, a_i, float(TILES * TPS), e_a, ALU.mult, ALU.add))
            my.after()
            my.did(dve.tensor_scalar(b_i, b_i, 8, None, ALU.logical_shift_right))
            my.after()
            my.did(dve.scalar_tensor_tensor(e_a, b_i, float(P * TILES * TPS - TPS), e_a, ALU.mult, ALU.add))
            my.did(dve.tensor_reduce(rows_min[0:ER, :], dstN, X, ALU.min))
            dve.wait_ge(s["row_set"], 2)
            my.did(dve.tensor_copy(row_f[:, :], row_no[:, :]))
            my.did(dve.tensor_copy(ends_f[:, :], ends[:, :]))
            my.after()
            dve.wait_ge(s["consts"], 3)
            my.did(dve.tensor_scalar(eflag[0:ER, 3:3 + STRIPS], ends_f[0:ER, :], rows_min[0:ER, 0:1], row_f[0:ER, 0:1], ALU.is_gt, ALU.mult))
            dve.wait_ge(s["fields_f"], 2)
            dve.wait_ge(s["halo_in"], 16)
            my.after()
            my.did(dve.tensor_scalar(dstH, keysB, 13, None, ALU.logical_shift_right))
            my.after()
            n = 2 * EC
            my.did(dve.tensor_tensor(same[:, 1:n], dstH[:, 1:n], dstH[:, 0:n - 1], ALU.is_lt))
            my.after()
            my.did(dve.tensor_reduce(eflag[0:ER, 1:2], same[:, 1:n], X, ALU.max))
            my.after()
            my.did(dve.tensor_tensor(same[:, 1:n], dstH[:, 1:n], dstH[:, 0:n - 1], ALU.is_equal))
            my.after()
            my.did(dve.scalar_tensor_tensor(same[:, 1:n], dstH[:, 1:n], float((KEY >> 13) + NONE), same[:, 1:n], ALU.is_lt, ALU.mult))
            my.after()
            my.did(dve.tensor_tensor_scan(run[:, 1:n], same[:, 1:n], same[:, 1:n], 0.0, ALU.mult, ALU.add))
            my.after()
            my.did(dve.tensor_reduce(eflag[0:ER, 0:1], run[:, EC:n], X, ALU.max))
            my.after()
            dve.nop().then_inc(s["flags"], 1)
            dve.wait_ge(s["flags_all"], 1)
            my.did(dve.tensor_scalar(lag_f[:, 0:1], eflag_a[:, 0:1], float(EC - 1), None, ALU.is_ge))
            my.after()
            my.did(dve.tensor_tensor(lag_f[:, 0:1], lag_f[:, 0:1], eflag_a[:, 1:2], ALU.max))
            my.after()
            my.did(dve.tensor_scalar(lag_f[:, 1:2], lag_f[:, 0:1], float(EC), eflag_a[:, 0:1], ALU.mult, ALU.max))
            my.after()
            my.did(dve.tensor_scalar(lag_i[:, 0:1], lag_f[:, 1:2], 1.0, 2.0, ALU.add, ALU.max))
            my.did(dve.tensor_scalar(lag_n[:, 1:2], lag_f[:, 0:1], float(FAR), None, ALU.mult))
            my.after()
            my.did(dve.tensor_scalar(lag_n[:, 0:1], lag_i[:, 0:1], 1, None, ALU.logical_shift_right))
            my.after()
            dve.nop().then_inc(s["lags_known"], 1)
            rounds = dve.value_load(lag_n[0:1, 0:1], min_val=1, max_val=EC // 2)
            far = dve.value_load(lag_n[0:1, 1:2], min_val=0, max_val=FAR)
            dve.nop().then_inc(s["eq_used"], 2)
            keyF, beforeF, afterF = keyN.bitcast(fp32), keysB.bitcast(fp32), keysA.bitcast(fp32)

            def distances(q):
                with dve.Fori(0, rounds) as i:
                    for b in range(2):
                        hold(dve, s["eq_used"], (rounds * q + i) * 2 + (b + 1))
                        dve.tensor_tensor(eqB[b], keyF, beforeF[:, bass.ds(EC - 1 - b - i * 2, EC)], ALU.is_equal).then_inc(s["eq_set"], 1)
                        dve.tensor_tensor(eqA[b], keyF, afterF[:, bass.ds(1 + b + i * 2, EC)], ALU.is_equal).then_inc(s["eq_set"], 1)

            dve.wait_ge(s["more_keys"], 16)
            distances(0)
            with dve.If(far > 0):
                with dve.Fori(0, far) as q:
                    hold(dve, s["eq_set"], (rounds * q + rounds) * 4)
                    dve.nop().then_inc(s["keys_used"], 1)
                    hold(dve, s["halo_in"], q * 16 + 32)
                    hold(dve, s["more_keys"], q * 16 + 32)
                    distances(q + 1)
            dve.wait_ge(s["after_set"], 1)
            before = psA[0:ER, :, :].rearrange("p a b -> p (a b)")
            my.did(dve.tensor_tensor(e_s, before, e_s, ALU.add))
            my.after()
            my.did(dve.scalar_tensor_tensor(e_s, before, 0.0, e_s, ALU.is_equal, ALU.mult))
            my.after()
            my.did(dve.scalar_tensor_tensor(e_s, dstN, float(NONE), e_s, ALU.is_lt, ALU.mult))
            my.after()
            dve.nop().then_inc(s["counted"], 1)
            my.did(dve.tensor_reduce(eflag[0:ER, 2:3], e_s, X, ALU.max))
            my.after()
            dve.nop().then_inc(s["flags"], 1)
            for a, t in ((1, hiT), (3, cntT)):
                dve.wait_ge(s["cols_ps"], a)
                bank = psG[:, 0:2, :].rearrange("q a (b p) -> q p (a b)", p=P)[:, 0:ER, :]
                my.did(dve.tensor_copy(t.rearrange("q (p b) -> q p b", b=EB), bank))
                my.after()
                dve.nop().then_inc(s["cols_dve"], 1)
            dve.wait_ge(s["cols_act"], 1)
            my.did(dve.scalar_tensor_tensor(idxT, hiT, 7, loT, ALU.logical_shift_left, ALU.bitwise_or))
            my.did(dve.tensor_scalar(bitT, cntT, 0.0, None, ALU.is_equal))
            my.after()
            my.did(dve.scalar_tensor_tensor(idxT, bitT, SKIP, idxT, ALU.logical_shift_left, ALU.bitwise_or))
            my.after()
            my.did(dve.tensor_scalar(bitT, cntT, 7, None, ALU.bitwise_and))
            my.after()
            my.did(dve.tensor_scalar(valT, bitT, 0.5, None, ALU.mult, saturate=False))
            my.after()
            dve.nop().then_inc(s["piece_vals"], 1)
            dve.wait_ge(s["flags_all"], 2)
            my.did(dve.tensor_scalar(strip_i[:, :], eflag_a[:, 3:3 + STRIPS], 1.0, 2.0, ALU.add, ALU.max))
            my.after()
            my.did(dve.tensor_scalar(strip_i[:, :], strip_i[:, :], 1, None, ALU.logical_shift_right))
            my.after()
            my.did(dve.tensor_scalar(strip_n[:, :], strip_i[:, :], 16 * EB, None, ALU.mult))
            my.after()
            dve.nop().then_inc(s["strips_known"], 1)
            my.did(dve.tensor_scalar(piece_f[:, :], eflag_a[:, 2:3], 8.0, None, ALU.is_ge))
            my.after()
            for k in range(2, PIECES):
                my.did(dve.scalar_tensor_tensor(piece_f[:, :], eflag_a[:, 2:3], float(8 ** k), piece_f[:, :], ALU.is_ge, ALU.add))
                my.after()
            my.did(dve.tensor_copy(piece_n[:, :], piece_f[:, :]))
            my.did(dve.memset(piece_v[:, :], 0.5))
            my.after()
            dve.nop().then_inc(s["pieces_known"], 1)

            dve.wait_ge(s["weights_in"], 16 * LOADS)
            my.did(dve.tensor_tensor(w_1sq[:, :], w_1[:, :], w_1[:, :], ALU.mult))
            my.after()
            dve.nop().then_inc(s["sq_set"], 1)
            my.did(dve.tensor_tensor(c_gate[:, :], c_ih[:, :], c_hh[:, :], ALU.add))
            for k in range(LAYERS):
                my.did(dve.tensor_reduce(mx[:, k:k + 1], w_conv[:, k, :], X, ALU.max, apply_absolute_value=True))
            my.did(dve.tensor_reduce(mx[:, 7:8], w_2[:, :, :].rearrange("p a b -> p (a b)"), X, ALU.max, apply_absolute_value=True))
            my.did(dve.scalar_tensor_tensor(c_b1a[:, :], c_b1[:, :], -1.0, c_b1[:, :], ALU.mult, ALU.max))
            my.after()

            dve.wait_ge(s["iota_set"], 1)
            dve.wait_ge(s["cols_act"], 2)

            def hot(b, col):
                lo, hi = loT[:, bass.ds(col, EB)], rowT[:, bass.ds(col, EB)]
                dve.tensor_tensor(oh_lo[b], lo.unsqueeze(2).broadcast_to((P, EB, P)), iota[:, :].unsqueeze(1).broadcast_to((P, EB, P)),
                                  ALU.is_equal).then_inc(s["hot_set"], 1)
                dve.tensor_tensor(oh_hi[b], hi.unsqueeze(2).broadcast_to((P, EB, 64)), iota[:, 0:64].unsqueeze(1).broadcast_to((P, EB, 64)),
                                  ALU.is_equal).then_inc(s["hot_set"], 1)

            for b in range(2):
                hot(b, b * EB)
            with dve.Fori(1, ER // 2) as i:
                for b in range(2):
                    hold(dve, s["hot_used"], i * 2 + (b - 1))
                    hot(b, i * (2 * EB) + b * EB)
            dve.wait_ge(s["deg_ps"], 1)
            my.did(dve.tensor_scalar(deg, psA[0:64, 0, 0:P], 1.0, None, ALU.max))
            my.after()
            my.did(dve.reciprocal(deg, deg))
            my.after()
            dve.nop().then_inc(s["deg_set"], 1)

            dve.wait_ge(s["parts_hi"], 2)
            for t, a in ((w_ih2, w_ih), (w_hh2, w_hh)):
                dve.tensor_tensor(t[:, 1, :], a, t[:, 0, :].bitcast(fp32), ALU.subtract).then_inc(s["parts_lo"], 1)
            dve.wait_ge(s["norm_set"], 1)
            my.after()
            my.did(dve.scalar_tensor_tensor(norm2[:, :], norm2[:, :], NORM, c_b1a[:, :], ALU.mult, ALU.add))
            my.after()
            my.did(dve.tensor_reduce(mx[:, 6:7], norm2[:, :], X, ALU.max))
            dve.wait_ge(s["h0_set"], 2 * STRIPS)
            my.did(dve.tensor_reduce(mx[:, 5:6], hT[:, :], X, ALU.max, apply_absolute_value=True))
            my.after()
            dve.nop().then_inc(s["max_set"], 1)
            dve.wait_ge(s["max_all"], 1)
            my.did(dve.tensor_scalar(mxa[:, 5:6], mxa[:, 5:6], 1.0, None, ALU.max))
            my.after()
            my.did(dve.tensor_scalar(prod[:, 0:LAYERS], mxa[:, 0:LAYERS], mxa[:, 5:6], None, ALU.mult))
            my.did(dve.scalar_tensor_tensor(prod[:, 5:6], mxa[:, 6:7], 2.0, mxa[:, 7:8], ALU.mult, ALU.mult))
            my.after()
            my.did(dve.tensor_scalar(expo[:, :], prod[:, :].bitcast(i32), 23, None, ALU.logical_shift_right))
            my.after()
            my.did(dve.tensor_scalar(expo[:, :], expo[:, :], 8.0, 253.0, ALU.max, ALU.min))
            my.after()
            my.did(dve.tensor_scalar(scale_i[:, :], expo[:, :], -1.0, 261.0, ALU.mult, ALU.add))
            my.did(dve.tensor_scalar(undo_i[:, :], expo[:, :], -6.0, None, ALU.add))
            my.after()
            my.did(dve.tensor_scalar(scale_b[:, :], scale_i[:, :], 23, None, ALU.logical_shift_left))
            my.did(dve.tensor_scalar(undo_b[:, :], undo_i[:, :], 23, None, ALU.logical_shift_left))
            my.after()
            for k in range(LAYERS):
                my.did(dve.tensor_scalar(w_convs[:, k, :], w_conv[:, k, :], scale[:, k:k + 1], None, ALU.mult))
            my.did(dve.tensor_scalar(w_2s[:, :, :], w_2[:, :, :], scale[:, 5:6], None, ALU.mult))
            my.did(dve.tensor_scalar(undo_y[:, :], undo[:, 5:6], 0.5, None, ALU.mult))
            my.after()
            dve.nop().then_inc(s["scales_set"], 1)
            for t in range(STRIPS):
                dve.wait_ge(s["m0_hi"], t + 1)
                dve.tensor_tensor(parts[:, 1, t * W:(t + 1) * W], rows_ps, parts[:, 0, t * W:(t + 1) * W], ALU.subtract).then_inc(s["m0_lo"], 1)
            dve.wait_ge(s["m0_lo"], STRIPS)
            dve.nop().then_inc(s["src_ready"], 3)

            more = dve.value_load(piece_n[0:1, 0:1], min_val=0, max_val=PIECES - 1)
            with dve.If(more > 0):
                dve.tensor_copy(rowT, cntT).then_inc(s["steps_piece"], 1)
                with dve.Fori(0, more) as k:
                    hold(dve, s["built"], k + 1)
                    st = Steps(dve, s["steps_piece"], hold, k * PIECE_STEPS + 1)
                    st.after()
                    st.did(dve.tensor_scalar(hiT, hiT, float(REG // P), None, ALU.add))
                    st.did(dve.tensor_scalar(piece_v[:, :], piece_v[:, :], 8.0, None, ALU.mult))
                    st.did(dve.tensor_scalar(bitT, cntT, 0.0, None, ALU.is_equal))
                    st.did(dve.tensor_scalar(rowT, rowT, 3, None, ALU.logical_shift_right))
                    st.after()
                    st.did(dve.scalar_tensor_tensor(idxT, hiT, 7, loT, ALU.logical_shift_left, ALU.bitwise_or))
                    st.after()
                    st.did(dve.scalar_tensor_tensor(idxT, bitT, SKIP, idxT, ALU.logical_shift_left, ALU.bitwise_or))
                    st.after()
                    st.did(dve.tensor_scalar(bitT, rowT, 7, None, ALU.bitwise_and))
                    st.after()
                    st.did(dve.tensor_scalar(valT, bitT, piece_v[:, 0:1], None, ALU.mult, saturate=False))
                    st.after()
                    assert st.n == PIECE_STEPS
                    dve.nop().then_inc(s["piece_vals"], 1)

            def sums_parts(v, by, st):
                for b, (ready, done) in enumerate(((s["sums0"], s["sums_a"]), (s["sums"], s["sums_b"]))):
                    hold(dve, ready, v + 1)
                    hb = slice(b * H, (b + 1) * H)
                    st.did(dve.tensor_scalar(agg_hi[:, hb], psA[:, b, 0:H], by, None, ALU.mult))
                    st.after()
                    dve.scalar_tensor_tensor(agg_lo[:, hb], psA[:, b, 0:H], by, agg_hi[:, hb].bitcast(fp32), ALU.mult, ALU.subtract).then_inc(done, 1)

            def h_low(v, strip):
                hold(dve, s["h_hi_set"], v + 1)
                dve.tensor_tensor(h_lo, hT[:, bass.ds(strip * W, W)], h_hi.bitcast(fp32), ALU.subtract).then_inc(s["h_lo_set"], 1)

            def sums_out(v, by):
                hold(dve, s["sums"], v + 1)
                dve.tensor_scalar(aggS[:, H:W], psA[:, 1, 0:H], by, None, ALU.mult).then_inc(s["sums_b"], 1)

            def promote(v):
                hold(dve, s["hi_set"], v)
                hold(dve, s["lo_set"], v)
                for k in range(2):
                    dve.tensor_copy(parts[:, k, 0:6 * W], later[:, k, :]).then_inc(s["src_ready"], 1)

            def low(v, target, source, by, hi, last):
                hold(dve, s["hi_set"], v + 1)
                if by is None:
                    dve.tensor_tensor(target, source, hi, ALU.subtract).then_inc(s["lo_set"], 1)
                else:
                    dve.scalar_tensor_tensor(target, source, by, hi, ALU.mult, ALU.subtract).then_inc(s["lo_set"], 1)
                if last:
                    hold(dve, s["lo_set"], v + 1)
                    dve.nop().then_inc(s["src_ready"], 1)

            def gates(v, strip, st, relu):
                for b in range(2):
                    hb = slice(b * H, (b + 1) * H)
                    hold(dve, s["rz"], v * 4 + (2 * b + 1))
                    st.did(dve.scalar_tensor_tensor(t_g[:, hb], psG[:, 3, 0:H], c_hh[:, 2:3], r_g[:, hb], ALU.add, ALU.mult))
                    st.after()
                    dve.tensor_tensor(t_g[:, hb], psG[:, 2, 0:H], t_g[:, hb], ALU.add).then_inc(s["n_in"], 1)
                    hold(dve, s["n_set"], v * 2 + (b + 1))
                    st.did(dve.tensor_tensor(r_g[:, hb], hT[:, bass.ds(strip * W + b * H, H)], n_g[:, hb], ALU.subtract))
                    st.after()
                    st.did(dve.tensor_tensor(r_g[:, hb], z_g[:, hb], r_g[:, hb], ALU.mult))
                    st.after()
                    if relu:
                        st.did(dve.tensor_tensor(r_g[:, hb], n_g[:, hb], r_g[:, hb], ALU.add))
                        st.after()
                        dve.tensor_scalar(h_new[:, hb], r_g[:, hb], 0.0, None, ALU.max).then_inc(s["h_set"], 1)
                    else:
                        if b == 0:
                            hold(dve, s["h_kept"], v + 1)
                        dve.tensor_tensor(h_new[:, hb], n_g[:, hb], r_g[:, hb], ALU.add).then_inc(s["h_set"], 1)

            def gru(v, layer, strip):
                st = Steps(dve, s["steps_gru"], hold, v * GRU_STEPS)
                last = isinstance(strip, int)
                if not last:
                    dve.nop().then_inc(s["src_ready"], 3)
                sums_parts(v, undo[:, bass.ds(layer, 1)], st)
                if last:
                    promote(v)
                gates(v, strip, st, False)
                h_low(v + 1, 0 if last else strip + 1)
                pick = (lambda k: parts[:, k, 6 * W:7 * W]) if last else (lambda k: later[:, k, bass.ds(strip * W, W)])
                low(v, pick(1), rows_ps, None, pick(0), last)
                assert st.n == GRU_STEPS

            h_low(0, 0)
            with dve.Fori(0, 4) as layer:
                with dve.Fori(0, STRIPS - 1) as strip:
                    gru(layer * STRIPS + strip, layer, strip)
                gru(layer * STRIPS + 6, layer, 6)
            dve.wait_ge(s["h_kept"], 4 * STRIPS + 1)

            def rows3(t):
                return t.rearrange("p (t f) -> p t f", f=F)

            def rows_of(t):
                return t.unsqueeze(1).broadcast_to((P, TPS, F))

            def normalise(st, value, target, n, free, when):
                for t in range(TPS):
                    st.did(dve.bn_stats(stats[:, t, :], rows3(value)[:, t, :]))
                st.after()
                for t in range(TPS):
                    st.did(dve.bn_aggr(mv[:, t, :], stats[:, t, :]))
                st.after()
                dve.nop().then_inc(s["var_set"], 1)
                hold(dve, s["dev_set"], n + 1)
                st.did(dve.reciprocal(rstd[:, :], dev[:, :]))
                st.after()
                if when is not None:
                    hold(dve, free, when)
                for t in range(TPS):
                    st.did(dve.tensor_scalar(rows3(target)[:, t, :], rows3(value)[:, t, :], mv[:, t, 0:1], rstd[:, t:t + 1],
                                             ALU.subtract, ALU.mult))
                st.after()

            def decoder(w, first, last):
                v = w + 4 * STRIPS
                st = Steps(dve, s["steps_dec"], hold, w * DEC_STEPS)
                if not last:
                    dve.nop().then_inc(s["src_ready"], 3)
                sums_parts(v, undo[:, 4:5], st)
                if last:
                    promote(v)
                gates(v, w, st, True)
                if not last:
                    h_low(v + 1, w + 1)
                hold(dve, s["dec2_ps"], w + 1)
                dve.tensor_tensor(rows3(o_s), rows3(rows_ps), rows_of(r_dec2[:, :]), ALU.add).then_inc(s["o_set"], 1)
                hold(dve, s["sig_set"], w + 1)
                hold(dve, s["x_rows"], 16 * 8 if last else w * 16 + 16)
                st.did(dve.tensor_tensor(o_s, t_g, x_s, ALU.add))
                st.after()
                dve.nop().then_inc(s["v_set"], 1)
                normalise(st, o_s, x1_s, w, s["x1_kept"], None if first else w * 16)
                dve.nop().then_inc(s["x1_set"], 1)
                pick = (lambda k: parts[:, k, 6 * W:7 * W]) if last else (lambda k: later[:, k, bass.ds(w * W, W)])
                low(v, pick(1), x1_s, X1_SCALE, pick(0), last)
                assert st.n == DEC_STEPS, st.n

            decoder(0, True, False)
            with dve.Fori(1, STRIPS - 1) as w:
                decoder(w, False, False)
            decoder(STRIPS - 1, False, True)

            def mean1(w, first, last):
                v = w + 5 * STRIPS
                st = Steps(dve, s["steps_s1"], hold, w * MEAN1_STEPS)
                if not last:
                    dve.nop().then_inc(s["src_ready"], 3)
                sums_out(v, 2.0 / X1_SCALE)
                if last:
                    promote(v)
                hold(dve, s["sums_a"], v + 1)
                hold(dve, s["sums_b"], v + 1)
                hold(dve, s["rdeg_in"], w * 16 + 16)
                st.did(dve.tensor_tensor(u_s, aggS, rdeg_s, ALU.mult))
                st.after()
                dve.tensor_tensor(u_s, u_s, hT[:, bass.ds(w * W, W)], ALU.add).then_inc(s["u_set"], 1)
                pick = (lambda k: parts[:, k, 6 * W:7 * W]) if last else (lambda k: later[:, k, bass.ds(w * W, W)])
                low(v, pick(1), rows_ps, None, pick(0), last)
                if not first:
                    hold(dve, s["y_kept"], w * 16)
                st.did(dve.tensor_scalar(y_s, rows_ps, undo_y[:, 0:1], None, ALU.mult))
                st.after()
                dve.nop().then_inc(s["y_set"], 1)

            mean1(0, True, False)
            with dve.Fori(1, STRIPS - 1) as w:
                mean1(w, False, False)
            mean1(STRIPS - 1, False, True)

            def mean2(w, first):
                v = w + 6 * STRIPS
                st = Steps(dve, s["steps_s2"], hold, w * MEAN2_STEPS)
                dve.nop().then_inc(s["src_ready"], 3)
                sums_out(v, undo[:, 5:6])
                hold(dve, s["sums_a"], v + 1)
                hold(dve, s["sums_b"], v + 1)
                hold(dve, s["last_in"], w * 48 + 48)
                dve.tensor_tensor(u_s, aggS, rdeg_s, ALU.mult).then_inc(s["mean_set"], 1)
                hold(dve, s["mean_ps"], w + 1)
                st.did(dve.tensor_tensor(o_w, rows_ps, y_s, ALU.add))
                st.after()
                dve.nop().then_inc(s["w_set"], 1)
                st.did(dve.tensor_tensor(rows3(o_w), rows3(o_w), rows_of(r_b2[:, :]), ALU.add))
                st.after()
                st.did(dve.scalar_tensor_tensor(o_w, o_w, 0.0, x_s, ALU.max, ALU.add))
                st.after()
                dve.nop().then_inc(s["v_set"], 1)
                normalise(st, o_w, x1_s, w + STRIPS, s["stored"], None if first else w * 16)
                dve.nop().then_inc(s["out_set"], 1)
                assert st.n == MEAN2_STEPS

            o_w = h1a
            mean2(0, True)
            with dve.Fori(1, STRIPS) as w:
                mean2(w, False)

        @block.tensor
        def _(pe):
            tag[id(pe)] = "pe"
            pe.wait_ge(s["ident_b_set"], 1)
            pe.wait_ge(s["zeros_set"], 1)

            def add(rowsB, rowsA, start, stop):
                for t, ps in ((rowsB, psA[0:ER, :, :].rearrange("p a b -> p (a b)")), (rowsA, psM[0:ER, :])):
                    for h in range(2):
                        last = pe.matmul(ps[:, h * 512:(h + 1) * 512], ident_b[0:ER, 0:ER], t[:, h * 512:(h + 1) * 512],
                                         start=start, stop=stop, skip_group_check=True)
                return last

            nothing = zeros.bitcast(bf16)[0:ER, 0:EC]
            add(nothing, nothing, True, False)
            pe.wait_ge(s["lags_known"], 1)
            rounds = pe.value_load(lag_n[0:1, 0:1], min_val=1, max_val=EC // 2)
            far = pe.value_load(lag_n[0:1, 1:2], min_val=0, max_val=FAR)

            def distances(q):
                with pe.Fori(0, rounds) as i:
                    for b in range(2):
                        hold(pe, s["eq_set"], (rounds * q + i) * 4 + (2 * b + 2))
                        add(eqB[b], eqA[b], False, False).then_inc(s["eq_used"], 1)

            distances(0)
            with pe.If(far > 0):
                with pe.Fori(0, far) as q:
                    distances(q + 1)
            add(nothing, nothing, False, True).then_inc(s["counts_ps"], 1)
            pe.wait_ge(s["ident_set"], 2)
            pe.wait_ge(s["counted"], 1)
            pe.wait_ge(s["fields_f"], 2)
            for a, t in enumerate((e_a, e_t, e_s, e_b)):
                if a >= 2:
                    pe.wait_ge(s["cols_dve"] if a == 2 else s["cols_act"], 1)
                for b in range(EB):
                    last = pe.matmul(psG[:, 2 * (a % 2) + b // 4, (b % 4) * P:(b % 4) * P + ER], t[:, b * P:(b + 1) * P],
                                     ident[0:ER, 0:ER], start=True, stop=True)
                last.then_inc(s["cols_ps"], 1)
            pe.wait_ge(s["cols_dve"], 2)
            pe.wait_ge(s["cols_act"], 2)
            pe.wait_ge(s["x_in"], 16)
            pe.wait_ge(s["weights_in"], 16 * LOADS)
            for j in range(2 * STRIPS):
                b = j % 2
                if j >= 2:
                    pe.wait_ge(s["e1_set"], j - 1)
                pe.matmul(psG[:, 2 * b, 0:H], w_enc1[:, :], hT[:, j * H:(j + 1) * H], start=True, stop=True).then_inc(s["hid_ps"], 1)
                if j >= 2:
                    pe.wait_ge(s["h0_set"], j - 1)
                pe.wait_ge(s["e1_set"], j + 1)
                pe.matmul(psG[:, 2 * b + 1, 0:H], w_enc2[:, :], e1[:, b * H:(b + 1) * H], start=True, stop=True).then_inc(s["h0_ps"], 1)
            pe.wait_ge(s["sq_set"], 1)
            pe.wait_ge(s["consts"], 3)
            for k in range(2):
                last = pe.matmul(psM[:, k:k + 1], w_1sq[:, k * P:(k + 1) * P], ones[:, :], start=True, stop=True)
            last.then_inc(s["norm_ps"], 1)
            def degrees(b, first, last):
                for j in range(EB):
                    mm = pe.matmul(psA[0:64, 0, 0:P], oh_hi[b][:, j, :], oh_lo[b][:, j, :], start=first and j == 0, stop=last and j == EB - 1)
                return mm

            pe.wait_ge(s["hot_set"], 2)
            degrees(0, True, False).then_inc(s["hot_used"], 1)
            with pe.Fori(0, ER // 2 - 1) as i:
                hold(pe, s["hot_set"], i * 4 + 4)
                degrees(1, False, False).then_inc(s["hot_used"], 1)
                hold(pe, s["hot_set"], i * 4 + 6)
                degrees(0, False, False).then_inc(s["hot_used"], 1)
            pe.wait_ge(s["hot_set"], 2 * ER)
            degrees(1, False, True).then_inc(s["deg_ps"], 1)

            pe.wait_ge(s["norm_set"], 1)
            pe.wait_ge(s["scales_set"], 1)
            for t in range(STRIPS):
                if t:
                    pe.wait_ge(s["m0_lo"], t)
                for k in range(TPS):
                    last = pe.matmul(psM[:, k * P:(k + 1) * P], hT[:, (t * TPS + k) * P:(t * TPS + k + 1) * P], w_convs[:, 0, :],
                                     start=True, stop=True)
                last.then_inc(s["m0_ps"], 1)

            pe.wait_ge(s["pieces_known"], 1)
            more = pe.value_load(piece_n[0:1, 0:1], min_val=0, max_val=PIECES - 1)
            pe.nop().then_inc(s["x_free"], 1)
            pe.wait_ge(s["deg_set"], 1)
            pe.wait_ge(s["parts_lo"], 2)

            def product(slot, t, k, part, b, start=False, stop=False):
                return pe.matmul(psA[:, b, 0:H], parts[:, part, t * P:(t + 1) * P], slot[:, k * W + b * H:k * W + (b + 1) * H],
                                 start=start, stop=stop, skip_group_check=True)

            def tiles(slot, c):
                for k in range(TPS):
                    for part in range(2):
                        for b in range(2):
                            last = product(slot, c * TPS + k, k, part, b)
                return last

            def further(u):
                with pe.If(more > 0):
                    with pe.Fori(0, more) as piece:
                        for c in range(STRIPS):
                            hold(pe, s["x_ready"], (more * u * STRIPS + piece * STRIPS + c) * 16 + 16)
                            tiles(spare[:, :].bitcast(f8), c).then_inc(s["x_free"], 1)

            def chunk(u, c):
                slot = ring[:, c, :].bitcast(f8)
                first, last_chunk = c == 0, c == STRIPS - 1
                if first:
                    hold(pe, s["src_ready"], u * 3 + 2)
                if last_chunk:
                    hold(pe, s["src_ready"], u * 3 + 3)
                    further(u)
                hold(pe, a_ready[c], u * 16 + 16)
                if not (first or last_chunk):
                    tiles(slot, c).then_inc(a_free[c], 1)
                    return
                for b, (left, done) in enumerate(((s["sums_a"], s["sums0"]), (s["sums_b"], s["sums"]))):
                    if first and not (isinstance(u, int) and u == 0):
                        hold(pe, left, u)
                    for k in range(TPS):
                        for part in range(2):
                            last = product(slot, c * TPS + k, k, part, b, first and k == part == 0, last_chunk and k == TPS - 1 and part == 1)
                    if last_chunk:
                        last.then_inc(done, 1)
                if first:
                    last.then_inc(a_free[c], 1)

            def chunks(u, a, b):
                for c in range(a, b):
                    chunk(u, c)

            def gates(v, b):
                hb = slice(b * H, (b + 1) * H)

                def gate(bank, g, w2, high, low, start, stop):
                    w_high, w_low = (w2[:, k, g * P:(g + 1) * P] for k in range(2))
                    pe.matmul(psG[:, bank, 0:H], w_high, low[:, hb], start=start, stop=False)
                    pe.matmul(psG[:, bank, 0:H], w_low, high[:, hb], start=False, stop=False)
                    return pe.matmul(psG[:, bank, 0:H], w_high, high[:, hb], start=False, stop=stop)

                if not (isinstance(v, int) and v == 0 and b == 0):
                    hold(pe, s["rz"], v * 4 + 2 * b)
                    hold(pe, s["n_in"], v * 2 + b)
                if b == 0:
                    hold(pe, s["h_lo_set"], v + 1)
                for g, bank in ((0, 0), (1, 1), (2, 3)):
                    gate(bank, g, w_hh2, h_hi, h_lo, True, g == 2)
                hold(pe, s["sums_a"] if b == 0 else s["sums_b"], v + 1)
                for g in range(3):
                    last = gate(g, g, w_ih2, agg_hi, agg_lo, g == 2, True)
                last.then_inc(s["gates"], 1)

            def gru(v, layer, first, ahead=True):
                gates(v, 0)
                if ahead:
                    chunks(v + 1, 0, 1)
                gates(v, 1)
                if ahead:
                    chunks(v + 1, 1, 4)
                hold(pe, s["h_set"], v * 2 + 2)
                if not first:
                    hold(pe, s["lo_set"], v)
                for k in range(TPS):
                    last = pe.matmul(psM[:, k * P:(k + 1) * P], h_new[:, k * P:(k + 1) * P], w_convs[:, bass.ds(layer + 1, 1), :].rearrange("p a b -> p (a b)"),
                                     start=True, stop=True)
                last.then_inc(s["rows_m"], 1)
                chunks(v + 1, 4 if ahead else 0, 7)

            chunks(0, 0, 7)
            gru(0, 0, True, ahead=False)
            with pe.Fori(1, STRIPS - 1) as strip:
                gru(strip, 0, False, ahead=False)
            gru(STRIPS - 1, 0, False)
            with pe.Fori(1, 4) as layer:
                with pe.Fori(0, STRIPS) as strip:
                    hold(pe, s["h_kept"], (layer - 1) * STRIPS + strip + 2)
                    gru(layer * STRIPS + strip, layer, False)

            def decoder(w, first):
                v = w + 4 * STRIPS
                hold(pe, s["h_kept"], w + (3 * STRIPS + 2))
                if not first:
                    hold(pe, s["x1T_set"], w)
                gates(v, 0)
                chunks(v + 1, 0, 1)
                gates(v, 1)
                chunks(v + 1, 1, 3)
                hold(pe, s["h_set"], v * 2 + 2)
                hold(pe, s["rz"], v * 4 + 4)
                for b in range(2):
                    last = pe.matmul(psG[:, b, 0:H], w_dec1[:, :], h_new[:, b * H:(b + 1) * H], start=True, stop=True)
                last.then_inc(s["dec1_ps"], 1)
                chunks(v + 1, 3, 4)
                hold(pe, s["d1_set"], w + 1)
                if first:
                    pe.wait_ge(s["lo_set"], 4 * STRIPS)
                else:
                    hold(pe, s["o_set"], w)
                for k in range(TPS):
                    last = pe.matmul(psM[:, k * P:(k + 1) * P], d1[:, k * P:(k + 1) * P], w_dec2[:, :], start=True, stop=True)
                last.then_inc(s["dec2_ps"], 1)
                chunks(v + 1, 4, 6)
                hold(pe, s["x1_set"], w + 1)
                hold(pe, s["n_in"], v * 2 + 2)
                for k in range(TPS):
                    last = pe.matmul(x1T_ps[:, k * P:(k + 1) * P], x1_s[:, k * P:(k + 1) * P], ident[:, :], start=True, stop=True)
                last.then_inc(s["x1T_ps_set"], 1)
                chunks(v + 1, 6, 7)

            decoder(0, True)
            with pe.Fori(1, STRIPS) as w:
                decoder(w, False)
            pe.wait_ge(s["x1T_set"], STRIPS)
            pe.wait_ge(s["d1_set"], STRIPS)
            pe.wait_ge(s["o_set"], STRIPS)

            def mean1(w, first):
                v = w + 5 * STRIPS
                chunks(v + 1, 0, 1)
                hold(pe, s["u_set"], w + 1)
                if not first:
                    hold(pe, s["h1_set"], w * 2)
                for hb in range(2):
                    for b in range(2):
                        last = pe.matmul(psG[:, 2 * hb + b, 0:H], w_1[:, hb * P:(hb + 1) * P], u_s[:, b * H:(b + 1) * H], start=True, stop=True)
                last.then_inc(s["hid1_ps"], 1)
                chunks(v + 1, 1, 3)
                hold(pe, s["h1_set"], w * 2 + 2)
                if not first:
                    hold(pe, s["y_set"], w)
                for k in range(TPS):
                    for hb, t in enumerate((h1a, h1b)):
                        last = pe.matmul(psM[:, k * P:(k + 1) * P], t[:, k * P:(k + 1) * P], w_2s[:, hb, :], start=hb == 0, stop=hb == 1)
                last.then_inc(s["y_ps"], 1)
                chunks(v + 1, 3, 7)

            mean1(0, True)
            with pe.Fori(1, STRIPS) as w:
                mean1(w, False)
            pe.wait_ge(s["y_set"], STRIPS)

            def mean2(w, first):
                hold(pe, s["mean_set"], w + 1)
                if not first:
                    hold(pe, s["w_set"], w)
                for k in range(TPS):
                    last = pe.matmul(psM[:, k * P:(k + 1) * P], u_s[:, k * P:(k + 1) * P], ident[:, :], start=True, stop=True)
                last.then_inc(s["mean_ps"], 1)

            v0 = 6 * STRIPS
            chunks(v0 + 1, 0, 2)
            mean2(0, True)
            chunks(v0 + 1, 2, 7)
            with pe.Fori(1, STRIPS - 1) as w:
                chunks(w + (v0 + 1), 0, 2)
                mean2(w, False)
                chunks(w + (v0 + 1), 2, 7)
            mean2(STRIPS - 1, False)


_INS = ["x", "xT", "src", "dst", "enc_w1T", "enc_b1", "enc_w2T", "enc_b2", "conv_w", "wihT", "whhT", "bih", "bhh",
        "dec_w1T", "dec_b1", "dec_w2T", "dec_b2", "W1", "b1", "W2", "b2"]


def kernel(x, src, dst, L0_gnn_enc_w1, L0_gnn_enc_b1, L0_gnn_enc_w2, L0_gnn_enc_b2, L0_gnn_conv_w, L0_gnn_gru_wih,
           L0_gnn_gru_whh, L0_gnn_gru_bih, L0_gnn_gru_bhh, L0_gnn_dec_w1, L0_gnn_dec_b1, L0_gnn_dec_w2, L0_gnn_dec_b2,
           L1_gnn_W1, L1_gnn_b1, L1_gnn_W2, L1_gnn_b2):
    import numpy as np
    import concourse.bacc as bacc
    from concourse.bass_utils import run_bass_kernel_spmd as run

    nc = bacc.Bacc("TRN2", target_bir_lowering=False, num_devices=1)

    def t(a):
        return np.ascontiguousarray(np.asarray(a).T)

    given = [x, t(x), src, dst, t(L0_gnn_enc_w1), L0_gnn_enc_b1, t(L0_gnn_enc_w2), L0_gnn_enc_b2, L0_gnn_conv_w,
             t(L0_gnn_gru_wih), t(L0_gnn_gru_whh), L0_gnn_gru_bih, L0_gnn_gru_bhh, t(L0_gnn_dec_w1), L0_gnn_dec_b1,
             t(L0_gnn_dec_w2), L0_gnn_dec_b2, L1_gnn_W1, L1_gnn_b1, L1_gnn_W2, L1_gnn_b2]
    arrays, args = {}, []
    for name, a in zip(_INS, given):
        a = np.ascontiguousarray(a)
        arrays[f"in_{name}"] = a
        args.append(nc.dram_tensor(f"in_{name}", a.shape, mybir.dt.from_np(a.dtype), kind="ExternalInput").ap())
    out = nc.dram_tensor("rows_out", (NODES, F), mybir.dt.float32, kind="ExternalOutput").ap()
    gnn_kernel(nc, *args, out)
    r = run(nc, [arrays], core_ids=[0])
    return r.results[0]["rows_out"]
```
